# Optimizing a Trainium2 kernel written in Bass

```python
import numpy as np
import jax
import jax.numpy as jnp

def _softmax(x, axis=-1):
    return jax.nn.softmax(x, axis=axis)

def _gelu(x):
    return jax.nn.gelu(x, approximate=True)

def _silu(x):
    return jax.nn.silu(x)

def _sigmoid(x):
    return jax.nn.sigmoid(x)

def _layernorm(x, axis=-1, eps=1e-05):
    m = jnp.mean(x, axis=axis, keepdims=True)
    v = jnp.var(x, axis=axis, keepdims=True)
    return (x - m) / jnp.sqrt(v + eps)

def _scatter_add(tgt, idx, src, axis=0):
    return tgt.at[idx].add(src)

def _segment_sum(src, seg, n):
    return jax.ops.segment_sum(src, seg, n)
kernel_name = 'mk_decoder_preln_d1_seqx_r8_6c8fbd'

def setup_inputs(seed: int=0):
    np.random.seed(seed)
    _w = jnp.asarray

    def _rec_inputs():
        import jax
        import jax.numpy as jnp
        _rk = jax.random.key(seed)
        x = -0.0001033 + 0.9999 * jax.random.normal(jax.random.fold_in(_rk, 1), (2, 512, 128), jnp.float32)
        _lenS = 512 - jax.random.randint(jax.random.fold_in(_rk, 7), (2,), 0, max(1, 512 // 4) + 1, jnp.int32)
        _lenS2 = 32 - jax.random.randint(jax.random.fold_in(_rk, 8), (2,), 0, max(1, 32 // 4) + 1, jnp.int32)
        _ctx_1024P = jax.random.normal(jax.random.fold_in(_rk, 11), (2, 16, 128), jnp.float32)
        _ctx_1024c = jax.random.dirichlet(jax.random.fold_in(_rk, 511), 0.3 * jnp.ones((16,), jnp.float32), (2, 32))
        _ctx_1024t = jnp.einsum('bsk,bkd->bsd', _ctx_1024c, _ctx_1024P)
        _ctx_1024t = _ctx_1024t * jax.lax.rsqrt(jnp.mean(jnp.square(_ctx_1024t)) + 1e-12) * 0.953939
        ctx_1024 = -0.000292821 + 1.00034 * (_ctx_1024t + 0.3 * jax.random.normal(jax.random.fold_in(_rk, 611), (2, 32, 128), jnp.float32))
        return (x, ctx_1024)
    x, ctx_1024 = _rec_inputs()

    def _L0_attn_setup():
        import jax, jax.numpy as jnp
        import numpy as np
        B, S, D, H, R = (2, 256, 128, 16, 64)
        HD = D // H
        VOCAB = 2 * R + 1
        key = jax.random.key(seed)
        ks = jax.random.split(key, 7)
        s = 0.02
        return {'x': jax.random.normal(ks[0], (B, S, D), jnp.float32), 'W_qkv': jax.random.normal(ks[1], (D, 3 * D), jnp.float32) * s, 'b_qkv': jnp.zeros((3 * D,), jnp.float32), 'W_out': jax.random.normal(ks[2], (D, D), jnp.float32) * s, 'b_out': jnp.zeros((D,), jnp.float32), 'rel_emb_k': jax.random.normal(ks[3], (VOCAB, HD), jnp.float32) * s, 'rel_emb_v': jax.random.normal(ks[4], (VOCAB, HD), jnp.float32) * s}
    _L0_attn_all = _L0_attn_setup()
    _L0_attn_in = {k: v for k, v in _L0_attn_all.items() if k in ('W_qkv', 'b_qkv', 'W_out', 'b_out', 'rel_emb_k', 'rel_emb_v')}
    del _L0_attn_all

    def _L0_xattn_setup():
        import jax, jax.numpy as jnp
        import numpy as np
        from jax import lax
        B, T, F = (32, 128, 128)
        CONV_UNITS = 256
        SHORT_UNITS = 256
        RATE = 4
        key = jax.random.key(seed)
        k1, k2, k3 = jax.random.split(key, 3)
        inputs = jax.random.normal(k1, (B, T, F), dtype=jnp.float32)
        memory = jax.random.normal(k2, (B, CONV_UNITS + SHORT_UNITS, F), dtype=jnp.float32)
        conv_w = jax.random.normal(k3, (RATE, F, F), dtype=jnp.float32) * 0.02
        conv_b = jnp.zeros((F,), dtype=jnp.float32)
        return {'inputs': inputs, 'memory': memory, 'conv_w': conv_w, 'conv_b': conv_b, 'conv_units': CONV_UNITS, 'short_units': SHORT_UNITS, 'rate': RATE}
    _L0_xattn_all = _L0_xattn_setup()
    _L0_xattn_in = {k: v for k, v in _L0_xattn_all.items() if k in ('conv_w', 'conv_b')}
    del _L0_xattn_all

    def _L0_ffn_setup():
        import jax, jax.numpy as jnp
        import numpy as np
        D = 128
        H = 16
        DH = D // H
        DC = D // 4
        HID = 256
        G = 2
        EPG = 4
        E = G * EPG
        TOPK = 2
        EPS = 1e-06
        B, T = (2, 256)

        def _rope_sincos(t, dh):
            inv_freq = 1.0 / 10000.0 ** (jnp.arange(0, dh, 2, dtype=jnp.float32) / dh)
            ang = jnp.arange(t, dtype=jnp.float32)[:, None] * inv_freq[None, :]
            return (jnp.sin(ang), jnp.cos(ang))

        def _apply_rope(x, sin, cos):
            x1 = x[..., ::2]
            x2 = x[..., 1::2]
            r = jnp.stack([x1 * cos - x2 * sin, x1 * sin + x2 * cos], axis=-1)
            return r.reshape(x.shape)

        def _swiglu(x):
            a, b = jnp.split(x, 2, axis=-1)
            return jax.nn.silu(a) * b

        def _rmsnorm(x, w):
            return x * jax.lax.rsqrt(jnp.mean(x * x, axis=-1, keepdims=True) + EPS) * w
        key = jax.random.key(seed)
        ks = jax.random.split(key, 14)
        s = 0.02
        return {'src': jax.random.normal(ks[0], (B, T, D), jnp.float32), 'Wq': jax.random.normal(ks[1], (D, D), jnp.float32) * s, 'Wk_c': jax.random.normal(ks[2], (D, DC), jnp.float32) * s, 'Wv_c': jax.random.normal(ks[3], (D, DC), jnp.float32) * s, 'Wk': jax.random.normal(ks[4], (DC, D), jnp.float32) * s, 'Wv': jax.random.normal(ks[5], (DC, D), jnp.float32) * s, 'Wo': jax.random.normal(ks[6], (D, D), jnp.float32) * s, 'W_shared_in': jax.random.normal(ks[7], (D, 2 * HID), jnp.float32) * s, 'W_shared_out': jax.random.normal(ks[8], (HID, D), jnp.float32) * s, 'W1_shared': jax.random.normal(ks[9], (D, 2 * HID), jnp.float32) * s, 'W2_experts': jax.random.normal(ks[10], (E, HID, D), jnp.float32) * s, 'Wg_gate': jax.random.normal(ks[11], (D, G), jnp.float32) * s, 'We_gate': jax.random.normal(ks[12], (D, E), jnp.float32) * s, 'group_bias': jnp.zeros((G,), jnp.float32), 'expert_bias': jnp.zeros((E,), jnp.float32), 'norm1_w': jnp.ones((D,), jnp.float32), 'norm2_w': jnp.ones((D,), jnp.float32)}
    _L0_ffn_all = _L0_ffn_setup()
    _L0_ffn_in = {k: v for k, v in _L0_ffn_all.items() if k in ('Wq', 'Wk_c', 'Wv_c', 'Wk', 'Wv', 'Wo', 'W_shared_in', 'W_shared_out', 'W1_shared', 'W2_experts', 'Wg_gate', 'We_gate', 'group_bias', 'expert_bias', 'norm1_w', 'norm2_w')}
    del _L0_ffn_all
    return {'x': x, 'ctx_1024': ctx_1024, 'L0_attn_W_qkv': _L0_attn_in['W_qkv'], 'L0_attn_b_qkv': _L0_attn_in['b_qkv'], 'L0_attn_W_out': _L0_attn_in['W_out'], 'L0_attn_b_out': _L0_attn_in['b_out'], 'L0_attn_rel_emb_k': _L0_attn_in['rel_emb_k'], 'L0_attn_rel_emb_v': _L0_attn_in['rel_emb_v'], 'L0_xattn_conv_w': _L0_xattn_in['conv_w'], 'L0_xattn_conv_b': _L0_xattn_in['conv_b'], 'L0_ffn_Wq': _L0_ffn_in['Wq'], 'L0_ffn_Wk_c': _L0_ffn_in['Wk_c'], 'L0_ffn_Wv_c': _L0_ffn_in['Wv_c'], 'L0_ffn_Wk': _L0_ffn_in['Wk'], 'L0_ffn_Wv': _L0_ffn_in['Wv'], 'L0_ffn_Wo': _L0_ffn_in['Wo'], 'L0_ffn_W_shared_in': _L0_ffn_in['W_shared_in'], 'L0_ffn_W_shared_out': _L0_ffn_in['W_shared_out'], 'L0_ffn_W1_shared': _L0_ffn_in['W1_shared'], 'L0_ffn_W2_experts': _L0_ffn_in['W2_experts'], 'L0_ffn_Wg_gate': _L0_ffn_in['Wg_gate'], 'L0_ffn_We_gate': _L0_ffn_in['We_gate'], 'L0_ffn_group_bias': _L0_ffn_in['group_bias'], 'L0_ffn_expert_bias': _L0_ffn_in['expert_bias'], 'L0_ffn_norm1_w': _L0_ffn_in['norm1_w'], 'L0_ffn_norm2_w': _L0_ffn_in['norm2_w']}

def reference(x, ctx_1024, L0_attn_W_qkv, L0_attn_b_qkv, L0_attn_W_out, L0_attn_b_out, L0_attn_rel_emb_k, L0_attn_rel_emb_v, L0_xattn_conv_w, L0_xattn_conv_b, L0_ffn_Wq, L0_ffn_Wk_c, L0_ffn_Wv_c, L0_ffn_Wk, L0_ffn_Wv, L0_ffn_Wo, L0_ffn_W_shared_in, L0_ffn_W_shared_out, L0_ffn_W1_shared, L0_ffn_W2_experts, L0_ffn_Wg_gate, L0_ffn_We_gate, L0_ffn_group_bias, L0_ffn_expert_bias, L0_ffn_norm1_w, L0_ffn_norm2_w):
    import jax
    import jax.numpy as jnp

    def _L0_attn_ref(x, W_qkv, b_qkv, W_out, b_out, rel_emb_k, rel_emb_v):
        import jax, jax.numpy as jnp
        import numpy as np
        B, S, D, H, R = (2, 256, 128, 16, 64)
        HD = D // H
        VOCAB = 2 * R + 1
        b, s, d = x.shape
        hd = d // H
        idx = jnp.arange(s)
        dist = jnp.clip(idx[None, :] - idx[:, None], -R, R) + R
        pe_k = rel_emb_k[dist]
        pe_v = rel_emb_v[dist]
        qkv = (x @ W_qkv + b_qkv).reshape(b, s, 3, H, hd)
        qkv = jnp.transpose(qkv, (2, 0, 3, 1, 4))
        q, k, v = (qkv[0], qkv[1], qkv[2])
        q = q / jnp.sqrt(jnp.asarray(hd, x.dtype))
        score = jnp.einsum('bhqd,bhkd->bhqk', q, k) + jnp.einsum('bhqd,qkd->bhqk', q, pe_k)
        attn = jax.nn.softmax(score, axis=-1)
        ctx = jnp.einsum('bhqk,bhkd->bhqd', attn, v) + jnp.einsum('bhqk,qkd->bhqd', attn, pe_v)
        ctx = jnp.transpose(ctx, (0, 2, 1, 3)).reshape(b, s, d)
        return ctx @ W_out + b_out

    def _L0_xattn_ref(inputs, memory, conv_w, conv_b, conv_units, short_units, rate):
        import jax, jax.numpy as jnp
        import numpy as np
        from jax import lax
        B, T, F = (32, 128, 128)
        CONV_UNITS = 256
        SHORT_UNITS = 256
        RATE = 4
        b, t, f = inputs.shape
        conv_mem = memory[:, :conv_units]
        short_mem = memory[:, -short_units:]
        old_memory = short_mem[:, :t]
        compression = lax.conv_general_dilated(old_memory, conv_w, window_strides=(rate,), padding='VALID', dimension_numbers=('NWC', 'WIO', 'NWC')) + conv_b
        tc = compression.shape[1]
        new_short = jnp.concatenate([short_mem[:, t:], inputs], axis=1)
        new_conv = jnp.concatenate([conv_mem[:, tc:], compression], axis=1)
        return jnp.concatenate([new_conv, new_short], axis=1)

    def _L0_ffn_ref(src, Wq, Wk_c, Wv_c, Wk, Wv, Wo, W_shared_in, W_shared_out, W1_shared, W2_experts, Wg_gate, We_gate, group_bias, expert_bias, norm1_w, norm2_w):
        import jax, jax.numpy as jnp
        import numpy as np
        D = 128
        H = 16
        DH = D // H
        DC = D // 4
        HID = 256
        G = 2
        EPG = 4
        E = G * EPG
        TOPK = 2
        EPS = 1e-06
        B, T = (2, 256)

        def _rope_sincos(t, dh):
            inv_freq = 1.0 / 10000.0 ** (jnp.arange(0, dh, 2, dtype=jnp.float32) / dh)
            ang = jnp.arange(t, dtype=jnp.float32)[:, None] * inv_freq[None, :]
            return (jnp.sin(ang), jnp.cos(ang))

        def _apply_rope(x, sin, cos):
            x1 = x[..., ::2]
            x2 = x[..., 1::2]
            r = jnp.stack([x1 * cos - x2 * sin, x1 * sin + x2 * cos], axis=-1)
            return r.reshape(x.shape)

        def _swiglu(x):
            a, b = jnp.split(x, 2, axis=-1)
            return jax.nn.silu(a) * b

        def _rmsnorm(x, w):
            return x * jax.lax.rsqrt(jnp.mean(x * x, axis=-1, keepdims=True) + EPS) * w
        Bb, Tt, C = src.shape
        q = (src @ Wq).reshape(Bb, Tt, H, DH).transpose(0, 2, 1, 3)
        k = (src @ Wk_c @ Wk).reshape(Bb, Tt, H, DH).transpose(0, 2, 1, 3)
        v = (src @ Wv_c @ Wv).reshape(Bb, Tt, H, DH).transpose(0, 2, 1, 3)
        sin, cos = _rope_sincos(Tt, DH)
        q = _apply_rope(q, sin, cos)
        k = _apply_rope(k, sin, cos)
        attn = jnp.einsum('bhqd,bhkd->bhqk', q, k) / np.sqrt(DH).astype(np.float32)
        attn = jax.nn.softmax(attn, axis=-1)
        sa = jnp.einsum('bhqk,bhkd->bhqd', attn, v)
        sa = sa.transpose(0, 2, 1, 3).reshape(Bb, Tt, C) @ Wo
        x = _rmsnorm(src + sa, norm1_w)
        S = Bb * Tt
        flat = x.reshape(S, C)
        shared = _swiglu(flat @ W_shared_in) @ W_shared_out
        g_probs = jax.nn.softmax(flat @ Wg_gate + group_bias, -1)
        g_idx = jnp.argmax(g_probs, axis=-1)
        e_logits = flat @ We_gate + expert_bias
        e_group = jnp.arange(E) // EPG
        in_group = e_group[None, :] == g_idx[:, None]
        e_probs = jax.nn.softmax(jnp.where(in_group, e_logits, -jnp.inf), -1)
        g_prob = jnp.take_along_axis(g_probs, g_idx[:, None], axis=1)
        p_expert = e_probs * g_prob
        topv, topi = jax.lax.top_k(p_expert, TOPK)
        w = jnp.zeros((S, E), flat.dtype).at[jnp.arange(S)[:, None], topi].set(topv)
        h = _swiglu(flat @ W1_shared)
        routed = jnp.zeros_like(shared)
        for e in range(E):
            routed = routed + h @ W2_experts[e] * w[:, e:e + 1]
        out = x + (shared + routed).reshape(Bb, Tt, C)
        return _rmsnorm(out, norm2_w)
    x = x + _L0_attn_ref(_layernorm(x, axis=-1), L0_attn_W_qkv, L0_attn_b_qkv, L0_attn_W_out, L0_attn_b_out, L0_attn_rel_emb_k, L0_attn_rel_emb_v)
    x = x + _L0_xattn_ref(ctx_1024, _layernorm(x, axis=-1), L0_xattn_conv_w, L0_xattn_conv_b, 256, 256, 4)
    x = x + _L0_ffn_ref(_layernorm(x, axis=-1), L0_ffn_Wq, L0_ffn_Wk_c, L0_ffn_Wv_c, L0_ffn_Wk, L0_ffn_Wv, L0_ffn_Wo, L0_ffn_W_shared_in, L0_ffn_W_shared_out, L0_ffn_W1_shared, L0_ffn_W2_experts, L0_ffn_Wg_gate, L0_ffn_We_gate, L0_ffn_group_bias, L0_ffn_expert_bias, L0_ffn_norm1_w, L0_ffn_norm2_w)
    return x

_drawn_inputs = setup_inputs


def setup_inputs(seed=0):
    import zlib

    import numpy as np

    out = dict(_drawn_inputs(seed))
    spreads = {'L0_attn_b_qkv': (0.0, 0.1),
     'L0_attn_b_out': (0.0, 0.1),
     'L0_xattn_conv_b': (0.0, 0.781),
     'L0_ffn_group_bias': (0.0, 0.8),
     'L0_ffn_expert_bias': (0.0, 0.8),
     'L0_ffn_norm1_w': (1.0, 0.2),
     'L0_ffn_norm2_w': (1.0, 0.2)}
    factors = {'L0_attn_W_qkv': 8.0,
     'L0_attn_rel_emb_k': 8.0,
     'L0_attn_rel_emb_v': 8.0,
     'L0_ffn_Wq': 8.0,
     'L0_ffn_Wk_c': 8.0,
     'L0_ffn_Wv_c': 8.0,
     'L0_ffn_Wk': 8.0,
     'L0_ffn_Wv': 8.0,
     'L0_ffn_Wo': 8.0,
     'L0_ffn_W_shared_in': 8.0,
     'L0_ffn_W_shared_out': 8.0,
     'L0_ffn_W1_shared': 8.0,
     'L0_ffn_W2_experts': 8.0,
     'L0_ffn_Wg_gate': 8.0,
     'L0_ffn_We_gate': 8.0}
    for name, (base, spread) in spreads.items():
        noise = np.random.default_rng([zlib.crc32(name.encode()), seed]).standard_normal(out[name].shape)
        drawn = base * np.exp(spread * noise) if base else spread * noise
        out[name] = jnp.asarray(drawn.astype(out[name].dtype))
    for name, factor in factors.items():
        out[name] = (out[name] * factor).astype(out[name].dtype)
    return out
```

```python
from contextlib import ExitStack

import concourse.bass as bass
from concourse import mybir

F32 = mybir.dt.float32
BF16 = mybir.dt.bfloat16
ALU = mybir.AluOpType
ACT = mybir.ActivationFunctionType
AX_X = mybir.AxisListType.X

P = 128
B, S, D, H = 2, 512, 128, 16
HD = D // H
NT = B * S // P
IT = S // P
TOK = B * S
R = 64
SLOTS = 6
KR = HD * SLOTS
Q_PARTS = (0, 1, 2, 0, 0, 1)
K_PARTS = (0, 0, 0, 1, 2, 1)
EXT = 512
ZERO = 255
VW = HD + 1
DC, HID, NE, NG = 32, 256, 8, 2
EPG = NE // NG
LN_EPS, RMS_EPS = 1e-5, 1e-6
Q_SCALE = float(HD) ** -0.5
Q = 64
STEPS = S // Q
CH = 8
BB = 16
CTX, RATE = 32, 4
CONV = CTX // RATE
C_BQ, C_BK, C_LO, C_HI = range(4)
R_BV, R_LO, R_HI, R_BOUT, R_CONV, R_N1, R_N2 = range(7)


def slots_of(s):
    it, half = divmod(s, 2)
    ja = min(max(it if half else it - 1, 0), IT - 2)
    rest = [j for j in range(IT) if j not in (ja, ja + 1)]
    return [(ja, 0), (ja + 1, 0)] + [(j, 1 if j < ja else 2) for j in rest]


def build(nc, t):
    with ExitStack() as ctx:
        def sb(name, shape, dt=F32):
            return ctx.enter_context(nc.sbuf_tensor(name, shape, dt))

        x = sb("x_sb", [P, NT, D])
        xn = sb("xn", [P, NT, D])
        xnT = sb("xnT", [P, TOK])
        q_op = sb("q_op", [P, H // 2, TOK], BF16)
        k_op = sb("k_op", [P, 3, H // 2, TOK], BF16)
        q_rel = sb("q_rel", [P, B * H, S // 2], BF16)
        band = sb("band", [P, 3, B * H, P])
        v_sb = sb("v_sb", [P, 3, NT, H * VW])
        rel_v = sb("rel_v", [P, 384 * HD])
        rel_k = sb("rel_k", [P, EXT], BF16)
        ctxT = sb("ctxT", [P, CH, S])
        p_out = sb("p_out", [P, 2, 4, P])
        crel = sb("crel", [HD, Q, B * H])
        ident = sb("ident", [P, P])
        rows = sb("rows", [P, 8, D])
        cols = sb("cols", [P, 8])
        w_qkv = sb("w_qkv", [P, 3 * D])
        w_out = sb("w_out", [P, D])
        stats = sb("stats", [P, NT, 6])
        mv = sb("mv", [P, NT, 2])
        var = sb("var", [P, NT])
        std = sb("std", [P, NT])
        rstd = sb("rstd", [P, NT])
        m_qk = sb("m_qk", [P, NT, H])
        m_rel = sb("m_rel", [P, NT, H])
        neg_m = sb("neg_m", [P, NT, H])
        rsum = sb("rsum", [P, 2, H])
        arena = band[:, :, :, :].rearrange("p a b c -> p (a b c)")
        f32_of = [arena[:, n * TOK:(n + 1) * TOK] for n in range(4)]
        rest_dve = arena[:, 4 * TOK:5 * TOK]
        rest_pool = arena[:, 5 * TOK:6 * TOK]
        parts = [arena[:, (6 + 3 * n) * TOK:(9 + 3 * n) * TOK].bitcast(BF16)
                 .rearrange("p (s t) -> p s t", s=SLOTS) for n in range(2)]
        scratchT = ctxT[:, :, :].rearrange("p a b -> p (a b)")
        relk_f = scratchT[0:HD, 0:EXT]
        relk_rest = scratchT[0:HD, EXT:2 * EXT]
        relk_parts = scratchT[0:HD, 2 * EXT:5 * EXT].bitcast(BF16).rearrange("p (s t) -> p s t", s=SLOTS)
        neg_mT = p_out[:, 0, :, :].rearrange("p a b -> p (a b)").bitcast(BF16)
        wide = q_rel[:, :, :].rearrange("p a b -> p (a b)").bitcast(F32)
        spare = k_op[:, 1:3, :, :].rearrange("p v a t -> p (v a t)").bitcast(F32)
        w_conv = wide[:, 0:512].rearrange("p (r o) -> p r o", r=RATE)
        w_in = [wide[:, 512 + 512 * n:1024 + 512 * n] for n in range(2)]
        w_so = wide[:, 1536:1792].rearrange("p (k o) -> p k o", k=2)
        w_2 = wide[:, 1792:3840].rearrange("p (k n) -> p k n", k=2)
        cos, sin = spare[:, 0:S], spare[:, S:2 * S]
        w_q, w_o = spare[:, 1024:1152], spare[:, 1152:1280]
        w_kc, w_vc = spare[:, 1280:1312], spare[:, 1312:1344]
        w_k, w_v = spare[0:DC, 1344:1472], spare[0:DC, 1472:1600]
        w_gate, b_gate = spare[:, 1600:1610], spare[:, 1610:1620]
        tri = spare[:, 1620:1636]
        w_qs, w_ks = spare[:, 1664:1792], spare[0:DC, 1792:1920]
        p_ring = spare[:, 2048:8192].rearrange("p (r h t) -> p r h t", r=3, h=4)
        hid = [spare[:, 2048 + 2048 * n:4096 + 2048 * n].rearrange("p (k t) -> p k t", k=2) for n in range(2)]
        silu = spare[:, 6144:8192].rearrange("p (r t) -> p r t", r=4)
        shifted = scratchT[:, 0:NT * D].rearrange("p (t d) -> p t d", d=D)
        memT, comp = scratchT[:, 1024:1088], scratchT[0:B * CONV, 1088:1216]
        latT = [scratchT[0:DC, 2048:3072], scratchT[0:DC, 3072:4096]]
        ctxn = arena[:, 10240:11264].rearrange("p (t d) -> p t d", d=D)
        squares = arena[:, 9216:10240].rearrange("p (t d) -> p t d", d=D)
        nm_T = crel[0:4, 0:16, :].rearrange("d i h -> d (i h)").bitcast(BF16).rearrange("d (r t) -> d r t", r=2)
        gsc = arena[:, 8192:9216]
        ps = ctx.enter_context(nc.psum_tensor("ps", [P, 8, 512], F32))

        names = """ld_x ld_w ld_rel ld_one ln_var ln_std ln_out xT_psum xT_ready
        q_psum k_psum v_psum f_ready cols_ready rows_ready q_split k_split kv_split v_ready
        scr_q scr_k scr_lo scr_hi scr_rel op_q op_k op_lo op_hi op_qrel rel_ready rel_split
        s_psum m_done r_psum r_done negm_ready mT_psum mT_ready m_rows pv_zero
        bias_psum bias_ready st_psum z_ready zexp_done oexp_done pv_done vrel_psum crel_ready
        crel_added ctx_ready ctx_tr ctx_norm cn_psum cn_ready y_psum x_added xb_ready
        ld_wide ld_spare ld_ctx shift_in shift1 shift_done memT_psum memT_ready comp_psum comp_ready
        x2_ready sw_ready lat_psum lat_ready q2_psum k2_psum v2_psum v2_ready ropeq_ready
        t_psum t_done n_ready nT_psum nT_ready n_rows n_rows_odd out_ready g_psum g_exp g_pv g_ctx g_nfree
        sq_done rms_var rms_std gate_psum g_sub g_soft e_sub e_soft gate_done a_psum silu_done hid_ready y3_psum
        y3_done sq2_done dve pool out_done v_one""".split()
        sm = {n: ctx.enter_context(nc.semaphore(n)) for n in names}
        block = ctx.enter_context(nc.Block())

        def head_slot(h):
            p, e = divmod(h, 2)
            return 8 * (p // 4) + 4 * e + p % 4

        @block.sync
        def _(sp):
            sp.dma_start(x[:, :, :], t["x"].rearrange("b (t p) d -> p (b t) d", p=P)).then_inc(sm["ld_x"], 16)
            sp.dma_start(ident[:, :], t["ident"]).then_inc(sm["ld_w"], 16)
            sp.dma_start(w_qkv[:, :], t["w_qkv"]).then_inc(sm["ld_w"], 16)
            sp.dma_start(cols[:, 0:4], t["cols"]).then_inc(sm["ld_w"], 16)
            sp.dma_start(relk_f, t["relk_ext"]).then_inc(sm["ld_rel"], 16)
            sp.dma_start(rows[:, 0:7, :], bass.AP(t["rows"].tensor, 0, [[0, P], [1, 7 * D]])).then_inc(sm["ld_w"], 16)
            sp.dma_start(w_out[:, :], t["w_out"]).then_inc(sm["ld_w"], 16)
            for e in range(2):
                sp.dma_start(k_op[64 * e + KR:64 * e + KR + 1, :, :, :].rearrange("o a b c -> o (a b c)"),
                             t["ones"]).then_inc(sm["ld_one"], 16)
            for n, (done, val, scr, op) in enumerate((("q_split", 1, "scr_q", "op_q"), ("k_split", 1, "scr_k", "op_k"),
                                                      ("kv_split", 1, "scr_lo", "op_lo"), ("kv_split", 2, "scr_hi", "op_hi"))):
                sp.wait_ge(sm[done], val)
                sp.dma_start(t["scr"][n], parts[n % 2]).then_inc(sm[scr], 16)
                sp.wait_ge(sm[scr], 16)
                for e in range(2):
                    dst = q_op if n == 0 else k_op[:, n - 1]
                    src = bass.AP(t["scr"].tensor, n * P * SLOTS * TOK + e * KR * TOK,
                                  [[TOK, KR], [2 * KR * TOK, H // 2], [1, TOK]])
                    sp.dma_start(dst[64 * e:64 * e + KR, :, :], src).then_inc(sm[op], 16)
                if n == 1:
                    for u in range(2):
                        for b in range(B):
                            src = bass.AP(t["scr"].tensor, b * S + u * (S // 2),
                                          [[TOK, KR], [KR * TOK, H], [1, S // 2]])
                            dst = q_rel[64 * u:64 * u + KR, :, :].rearrange("r (h b) i -> r h b i", b=B)[:, :, b, :]
                            sp.dma_start(dst, src).then_inc(sm["op_qrel"], 16)
                    sp.wait_ge(sm["rel_split"], 1)
                    sp.dma_start(t["scr_rel"].rearrange("d s n -> d s n"), relk_parts).then_inc(sm["scr_rel"], 16)
                    sp.wait_ge(sm["scr_rel"], 16)
                    for u in range(2):
                        sp.dma_start(rel_k[64 * u:64 * u + KR, :],
                                     t["scr_rel"].rearrange("d s n -> (d s) n")).then_inc(sm["rel_ready"], 16)
                    sp.dma_start(rel_v[:, :], bass.AP(t["relv_ext"].tensor, 0, [[HD, P], [1, 384 * HD]])
                                 ).then_inc(sm["rel_ready"], 16)
            sp.wait_ge(sm["mT_ready"], 1)
            for e in range(2):
                for u in range(2):
                    r0 = 8 * u + 4 * e
                    dst = q_op[64 * e + KR:64 * e + KR + 1, 4 * u:4 * u + 4, :]
                    sp.dma_start(dst.rearrange("o p t -> o (p t)"),
                                 neg_mT[r0:r0 + 4, :]).then_inc(sm["m_rows"], 16)
            sp.wait_ge(sm["bias_psum"], STEPS * CH)
            sp.dma_start(w_conv, t["w_conv"].rearrange("r i o -> i r o")).then_inc(sm["ld_wide"], 16)
            sp.dma_start(w_in[0], t["w_sin"]).then_inc(sm["ld_wide"], 16)
            sp.dma_start(w_in[1], t["w_1"]).then_inc(sm["ld_wide"], 16)
            sp.dma_start(w_so, t["w_so"].rearrange("(k i) o -> i k o", i=P)).then_inc(sm["ld_wide"], 16)
            for k in range(2):
                sp.dma_start(w_2[:, k, :].rearrange("p (e o) -> p e o", e=NE),
                             t["w_2"].rearrange("e (k i) o -> k i e o", i=P)[k]).then_inc(sm["ld_wide"], 16)
            sp.wait_ge(sm["st_psum"], STEPS * CH)
            for dst, name in ((cos, "cos"), (sin, "sin"), (w_q, "w_q"), (w_o, "w_o"), (w_kc, "w_kc"), (w_vc, "w_vc"),
                              (w_k, "w_k"), (w_v, "w_v"), (w_gate[:, 0:NG], "w_gg"), (w_gate[:, NG:], "w_ge")):
                sp.dma_start(dst, t[name]).then_inc(sm["ld_spare"], 16)
            for dst, name, n in ((b_gate[:, 0:NG], "b_gg", NG), (b_gate[:, NG:], "b_ge", NE), (tri, "tri", 16)):
                sp.dma_start(dst, bass.AP(t[name].tensor, 0, [[0, P], [1, n]])).then_inc(sm["ld_spare"], 16)
            sp.wait_ge(sm["ctx_tr"], NT)
            sp.dma_start(shifted[P - CTX:P, 3:NT:4, :], t["ctx"].rearrange("b t d -> t b d")).then_inc(sm["shift_in"], 16)
            sp.wait_ge(sm["ln_out"], 2 * NT)
            by_b = lambda a: a.rearrange("p (b t) d -> p b t d", b=B)
            for sh, t0 in ((CONV, 0), (CTX, 2)):
                sp.dma_start(by_b(shifted[0:P - sh, :, :])[:, :, t0:t0 + 2, :],
                             by_b(xn[sh:P, :, :])[:, :, t0:t0 + 2, :]).then_inc(sm["shift_in"], 16)
                sp.dma_start(shifted[P - sh:P, t0:NT:4, :], xn[0:sh, t0 + 1:NT:4, :]).then_inc(sm["shift_in"], 16)
            sp.wait_ge(sm["comp_ready"], 1)
            for b in range(B):
                sp.dma_start(shifted[P - CONV:P, IT * b + 1, :], comp[CONV * b:CONV * b + CONV, :]).then_inc(sm["shift_in"], 16)
            for n, (done, scr, op) in enumerate((("q_split", "scr_q", "op_q"), ("k_split", "scr_k", "op_k"))):
                sp.wait_ge(sm[done], 2)
                sp.dma_start(t["scr"][n], parts[n]).then_inc(sm[scr], 16)
                sp.wait_ge(sm[scr], 32)
                for e in range(2):
                    dst = q_op if n == 0 else k_op[:, 0]
                    src = bass.AP(t["scr"].tensor, n * P * SLOTS * TOK + e * KR * TOK,
                                  [[TOK, KR], [2 * KR * TOK, H // 2], [1, TOK]])
                    sp.dma_start(dst[64 * e:64 * e + KR, :, :], src).then_inc(sm[op], 16)
            for n in range(B * 4):
                b, g = divmod(n, 4)
                sp.wait_ge(sm["nT_ready"], n + 1)
                for e in range(2):
                    sp.dma_start(q_op[64 * e + KR:64 * e + KR + 1, 2 * g:2 * g + 2, b * S:b * S + S],
                                 nm_T[2 * e:2 * e + 2, n % 2, :]).then_inc(sm["n_rows" if n % 2 == 0 else "n_rows_odd"], 16)
            for tt in range(NT):
                b, it = divmod(tt, IT)
                sp.wait_ge(sm["out_ready"], tt + 1)
                sp.dma_start(t["out"][b, it * P:it * P + P, :], x[:, tt, :]).then_inc(sm["out_done"], 16)
            sp.wait_ge(sm["out_done"], 16 * NT)

        @block.gpsimd
        def _(pool):
            chain = [0]

            def link(ins):
                chain[0] += 1
                ins.then_inc(sm["pool"], 1)
                pool.wait_ge(sm["pool"], chain[0])

            ones_col = v_sb[:, :, :, :].rearrange("p v t (h w) -> p (v t h) w", w=VW)[:, :, HD:VW]
            pool.memset(ones_col, 1.0).then_inc(sm["v_one"], 1)
            pool.wait_ge(sm["ld_rel"], 16)
            link(pool.tensor_copy(relk_parts[:, 0, :], relk_f))
            link(pool.tensor_tensor(relk_rest, relk_f, relk_parts[:, 0, :], ALU.subtract))
            link(pool.tensor_copy(relk_parts[:, 3, :], relk_rest))
            link(pool.tensor_tensor(relk_parts[:, 4, :], relk_rest, relk_parts[:, 3, :], ALU.subtract))
            for s in (1, 2):
                pool.tensor_copy(relk_parts[:, s, :], relk_parts[:, 0, :])
            link(pool.tensor_copy(relk_parts[:, 5, :], relk_parts[:, 3, :]))
            pool.sem_inc(sm["rel_split"], 1)
            for n in (2, 3):
                f, o = f32_of[n], parts[n % 2]
                pool.wait_ge(sm["f_ready"], n + 1)
                pool.wait_ge(sm["scr_q" if n == 2 else "scr_k"], 16)
                link(pool.tensor_copy(o[:, 0, :], f))
                link(pool.tensor_tensor(rest_pool, f, o[:, 0, :], ALU.subtract))
                link(pool.tensor_copy(o[:, 3, :], rest_pool))
                link(pool.tensor_tensor(o[:, 4, :], rest_pool, o[:, 3, :], ALU.subtract))
                link(pool.tensor_copy(o[:, 1, :], o[:, 0, :]))
                link(pool.tensor_copy(o[:, 2, :], o[:, 0, :]))
                pool.tensor_copy(o[:, 5, :], o[:, 3, :]).then_inc(sm["kv_split"], 1)
            pool.wait_ge(sm["ln_out"], NT)
            pool.wait_ge(sm["ld_w"], 80)
            pool.tensor_tensor(x[:, :, :], x[:, :, :], bass.AP(rows[:, R_BOUT, :].tensor, rows[:, R_BOUT, :].offset, [[8 * D, P], [0, NT], [1, D]]),
                               ALU.add).then_inc(sm["xb_ready"], 1)
            pool.wait_ge(sm["ld_spare"], 16 * 13)
            for w, ws in ((w_q, w_qs), (w_k, w_ks)):
                w, ws = (v.rearrange("p (n c) -> p n c", c=2) for v in (w, ws))
                pool.tensor_scalar(ws[:, :, 0], w[:, :, 1], -1.0, None, ALU.mult).then_inc(sm["sw_ready"], 1)
                pool.tensor_copy(ws[:, :, 1], w[:, :, 0]).then_inc(sm["sw_ready"], 1)

        @block.scalar
        def _(act):
            def ln_sqrt(n):
                act.wait_ge(sm["ln_var"], n + 1)
                act.activation(std[:, :], var[:, :], ACT.Sqrt).then_inc(sm["ln_std"], 1)

            def copy_xT(n):
                for c in range(2):
                    act.wait_ge(sm["xT_psum"], NT * n + 4 * c + 4)
                    act.activation(xnT[:, 512 * c:512 * c + 512], ps[:, c, :], ACT.Identity).then_inc(sm["xT_ready"], 1)

            ln_sqrt(0)
            copy_xT(0)
            act.wait_ge(sm["cols_ready"], 1)
            act.wait_ge(sm["q_psum"], 1)
            act.activation(f32_of[0], ps[:, 2:4, :].rearrange("p a b -> p (a b)"), ACT.Identity,
                           bias=cols[:, 4:5], scale=Q_SCALE).then_inc(sm["f_ready"], 1)
            act.wait_ge(sm["k_psum"], 1)
            for n, c in ((1, C_BK), (2, 5), (3, 6)):
                act.activation(f32_of[n], ps[:, 4:6, :].rearrange("p a b -> p (a b)"), ACT.Identity,
                               bias=cols[:, c:c + 1]).then_inc(sm["f_ready"], 1)
            act.wait_ge(sm["mT_psum"], 1)
            act.activation(neg_mT[0:H, :], ps[0:H, 0:2, :].rearrange("p a b -> p (a b)"), ACT.Identity
                           ).then_inc(sm["mT_ready"], 1)

            def bias_evac(s, k):
                n, slot = CH * s + k, k // 4
                act.wait_ge(sm["bias_psum"], n + 1)
                if s >= 3:
                    act.wait_ge(sm["vrel_psum"], 4 * (s - 2))
                col = slot * Q + BB * (k % 4)
                act.activation(band[:, s % 3, :, col:col + BB],
                               ps[:, 4, :].rearrange("p (i h) -> p h i", i=BB), ACT.Identity).then_inc(sm["bias_ready"], 1)

            act.wait_ge(sm["kv_split"], 2)
            act.wait_ge(sm["scr_lo"], 16)
            act.wait_ge(sm["scr_hi"], 16)
            for k in range(CH):
                bias_evac(0, k)
            for n in range(STEPS * CH):
                s, c = divmod(n, CH)
                g, b = divmod(c, 2)
                act.wait_ge(sm["st_psum"], n + 1)
                if n == 0:
                    act.wait_ge(sm["m_rows"], 64)
                if n >= 2:
                    act.wait_ge(sm["pv_done"], n - 1)
                src = ps[:, 2 * (n % 2):2 * (n % 2) + 2, :].rearrange("p e (a c) -> p e a c", a=2)[:, :, :, P:2 * P]
                dst = p_out[:, n % 2, :, :].rearrange("p (a e) c -> p e a c", e=2)
                act.activation(dst, src, ACT.Exp).then_inc(sm["oexp_done"], 1)
                if s + 1 < STEPS:
                    bias_evac(s + 1, c)
                act.wait_ge(sm["z_ready"], n + 1)
                z = band[:, s % 3, 8 * g:8 * g + 8, :].rearrange("p (h b) c -> p h b c", b=B)[:, :, b, :]
                act.activation(z, z, ACT.Exp).then_inc(sm["zexp_done"], 1)

            def copy_ctxn(k):
                for tt in range(NT):
                    act.wait_ge(sm["cn_psum"], NT * k + tt + 1)
                    act.activation(xnT[:, tt * P:tt * P + P], ps[:, 2 + tt % 2, 0:P], ACT.Identity).then_inc(sm["cn_ready"], 1)

            copy_ctxn(0)
            ln_sqrt(1)
            act.wait_ge(sm["memT_psum"], 1)
            act.activation(memT, ps[:, 0, 0:B * CTX], ACT.Identity).then_inc(sm["memT_ready"], 1)
            ln_sqrt(2)
            copy_xT(1)
            for n in range(2):
                act.wait_ge(sm["lat_psum"], n + 1)
                act.activation(latT[n], ps[0:DC, 4 + 2 * n:6 + 2 * n, :].rearrange("p a b -> p (a b)"), ACT.Identity).then_inc(sm["lat_ready"], 1)
            for j in range(-16, 128):
                if j % 16 == 2 and j // 16 + 1 < 8:
                    m = j // 16 + 1
                    act.wait_ge(sm["nT_psum"], m + 1)
                    if m >= 2:
                        act.wait_ge(sm["n_rows" if m % 2 == 0 else "n_rows_odd"], 32 * (m // 2))
                    act.activation(nm_T[:, m % 2, :], ps[0:4, 7, :], ACT.Identity).then_inc(sm["nT_ready"], 1)
                if j >= 0:
                    k = j // 4
                    act.wait_ge(sm["g_psum"], j + 1)
                    if k >= 3:
                        act.wait_ge(sm["g_pv"], k - 2)
                    act.activation(p_ring[:, k % 3, j % 4, :], ps[:, 4 + j % 2, :], ACT.Exp).then_inc(sm["g_exp"], 1)
            copy_ctxn(1)

            def sum_squares(k, src):
                for tt in range(NT):
                    if k == 0:
                        act.wait_ge(sm["x_added"], NT + tt + 1)
                    else:
                        act.wait_ge(sm["y3_done"], tt + 1)
                    act.activation(squares[:, tt, :], src[:, tt, :], ACT.Square, accum_out=mv[:, tt, k:k + 1]).then_inc(sm["sq_done"], 1)
                act.wait_ge(sm["rms_var"], k + 1)
                act.activation(std[:, :], var[:, :], ACT.Sqrt).then_inc(sm["rms_std"], 1)

            sum_squares(0, xn)
            copy_xT(2)
            act.wait_ge(sm["g_sub"], 1)
            act.activation(gsc[:, 128:144], gsc[:, 112:128], ACT.Exp).then_inc(sm["g_soft"], 1)
            act.wait_ge(sm["e_sub"], 1)
            act.activation(gsc[:, 256:288], gsc[:, 224:256], ACT.Exp).then_inc(sm["e_soft"], 1)
            for n in range(8):
                act.wait_ge(sm["a_psum"], n + 1)
                if n >= 4:
                    act.wait_ge(sm["hid_ready"], n - 3)
                act.activation(silu[:, n % 4, :], ps[:, 2 * (n % 3), :], ACT.Silu).then_inc(sm["silu_done"], 1)
            sum_squares(1, xn)

        @block.vector
        def _(dve):
            chain = [0]

            def link(ins):
                chain[0] += 1
                ins.then_inc(sm["dve"], 1)
                dve.wait_ge(sm["dve"], chain[0])

            def layernorm(n, src, dst):
                for tt in range(NT):
                    i = dve.bn_stats(stats[:, tt, :], src[:, tt, :])
                link(i)
                for tt in range(NT):
                    i = dve.bn_aggr(mv[:, tt, :], stats[:, tt, :])
                link(i)
                dve.tensor_scalar(var[:, :], mv[:, :, 1], LN_EPS, None, ALU.add).then_inc(sm["ln_var"], 1)
                dve.wait_ge(sm["ln_std"], n + 1)
                link(dve.reciprocal(rstd[:, :], std[:, :]))
                for tt in range(NT):
                    dve.tensor_scalar(dst[:, tt, :], src[:, tt, :], mv[:, tt, 0:1], rstd[:, tt:tt + 1],
                                      ALU.subtract, ALU.mult).then_inc(sm["ln_out"], 1)

            def split(f, o, order, rest, done):
                one, two, three = order
                link(dve.tensor_copy(o[:, one[0], :], f))
                link(dve.tensor_tensor(rest, f, o[:, one[0], :], ALU.subtract))
                link(dve.tensor_copy(o[:, two[0], :], rest))
                link(dve.tensor_tensor(o[:, three[0], :], rest, o[:, two[0], :], ALU.subtract))
                link(dve.tensor_copy(o[:, two[1], :], o[:, two[0], :]))
                link(dve.tensor_copy(o[:, one[1], :], o[:, one[0], :]))
                dve.tensor_copy(o[:, one[2], :], o[:, one[0], :]).then_inc(sm[done], 1)

            slot_of = lambda ps_: [[s for s in range(SLOTS) if ps_[s] == k] for k in range(3)]
            dve.wait_ge(sm["ld_x"], 16)
            layernorm(0, x, xn)
            dve.wait_ge(sm["ld_w"], 80)
            dve.tensor_scalar(cols[:, 4:5], cols[:, C_BQ:C_BQ + 1], Q_SCALE, None, ALU.mult)
            dve.tensor_scalar(cols[:, 5:7], cols[:, C_LO:C_HI + 1], cols[:, C_BK:C_BK + 1], None, ALU.add).then_inc(sm["cols_ready"], 1)
            for r in (R_LO, R_HI):
                link(dve.tensor_tensor(rows[:, r, :], rows[:, r, :], rows[:, R_BV, :], ALU.add))
            dve.wait_ge(sm["f_ready"], 1)
            split(f32_of[0], parts[0], slot_of(Q_PARTS), rest_dve, "q_split")
            dve.wait_ge(sm["f_ready"], 2)
            split(f32_of[1], parts[1], slot_of(K_PARTS), rest_dve, "k_split")
            dve.wait_ge(sm["v_psum"], 1)
            dve.wait_ge(sm["v_one"], 1)
            for v, r in enumerate((R_BV, R_LO, R_HI)):
                row = rows[:, r, :]
                add = bass.AP(row.tensor, row.offset, [[8 * D, P], [0, NT], [HD, H], [1, HD]])
                dve.tensor_tensor(v_sb[:, v, :, :].rearrange("p t (h w) -> p t h w", w=VW)[:, :, :, 0:HD],
                                  ps[:, 6:8, :].rearrange("p a (t h d) -> p (a t) h d", t=4, d=HD), add, ALU.add
                                  ).then_inc(sm["v_ready"], 1)

            for n in range(B * IT * (H // 2)):
                tt, p = divmod(n, H // 2)
                dve.wait_ge(sm["s_psum"], n + 1)
                c = head_slot(2 * p)
                dve.tensor_reduce(m_qk[:, tt, c:c + 5:4], ps[:, 2 * (n % 4):2 * (n % 4) + 2, :], AX_X, ALU.max
                                  ).then_inc(sm["m_done"], 1)
            for n in range(NT * 2):
                tt, u = divmod(n, 2)
                dve.wait_ge(sm["r_psum"], n + 1)
                dve.tensor_reduce(m_rel[:, tt, 8 * u:8 * u + 8].rearrange("p (a b) -> p a b", b=2),
                                  ps[:, 4 * (n % 2):4 * (n % 2) + 4, 0:2 * (2 * R + 1)].rearrange("p a (b c) -> p a b c", b=2),
                                  AX_X, ALU.max).then_inc(sm["r_done"], 1)
            dve.wait_ge(sm["r_done"], NT * 2)
            dve.wait_ge(sm["m_done"], 64)
            dve.scalar_tensor_tensor(neg_m[:, :, :], m_qk[:, :, :], -1.0, m_rel[:, :, :], ALU.mult, ALU.subtract
                                     ).then_inc(sm["negm_ready"], 1)
            dve.memset(ps[:, 5:7, :], 0.0).then_inc(sm["pv_zero"], 1)

            def crel_evac(kb):
                dve.wait_ge(sm["vrel_psum"], kb + 1)
                if kb >= 4:
                    dve.wait_ge(sm["crel_added"], kb // 4)
                i0 = BB * (kb % 4)
                dve.tensor_copy(crel[:, i0:i0 + BB, :].rearrange("d i h -> d (i h)"), ps[0:HD, 7, :]).then_inc(sm["crel_ready"], 1)

            def ctx_evac(s):
                dve.wait_ge(sm["crel_added"], s + 1)
                dve.tensor_copy(ctxT[:, :, Q * s:Q * s + Q], ps[:, 5 + s % 2, :].rearrange("p (c i) -> p c i", i=Q)
                                ).then_inc(sm["ctx_ready"], 1)

            for n in range(STEPS * CH + 2 * CH):
                s, c = divmod(n, CH)
                g, b = divmod(c, 2)
                if c == 0 and s >= 2:
                    ctx_evac(s - 2)
                if s < STEPS:
                    dve.wait_ge(sm["oexp_done"], n + 1)
                    dve.wait_ge(sm["bias_ready"], CH * (s + 1))
                    z = band[:, s % 3, 8 * g:8 * g + 8, :].rearrange("p (a e b) c -> p e a b c", e=2, b=B)[:, :, :, b, :]
                    src = ps[:, 2 * (n % 2):2 * (n % 2) + 2, :].rearrange("p e (a c) -> p e a c", a=2)[:, :, :, 0:P]
                    dve.tensor_tensor(z, src, z, ALU.add).then_inc(sm["z_ready"], 1)
                if 1 <= s <= STEPS and c % 2:
                    crel_evac(4 * (s - 1) + c // 2)

            def attn_finish(k, dst, resid):
                for tt in range(NT + 1):
                    if tt < NT:
                        dve.wait_ge(sm["ctx_tr"], NT * k + tt + 1)
                        src = ps[:, tt % 2, :].rearrange("p (h r) -> p h r", r=32)
                        link(dve.reciprocal(rsum[:, tt % 2, :], src[:, :, HD]))
                        rs = rsum[:, tt % 2, :]
                        dve.tensor_tensor(dst[:, tt, :].rearrange("p (h d) -> p h d", d=HD), src[:, :, 0:HD],
                                          bass.AP(rs.tensor, rs.offset, [[2 * H, P], [1, H], [0, HD]]), ALU.mult
                                          ).then_inc(sm["ctx_norm"], 1)
                    if tt == 0 and k == 0:
                        dve.wait_ge(sm["xb_ready"], 1)
                    if tt >= 1:
                        dve.wait_ge(sm["y_psum"], NT * k + tt)
                        dve.tensor_tensor(resid[:, tt - 1, :], ps[:, 4 + (tt - 1) % 2, 0:P], resid[:, tt - 1, :], ALU.add
                                          ).then_inc(sm["x_added"], 1)

            attn_finish(0, xn, x)
            dve.wait_ge(sm["x_added"], NT)
            layernorm(1, x, xn)
            dve.wait_ge(sm["comp_psum"], 1)
            dve.tensor_tensor(comp, ps[0:B * CONV, 1, 0:D], rows[0:B * CONV, R_CONV, :], ALU.add).then_inc(sm["comp_ready"], 1)
            dve.wait_ge(sm["shift_in"], 16 * 7)
            link(dve.tensor_tensor(x[:, :, :], x[:, :, :], shifted, ALU.add))
            layernorm(2, x, xn)

            for n, (first, scale) in enumerate(((2, Q_SCALE), (0, 1.0))):
                dve.wait_ge(sm["q2_psum" if n == 0 else "k2_psum"], 1)
                f = f32_of[n]
                for c in range(2):
                    dve.scalar_tensor_tensor(f[:, c * S:c * S + S], ps[:, first + c, :], scale, cos, ALU.mult, ALU.mult)
                for c in range(2):
                    i = dve.scalar_tensor_tensor(rest_dve[:, c * S:c * S + S],
                                                 ps[:, (6 if n == 0 else 2) + c, :], scale, sin, ALU.mult, ALU.mult)
                i.then_inc(sm["ropeq_ready"], 1)
                dve.wait_ge(sm["ropeq_ready"], n + 1)
                link(dve.tensor_tensor(f, f, rest_dve, ALU.add))
                if n == 0:
                    dve.wait_ge(sm["scr_lo"], 16)
                split(f, parts[n], slot_of(Q_PARTS if n == 0 else K_PARTS), rest_dve, "q_split" if n == 0 else "k_split")
            dve.wait_ge(sm["v2_psum"], 1)
            dve.tensor_copy(v_sb[:, 0, :, :].rearrange("p t (h w) -> p (t h) w", w=VW)[:, :, 0:HD],
                            ps[:, 4:6, :].rearrange("p a (n d) -> p (a n) d", d=HD)).then_inc(sm["v2_ready"], 1)

            for j in range(-32, 128 + 8):
                if j % 2 == 0 and (j + 32) // 2 < 64:
                    su = (j + 32) // 2
                    m, k = divmod(su, 8)
                    b, g = divmod(m, 4)
                    a, it = divmod(k, 4)
                    dve.wait_ge(sm["t_psum"], su + 1)
                    c = 4 * g + a
                    dve.tensor_reduce(m_qk[:, IT * b + it, c:c + 3:2], ps[:, 2 * (su % 2):2 * (su % 2) + 2, :], AX_X, ALU.max
                                      ).then_inc(sm["t_done"], 1)
                if j % 16 == 15 and j // 16 + 2 < 8:
                    m = j // 16 + 2
                    b, g = divmod(m, 4)
                    dve.wait_ge(sm["t_done"], 8 * m + 8)
                    dve.tensor_scalar(neg_m[:, IT * b:IT * b + IT, 4 * g:4 * g + 4], m_qk[:, IT * b:IT * b + IT, 4 * g:4 * g + 4],
                                      -1.0, None, ALU.mult).then_inc(sm["n_ready"], 1)
                if j >= 19 and (j - 19) % 16 == 0:
                    n = (j - 19) // 16
                    b, g = divmod(n, 4)
                    dve.wait_ge(sm["g_pv"], 4 * n + 4)
                    dve.tensor_copy(ctxT[:, 2 * g + b, :], ps[:, 6, :]).then_inc(sm["g_ctx"], 1)

            attn_finish(1, ctxn, xn)

            def rms(k, src, gain, out):
                dve.wait_ge(sm["sq_done"], NT * (k + 1))
                dve.tensor_scalar(var[:, :], mv[:, :, k], 1.0 / D, RMS_EPS, ALU.mult, ALU.add).then_inc(sm["rms_var"], 1)
                dve.wait_ge(sm["rms_std"], k + 1)
                link(dve.reciprocal(rstd[:, :], std[:, :]))
                for tt in range(NT):
                    i = dve.scalar_tensor_tensor(out[:, tt, :], src[:, tt, :], rstd[:, tt:tt + 1], rows[:, gain, :], ALU.mult, ALU.mult)
                    if k == 0:
                        i.then_inc(sm["ln_out"], 1)
                    else:
                        link(i)
                        dve.tensor_tensor(x[:, tt, :], x[:, tt, :], out[:, tt, :], ALU.add).then_inc(sm["out_ready"], 1)

            rms(0, xn, R_N1, xn)

            def cut(a, n, w=1):
                v = gsc[:, a:a + NT * n * w]
                return v.rearrange("p (t n) -> p t n", n=n) if w == 1 else v.rearrange("p (t n w) -> p t n w", n=n, w=w)

            def spread(v, n):
                return bass.AP(v.tensor, v.offset, [v.ap[0], v.ap[1], [0, n]])

            logit, gmax = cut(0, 10), gsc[:, 80:88]
            dve.wait_ge(sm["gate_psum"], 1)
            link(dve.tensor_tensor(logit, ps[:, 7, 0:80].rearrange("p (t n) -> p t n", n=10),
                                   bass.AP(b_gate.tensor, b_gate.offset, [b_gate.ap[0], [0, NT], [1, 10]]), ALU.add))
            link(dve.tensor_reduce(gmax, logit[:, :, 0:NG], AX_X, ALU.max))
            dve.tensor_tensor(cut(112, 2), logit[:, :, 0:NG], spread(gmax, 2), ALU.subtract).then_inc(sm["g_sub"], 1)
            gexp, gsum, grec, gprob = cut(128, 2), gsc[:, 88:96], gsc[:, 96:104], cut(144, 2)
            dve.wait_ge(sm["g_soft"], 1)
            link(dve.tensor_reduce(gsum, gexp, AX_X, ALU.add))
            link(dve.reciprocal(grec, gsum))
            link(dve.tensor_tensor(gprob, gexp, spread(grec, 2), ALU.mult))
            gtop, second, first = gsc[:, 104:112], gsc[:, 160:168], gsc[:, 168:176]
            dve.tensor_reduce(gtop, gprob, AX_X, ALU.max)
            link(dve.tensor_tensor(second, gprob[:, :, 1], gprob[:, :, 0], ALU.is_gt))
            link(dve.tensor_scalar(first, second, -1.0, 1.0, ALU.mult, ALU.add))
            sel, sel2 = cut(192, 4), cut(288, 4)
            dve.tensor_tensor(sel, logit[:, :, 2:6], spread(first, 4), ALU.mult)
            link(dve.tensor_tensor(sel2, logit[:, :, 6:10], spread(second, 4), ALU.mult))
            link(dve.tensor_tensor(sel, sel, sel2, ALU.add))
            emax, esum, erec = gsc[:, 176:184], gsc[:, 184:192], gsc[:, 320:328]
            link(dve.tensor_reduce(emax, sel, AX_X, ALU.max))
            dve.tensor_tensor(cut(224, 4), sel, spread(emax, 4), ALU.subtract).then_inc(sm["e_sub"], 1)
            prob = cut(256, 4)
            dve.wait_ge(sm["e_soft"], 1)
            link(dve.tensor_reduce(esum, prob, AX_X, ALU.add))
            link(dve.reciprocal(erec, esum))
            link(dve.tensor_tensor(prob, prob, spread(erec, 4), ALU.mult))
            link(dve.tensor_tensor(prob, prob, spread(gtop, 4), ALU.mult))
            other = bass.AP(prob.tensor, prob.offset, [prob.ap[0], [4, NT], [0, 4], [1, 4]])
            own = bass.AP(prob.tensor, prob.offset, [prob.ap[0], [4, NT], [1, 4], [0, 4]])
            above, tied, ahead, keep = cut(384, 4, 4), cut(512, 4, 4), cut(640, 4), cut(672, 4)
            dve.tensor_tensor(above, other, own, ALU.is_gt)
            link(dve.tensor_tensor(tied, other, own, ALU.is_equal))
            link(dve.tensor_tensor(tied, tied, bass.AP(tri.tensor, tri.offset, [tri.ap[0], [0, NT], [4, 4], [1, 4]]), ALU.mult))
            link(dve.tensor_tensor(above, above, tied, ALU.add))
            link(dve.tensor_reduce(ahead, above, AX_X, ALU.add))
            link(dve.scalar_tensor_tensor(keep, ahead, 1.5, prob, ALU.is_lt, ALU.mult))
            gate = cut(768, 8)
            dve.tensor_tensor(gate[:, :, 0:4], keep, spread(first, 4), ALU.mult)
            link(dve.tensor_tensor(gate[:, :, 4:8], keep, spread(second, 4), ALU.mult))

            for n in range(8):
                w, k, c = n // 4, (n // 2) % 2, n % 2
                dve.wait_ge(sm["silu_done"], n + 1)
                dve.tensor_tensor(hid[w][:, k, c * 512:c * 512 + 512], ps[:, 2 * (n % 3) + 1, :], silu[:, n % 4, :], ALU.mult
                                  ).then_inc(sm["hid_ready"], 1)
            for tt in range(NT):
                dve.wait_ge(sm["y3_psum"], tt + 1)
                b0 = 3 * (tt % 2)
                link(dve.tensor_tensor(xn[:, tt, :], ps[:, b0 + 2, 0:D], xn[:, tt, :], ALU.add))
                for e in range(NE):
                    i = dve.scalar_tensor_tensor(xn[:, tt, :], ps[:, b0 + e // 4, (e % 4) * D:(e % 4) * D + D], gate[:, tt, e:e + 1],
                                                 xn[:, tt, :], ALU.mult, ALU.add)
                    if e < NE - 1:
                        link(i)
                    else:
                        i.then_inc(sm["y3_done"], 1)
            rms(1, xn, R_N2, shifted)

        @block.tensor
        def _(pe):
            def transpose_x(n):
                for tt in range(NT):
                    pe.wait_ge(sm["ln_out"], NT * n + tt + 1)
                    pe.transpose(ps[:, tt // 4, (tt % 4) * P:(tt % 4) * P + P], xn[:, tt, :], ident[:, :]).then_inc(sm["xT_psum"], 1)

            pe.wait_ge(sm["ld_w"], 80)
            transpose_x(0)
            pe.wait_ge(sm["xT_ready"], 2)
            for n, done in ((0, "q_psum"), (1, "k_psum")):
                for c in range(2):
                    i = pe.matmul(ps[:, 2 + 2 * n + c, :], w_qkv[:, n * D:n * D + D], xnT[:, 512 * c:512 * c + 512], start=True, stop=True)
                i.then_inc(sm[done], 1)
            for tt in range(NT):
                i = pe.matmul(ps[:, 6 + tt // 4, (tt % 4) * P:(tt % 4) * P + P], xnT[:, tt * P:tt * P + P], w_qkv[:, 2 * D:3 * D],
                              start=True, stop=True)
            i.then_inc(sm["v_psum"], 1)

            pe.wait_ge(sm["op_q"], 32)
            pe.wait_ge(sm["op_k"], 32)
            pe.wait_ge(sm["f_ready"], 4)
            pe.wait_ge(sm["v_ready"], 3)
            for n in range(B * IT * (H // 2)):
                tt, p = divmod(n, H // 2)
                b, it = divmod(tt, IT)
                if n >= 4:
                    pe.wait_ge(sm["m_done"], n - 3)
                for e in range(2):
                    i = pe.matmul(ps[:, 2 * (n % 4) + e, :], q_op[64 * e:64 * e + KR, p, tt * P:tt * P + P],
                                  k_op[64 * e:64 * e + KR, 0, p, b * S:b * S + S], start=True, stop=True)
                i.then_inc(sm["s_psum"], 1)
            pe.wait_ge(sm["rel_ready"], 48)
            for n in range(NT * 2):
                tt, u = divmod(n, 2)
                if n < 2:
                    pe.wait_ge(sm["m_done"], 64)
                else:
                    pe.wait_ge(sm["r_done"], n - 1)
                for j in range(2):
                    for k in range(2):
                        for e in range(2):
                            i = pe.matmul(ps[:, 4 * (n % 2) + 2 * e + k, j * (2 * R + 1):(j + 1) * (2 * R + 1)],
                                          q_op[64 * e:64 * e + KR, 4 * u + 2 * k + j, tt * P:tt * P + P],
                                          rel_k[64 * e:64 * e + KR, ZERO - R:ZERO + R + 1], start=True, stop=True)
                i.then_inc(sm["r_psum"], 1)
            pe.wait_ge(sm["negm_ready"], 1)
            for tt in range(NT):
                i = pe.transpose(ps[0:H, tt // 4, (tt % 4) * P:(tt % 4) * P + P], neg_m[:, tt, :], ident[:, :])
            i.then_inc(sm["mT_psum"], 1)

            def bias_block(s, k):
                n, jt = CH * s + k, slots_of(s)[k // 4][0]
                if n >= 1:
                    pe.wait_ge(sm["bias_ready"], n)
                u = s * Q // (S // 2)
                for ii in range(BB):
                    i = Q * s + BB * (k % 4) + ii
                    w = P * jt - i + ZERO
                    mm = pe.matmul(ps[:, 4, B * H * ii:B * H * (ii + 1)], rel_k[64 * u:64 * u + KR, w:w + P],
                                   q_rel[64 * u:64 * u + KR, :, i - u * (S // 2)], start=True, stop=True)
                mm.then_inc(sm["bias_psum"], 1)

            def scores(n):
                s, c = divmod(n, CH)
                g, b = divmod(c, 2)
                if n >= 2:
                    pe.wait_ge(sm["z_ready"], n - 1)
                    pe.wait_ge(sm["oexp_done"], n - 1)
                for slot, (jt, v) in enumerate(slots_of(s)):
                    for a in range(2):
                        for e in range(2):
                            col = 2 * P * a + Q * slot
                            i = pe.matmul(ps[:, 2 * (n % 2) + e, col:col + Q],
                                          k_op[64 * e:64 * e + KR + 1, v, 2 * g + a, b * S + jt * P:b * S + jt * P + P],
                                          q_op[64 * e:64 * e + KR + 1, 2 * g + a, b * S + Q * s:b * S + Q * s + Q],
                                          start=True, stop=True)
                i.then_inc(sm["st_psum"], 1)

            def products(n):
                s, c = divmod(n, CH)
                g, b = divmod(c, 2)
                pe.wait_ge(sm["oexp_done"], n + 1)
                pe.wait_ge(sm["zexp_done"], n + 1)
                if c == 0 and s >= 2:
                    pe.wait_ge(sm["ctx_ready"], s - 1)
                for slot, (jt, v) in enumerate(slots_of(s)):
                    for hh in range(4):
                        h = 4 * g + hh
                        if slot < 2:
                            rhs = band[:, s % 3, 2 * h + b, slot * Q:slot * Q + Q]
                        else:
                            rhs = p_out[:, n % 2, hh, (slot - 2) * Q:(slot - 1) * Q]
                        i = pe.matmul(ps[32 * hh:32 * hh + VW, 5 + s % 2, Q * c:Q * c + Q],
                                      v_sb[:, v, IT * b + jt, h * VW:h * VW + VW], rhs,
                                      start=(c == 0 and slot == 0), stop=False, skip_group_check=True)
                i.then_inc(sm["pv_done"], 1)

            def rel_values(s, c):
                kb = 4 * s + c // 2
                if c == 0:
                    pe.wait_ge(sm["zexp_done"], CH * (s + 1))
                if c % 2 == 0 and kb >= 1:
                    pe.wait_ge(sm["crel_ready"], kb)
                for ii in range(8):
                    for slot in range(2):
                        jt = slots_of(s)[slot][0]
                        w = P * jt - (Q * s + 8 * c + ii) + ZERO
                        o = 8 * (c % 2) + ii
                        i = pe.matmul(ps[0:HD, 7, B * H * o:B * H * (o + 1)], rel_v[:, w * HD:(w + 1) * HD],
                                      band[:, s % 3, :, slot * Q + 8 * c + ii], start=(slot == 0), stop=(slot == 1))
                if c % 2:
                    i.then_inc(sm["vrel_psum"], 1)

            def add_crel(s):
                pe.wait_ge(sm["crel_ready"], 4 * (s + 1))
                for c in range(CH):
                    g, b = divmod(c, 2)
                    for hh in range(4):
                        i = pe.matmul(ps[32 * hh:32 * hh + HD, 5 + s % 2, Q * c:Q * c + Q], ident[0:HD, 0:HD],
                                      crel[:, :, 2 * (4 * g + hh) + b], start=False, stop=True, skip_group_check=True)
                i.then_inc(sm["crel_added"], 1)

            pe.wait_ge(sm["op_qrel"], 64)
            pe.wait_ge(sm["pv_zero"], 1)
            for k in range(CH):
                bias_block(0, k)
            for name, val in (("m_rows", 64), ("ld_one", 32), ("op_lo", 32), ("op_hi", 32), ("mT_ready", 1)):
                pe.wait_ge(sm[name], val)
            scores(0)
            for n in range(STEPS * CH + 2 * CH):
                s, c = divmod(n, CH)
                if n + 1 < STEPS * CH:
                    scores(n + 1)
                if s + 1 < STEPS:
                    bias_block(s + 1, c)
                if c == 0 and s >= 2:
                    add_crel(s - 2)
                if 1 <= n <= STEPS * CH:
                    products(n - 1)
                if 1 <= s <= STEPS:
                    rel_values(s - 1, c)

            def attn_finish(k, src, w):
                for tt in range(NT + 2):
                    b, it = divmod(tt, IT)
                    if tt < NT:
                        if tt >= 2:
                            pe.wait_ge(sm["ctx_norm"], NT * k + tt - 1)
                        for g in range(4):
                            i = pe.transpose(ps[:, tt % 2, g * P:g * P + P], ctxT[:, 2 * g + b, it * P:it * P + P], ident[:, :])
                        i.then_inc(sm["ctx_tr"], 1)
                    if 1 <= tt <= NT:
                        u = tt - 1
                        pe.wait_ge(sm["ctx_norm"], NT * k + u + 1)
                        if u >= 2:
                            pe.wait_ge(sm["cn_ready"], NT * k + u - 1)
                        pe.transpose(ps[:, 2 + u % 2, 0:P], src[:, u, :], ident[:, :]).then_inc(sm["cn_psum"], 1)
                    if tt >= 2:
                        u = tt - 2
                        pe.wait_ge(sm["cn_ready"], NT * k + u + 1)
                        if u >= 2:
                            pe.wait_ge(sm["x_added"], NT * k + u - 1)
                        pe.matmul(ps[:, 4 + u % 2, 0:P], xnT[:, u * P:u * P + P], w, start=True, stop=True).then_inc(sm["y_psum"], 1)

            pe.wait_ge(sm["ctx_ready"], STEPS)
            attn_finish(0, xn, w_out[:, :])

            pe.wait_ge(sm["ln_out"], 2 * NT)
            for b in range(B):
                i = pe.transpose(ps[:, 0, CTX * b:CTX * b + CTX], xn[0:CTX, IT * b + 2, :], ident[0:CTX, 0:CTX])
            i.then_inc(sm["memT_psum"], 1)
            pe.wait_ge(sm["memT_ready"], 1)
            pe.wait_ge(sm["ld_wide"], 16 * 6)
            for r in range(RATE):
                i = pe.matmul(ps[0:B * CONV, 1, 0:D], memT[:, r:B * CTX:RATE], w_conv[:, r, :], start=(r == 0), stop=(r == RATE - 1))
            i.then_inc(sm["comp_psum"], 1)

            def transpose_again(k, n):
                for tt in range(NT):
                    pe.wait_ge(sm["ln_out"], NT * n + tt + 1)
                    pe.transpose(ps[:, tt // 4, (tt % 4) * P:(tt % 4) * P + P], xn[:, tt, :], ident[:, :]).then_inc(sm["xT_psum"], 1)
                pe.wait_ge(sm["xT_ready"], 2 * (k + 1))

            transpose_again(1, 2)
            pe.wait_ge(sm["sw_ready"], 4)

            def project(bank, w, rhs, done):
                for c in range(2):
                    i = pe.matmul(ps[0:w.shape[1], bank + c, :], w, rhs[:, 512 * c:512 * c + 512], start=True, stop=True)
                i.then_inc(sm[done], 1) if done else None
                return i

            project(4, w_kc, xnT, "lat_psum")
            project(2, w_q, xnT, None)
            pe.wait_ge(sm["lat_ready"], 1)
            project(6, w_vc, xnT, "lat_psum")
            pe.wait_ge(sm["lat_ready"], 2)
            project(6, w_qs, xnT, "q2_psum")
            for tt in range(NT):
                i = pe.matmul(ps[:, 4 + tt // 4, (tt % 4) * P:(tt % 4) * P + P], latT[1][:, tt * P:tt * P + P], w_v, start=True, stop=True)
            i.then_inc(sm["v2_psum"], 1)
            project(0, w_k, latT[0], None)
            pe.wait_ge(sm["ropeq_ready"], 1)
            project(2, w_ks, latT[0], "k2_psum")

            pe.wait_ge(sm["op_q"], 64)
            pe.wait_ge(sm["op_k"], 64)
            pe.wait_ge(sm["ropeq_ready"], 2)
            pe.wait_ge(sm["v2_ready"], 1)
            for j in range(-32, 128 + 8):
                if 0 <= j < 128:
                    n, k = divmod(j, 16)
                    b, g = divmod(n, 4)
                    jt, hh = divmod(k, 4)
                    a, e = divmod(hh, 2)
                    if k == 0:
                        pe.wait_ge(sm["n_rows" if n % 2 == 0 else "n_rows_odd"], 32 * (n // 2 + 1))
                    if j >= 2:
                        pe.wait_ge(sm["g_exp"], j - 1)
                    pe.matmul(ps[:, 4 + j % 2, :], k_op[64 * e:64 * e + KR + 1, 0, 2 * g + a, b * S + jt * P:b * S + jt * P + P],
                              q_op[64 * e:64 * e + KR + 1, 2 * g + a, b * S:b * S + S], start=True, stop=True).then_inc(sm["g_psum"], 1)
                if j % 2 == 0 and (j + 32) // 2 < 64:
                    su = (j + 32) // 2
                    m, k = divmod(su, 8)
                    b, g = divmod(m, 4)
                    a, it = divmod(k, 4)
                    if su >= 2:
                        pe.wait_ge(sm["t_done"], su - 1)
                    for e in range(2):
                        i = pe.matmul(ps[:, 2 * (su % 2) + e, :], q_op[64 * e:64 * e + KR, 2 * g + a, b * S + it * P:b * S + it * P + P],
                                      k_op[64 * e:64 * e + KR, 0, 2 * g + a, b * S:b * S + S], start=True, stop=True)
                    i.then_inc(sm["t_psum"], 1)
                if j % 16 == 1 and 0 <= j // 16 + 1 < 8:
                    m = j // 16 + 1
                    b, g = divmod(m, 4)
                    pe.wait_ge(sm["n_ready"], m + 1)
                    if m >= 1:
                        pe.wait_ge(sm["nT_ready"], m)
                    for it in range(IT):
                        i = pe.transpose(ps[0:4, 7, it * P:it * P + P], neg_m[:, IT * b + it, 4 * g:4 * g + 4], ident[:, :])
                    i.then_inc(sm["nT_psum"], 1)
                if j >= 6 and (j - 6) % 4 == 0 and (j - 6) // 4 < 32:
                    k = (j - 6) // 4
                    n, jt = divmod(k, 4)
                    b, g = divmod(n, 4)
                    pe.wait_ge(sm["g_exp"], 4 * k + 4)
                    if jt == 0 and n >= 1:
                        pe.wait_ge(sm["g_ctx"], n)
                    for hh in range(4):
                        h = 4 * g + hh
                        i = pe.matmul(ps[32 * hh:32 * hh + VW, 6, :], v_sb[:, 0, IT * b + jt, h * VW:h * VW + VW],
                                      p_ring[:, k % 3, hh, :], start=(jt == 0), stop=(jt == IT - 1))
                    i.then_inc(sm["g_pv"], 1)

            pe.wait_ge(sm["g_ctx"], 8)
            attn_finish(1, ctxn, w_o)

            pe.wait_ge(sm["x_added"], 2 * NT)
            transpose_again(2, 3)
            for tt in range(NT):
                i = pe.matmul(ps[:, 7, 10 * tt:10 * tt + 10], xnT[:, tt * P:tt * P + P], w_gate, start=True, stop=True)
            i.then_inc(sm["gate_psum"], 1)
            for n in range(8):
                w, k, c = n // 4, (n // 2) % 2, n % 2
                if n >= 3:
                    pe.wait_ge(sm["hid_ready"], n - 2)
                for z in range(2):
                    i = pe.matmul(ps[:, 2 * (n % 3) + z, :], w_in[w][:, HID * z + P * k:HID * z + P * k + P], xnT[:, c * 512:c * 512 + 512],
                                  start=True, stop=True)
                i.then_inc(sm["a_psum"], 1)
            pe.wait_ge(sm["hid_ready"], 8)
            for tt in range(NT):
                b0 = 3 * (tt % 2)
                if tt >= 2:
                    pe.wait_ge(sm["y3_done"], tt - 1)
                for c in range(2):
                    for k in range(2):
                        pe.matmul(ps[:, b0 + c, :], hid[1][:, k, tt * P:tt * P + P], w_2[:, k, c * 512:c * 512 + 512],
                                  start=(k == 0), stop=(k == 1))
                for k in range(2):
                    i = pe.matmul(ps[:, b0 + 2, 0:D], hid[0][:, k, tt * P:tt * P + P], w_so[:, k, :], start=(k == 0), stop=(k == 1))
                i.then_inc(sm["y3_psum"], 1)


def kernel(**inputs):
    import numpy as np
    import concourse.bacc as bacc
    from concourse.bass_utils import run_bass_kernel_spmd

    a = {k: np.ascontiguousarray(v) for k, v in inputs.items()}
    off = np.clip(np.arange(EXT) - ZERO, -R, R) + R
    relk, relv = a["L0_attn_rel_emb_k"], a["L0_attn_rel_emb_v"]
    bqkv = a["L0_attn_b_qkv"]
    import ml_dtypes
    freq = (np.float32(1.0) / np.float32(10000.0) ** (np.arange(0, HD, 2, dtype=np.float32) / np.float32(HD))).astype(np.float32)
    angle = np.tile(np.repeat(freq, 2), H)[:, None] * np.arange(S, dtype=np.float32)[None, :]
    arrays = {
        "x": a["x"],
        "w_qkv": a["L0_attn_W_qkv"],
        "w_out": a["L0_attn_W_out"],
        "ident": np.eye(P, dtype=np.float32),
        "ones": np.ones((1, 3 * (H // 2) * TOK), ml_dtypes.bfloat16),
        "cols": np.ascontiguousarray(np.stack([bqkv[:D], bqkv[D:2 * D], np.tile(relk[0], H), np.tile(relk[2 * R], H)], 1)),
        "rows": np.ascontiguousarray(np.stack([bqkv[2 * D:], np.tile(relv[0], H), np.tile(relv[2 * R], H), a["L0_attn_b_out"],
                          a["L0_xattn_conv_b"], a["L0_ffn_norm1_w"], a["L0_ffn_norm2_w"]])),
        "relk_ext": np.ascontiguousarray(relk[off].T),
        "relv_ext": relv[off],
        "ctx": a["ctx_1024"],
        "w_conv": a["L0_xattn_conv_w"],
        "w_q": a["L0_ffn_Wq"], "w_kc": a["L0_ffn_Wk_c"], "w_vc": a["L0_ffn_Wv_c"],
        "w_k": a["L0_ffn_Wk"], "w_v": a["L0_ffn_Wv"], "w_o": a["L0_ffn_Wo"],
        "w_sin": a["L0_ffn_W_shared_in"], "w_so": a["L0_ffn_W_shared_out"],
        "w_1": a["L0_ffn_W1_shared"], "w_2": a["L0_ffn_W2_experts"],
        "w_gg": a["L0_ffn_Wg_gate"], "w_ge": a["L0_ffn_We_gate"],
        "b_gg": a["L0_ffn_group_bias"], "b_ge": a["L0_ffn_expert_bias"],
        "cos": np.ascontiguousarray(np.cos(angle)), "sin": np.ascontiguousarray(np.sin(angle)),
        "tri": np.tril(np.ones((EPG, EPG), np.float32), -1).reshape(-1),
    }
    nc = bacc.Bacc("TRN2", target_bir_lowering=False, num_devices=1)
    t = {n: nc.dram_tensor("in_" + n, v.shape, mybir.dt.from_np(v.dtype), kind="ExternalInput").ap() for n, v in arrays.items()}
    t["scr"] = nc.dram_tensor("scr", (4, P, SLOTS, TOK), BF16, kind="Internal").ap()
    t["scr_rel"] = nc.dram_tensor("scr_rel", (HD, SLOTS, EXT), BF16, kind="Internal").ap()
    t["out"] = nc.dram_tensor("out", (B, S, D), F32, kind="ExternalOutput").ap()
    build(nc, t)
    r = run_bass_kernel_spmd(nc, [{"in_" + n: v for n, v in arrays.items()}], core_ids=[0])
    return r.results[0]["out"]
```

```python
from contextlib import ExitStack

import concourse.bass as bass
from concourse import mybir

F32 = mybir.dt.float32
BF16 = mybir.dt.bfloat16
ALU = mybir.AluOpType
ACT = mybir.ActivationFunctionType
AX_X = mybir.AxisListType.X

P = 128
B, S, D, H = 2, 512, 128, 16
HD = D // H
NT = B * S // P
IT = S // P
TOK = B * S
R = 64
SLOTS = 6
KR = HD * SLOTS
PR = 64 + KR
Q_PARTS = (0, 1, 2, 0, 0, 1)
K_PARTS = (0, 0, 0, 1, 2, 1)
EXT = 512
ZERO = 255
VW = HD + 1
DC, HID, NE, NG = 32, 256, 8, 2
EPG = NE // NG
LN_EPS, RMS_EPS = 1e-5, 1e-6
Q_SCALE = float(HD) ** -0.5
Q = 64
STEPS = S // Q
CH = 8
BB = 16
XB = (3, 7)
V_ACT = (0, 1, 2, 3)
V_DVE = tuple(q for q in range(4) if q not in V_ACT)
FIRST_BIAS = 24
HI_AT = 0
M_LEAD = 4
CTX, RATE = 32, 4
CONV = CTX // RATE
C_BQ, C_BK, C_LO, C_HI = range(4)
R_BV, R_LO, R_HI, R_BOUT, R_CONV, R_N1, R_N2 = range(7)


def slots_of(s):
    it, half = divmod(s, 2)
    ja = min(max(it if half else it - 1, 0), IT - 2)
    rest = [j for j in range(IT) if j not in (ja, ja + 1)]
    return [(ja, 0), (ja + 1, 0)] + [(j, 1 if j < ja else 2) for j in rest]


def shared_bank_units():
    units, count = [], {}

    def add(n, kind, args, sem, k=1):
        count[sem] = count.get(sem, 0) + k
        units.append((n, kind, args, sem, count[sem]))

    of_tile = {it: [("s", (IT * b + it, p, e)) if r is None else ("r", (IT * b + it, r, e))
                    for b in range(B) for p, r in [(p, None) for p in range(H // 2)] + [(None, r) for r in range(3)]
                    for e in range(2)] for it in range(IT)}
    plan = [(-1, u) for u in of_tile[0]] + [(-1, ("m", (0,)))]
    for it in range(1, IT):
        first = 0 if it == 1 else 2 * CH * (it - 1) - M_LEAD
        last = 2 * CH * it - M_LEAD
        us = of_tile[it]
        plan += [(first + k * (last - first) // len(us), u) for k, u in enumerate(us)] + [(last, ("m", (it,)))]
    for s_ in range(STEPS):
        plan += [(CH * (s_ + 1) + 2 + 3 * u, ("v", (s_, u))) for u in range(2)]
    for n, (kind, args) in sorted(plan, key=lambda x: x[0]):
        add(n, kind, args, {"s": "m_done", "r": "r_done", "m": "mT_ready", "v": "crel_ready"}[kind], 4 if kind == "v" else 1)
    return units


def build(nc, t):
    with ExitStack() as ctx:
        def sb(name, shape, dt=F32):
            return ctx.enter_context(nc.sbuf_tensor(name, shape, dt))

        x = sb("x_sb", [P, NT, D])
        xn = sb("xn", [P, NT, D])
        xnT = sb("xnT", [P, TOK])
        q_op = sb("q_op", [P, 2, H // 2, TOK], BF16)
        k_op = sb("k_op", [P, 3, H // 2, TOK], BF16)
        band = sb("band", [P, 3, B * H, P])
        v_sb = sb("v_sb", [P, 3, NT, H * VW])
        rel_v = sb("rel_v", [P, 384 * HD])
        rel_k = sb("rel_k", [P, EXT], BF16)
        ctxT = sb("ctxT", [P, CH, S])
        p_out = sb("p_out", [P, 2, 4, P])
        crel = sb("crel", [HD, Q, B * H])
        ident = sb("ident", [P, P])
        rows = sb("rows", [P, 8, D])
        cols = sb("cols", [P, 8])
        w_qkv = sb("w_qkv", [P, 3 * D])
        w_out = sb("w_out", [P, D])
        stats = sb("stats", [P, NT, 6])
        mv = sb("mv", [P, NT, 2])
        var = sb("var", [P, NT])
        std = sb("std", [P, NT])
        rstd = sb("rstd", [P, NT])
        m_qk = sb("m_qk", [P, NT, H])
        m_rel = sb("m_rel", [P, NT, H])
        neg_m = sb("neg_m", [P, NT, H])
        rsum = sb("rsum", [P, 2, H])
        arena = band[:, :, :, :].rearrange("p a b c -> p (a b c)")
        f32_of = [arena[:, n * TOK:(n + 1) * TOK] for n in (0, 1, 8, 2)]
        rest_dve = arena[:, 3 * TOK:4 * TOK]
        scratchT = ctxT[:, :, :].rearrange("p a b -> p (a b)")
        v_f32 = arena[:, 7 * TOK:8 * TOK]
        rest_pool = scratchT[:, 3 * TOK:4 * TOK]
        parts_q, parts_k, parts_lo, parts_hi = (m.bitcast(BF16).rearrange("p (s t) -> p s t", s=SLOTS) for m in
                                      (arena[:, 4 * TOK:7 * TOK], rel_v[:, :], arena[:, 9 * TOK:12 * TOK], scratchT[:, 0:3 * TOK]))
        relk_f, relk_rest = (p_out[0:HD, n, :, :].rearrange("p a b -> p (a b)") for n in range(2))
        relk_parts = crel[:, :, :].rearrange("d i h -> d (i h)")[:, 0:3 * EXT].bitcast(BF16).rearrange("p (s t) -> p s t", s=SLOTS)
        neg_mT = sb("neg_mT", [H, B * P], BF16)
        spare = k_op[:, 1:3, :, :].rearrange("p v a t -> p (v a t)").bitcast(F32)
        wide = spare[:, 2048:5888]
        w_conv = wide[:, 0:512].rearrange("p (r o) -> p r o", r=RATE)
        w_in = [wide[:, 512 + 512 * n:1024 + 512 * n] for n in range(2)]
        w_so = wide[:, 1536:1792].rearrange("p (k o) -> p k o", k=2)
        w_2 = wide[:, 1792:3840].rearrange("p (k n) -> p k n", k=2)
        cos, sin = spare[:, 0:S], spare[:, S:2 * S]
        w_q, w_o = spare[:, 1024:1152], spare[:, 1152:1280]
        w_kc, w_vc = spare[:, 1280:1312], spare[:, 1312:1344]
        w_k, w_v = spare[0:DC, 1344:1472], spare[0:DC, 1472:1600]
        w_gate, b_gate = spare[:, 1600:1610], spare[:, 1610:1620]
        tri = spare[:, 1620:1636]
        w_qs, w_ks = spare[:, 1664:1792], spare[0:DC, 1792:1920]
        p_ring = arena[:, 0:8192].rearrange("p (r h t) -> p r h t", r=4, h=4)
        hid = [arena[:, 2048 * n:2048 + 2048 * n].rearrange("p (k t) -> p k t", k=2) for n in range(2)]
        silu = arena[:, 4096:6144].rearrange("p (r t) -> p r t", r=4)
        shifted = scratchT[:, 0:NT * D].rearrange("p (t d) -> p t d", d=D)
        memT, comp = scratchT[:, 1024:1088], scratchT[0:B * CONV, 1088:1216]
        latT = [scratchT[0:DC, 2048:3072], scratchT[0:DC, 3072:4096]]
        parts2 = [arena[:, (6 + 3 * n) * TOK:(9 + 3 * n) * TOK].bitcast(BF16).rearrange("p (s t) -> p s t", s=SLOTS) for n in range(2)]
        rest2 = arena[:, 4 * TOK:5 * TOK]
        ctxn = arena[:, 10240:11264].rearrange("p (t d) -> p t d", d=D)
        squares = arena[:, 9216:10240].rearrange("p (t d) -> p t d", d=D)
        nm_T = crel[0:4, 0:16, :].rearrange("d i h -> d (i h)").bitcast(BF16).rearrange("d (r t) -> d r t", r=2)
        q_flat = q_op[:, :, :, :].rearrange("r e p (b t) -> r (e p b) t", b=B)
        gsc = arena[:, 8192:9216]
        ps = ctx.enter_context(nc.psum_tensor("ps", [P, 8, 512], F32))

        units = shared_bank_units()
        names = """x_psum ld_x ld_w ld_rel ld_one ln_var ln_std ln_out xT_psum xT_ready
        q_psum k_psum v_psum f_ready cols_ready rows_ready q_split k_split lo_split hi_split lo_ready hi_ready relv_ready v_ready vf_ready
        scr_q scr_k scr_lo scr_hi scr_rel op_q op_k op_lo op_hi rel_zero rel_ready rel_split
        s_psum m_done r_psum r_done negm_ready mT_psum mT_ready m_rows pv_zero
        bias_psum bias_ready st_psum z_ready zexp_done oexp_done pv_done vrel_psum crel_ready
        crel_added ctx_ready ctx_tr ctx_norm cn_psum cn_ready y_psum x_added xb_ready
        ld_wide ld_spare ld_ctx shift_in shift1 shift_done memT_psum memT_ready comp_psum comp_ready
        x2_ready sw_ready lat_psum lat_ready q2_psum k2_psum v2_psum v2_ready rot_done part_ready rope_psum latk_psum latv_psum latk_ready latv_ready
        t_psum t_done n_ready nT_psum nT_ready n_rows n_rows_odd out_ready g_psum g_exp g_pv g_ctx g_nfree
        sq_done rms_var rms_std gate_psum g_sub g_soft e_sub e_soft gate_done a_psum silu_done hid_ready y3_psum
        y3_done sq2_done dve pool out_done v_one""".split()
        sm = {n: ctx.enter_context(nc.semaphore(n)) for n in names}
        block = ctx.enter_context(nc.Block())

        def row_of(h, b):
            return H * (h % 2) + 2 * (h // 2) + b

        def units_of(n):
            return [(k, *u[1:]) for k, u in enumerate(units) if u[0] == n]

        @block.sync
        def _(sp):
            sp.dma_start(x[:, :, :], t["x"].rearrange("b (t p) d -> p (b t) d", p=P)).then_inc(sm["ld_x"], 16)
            sp.dma_start(ident[:, :], t["ident"]).then_inc(sm["ld_w"], 16)
            sp.dma_start(w_qkv[:, :], t["w_qkv"]).then_inc(sm["ld_w"], 16)
            sp.dma_start(cols[:, 0:4], t["cols"]).then_inc(sm["ld_w"], 16)
            sp.dma_start(relk_f, t["relk_ext"]).then_inc(sm["ld_rel"], 16)
            sp.dma_start(rows[:, 0:7, :], bass.AP(t["rows"].tensor, 0, [[0, P], [1, 7 * D]])).then_inc(sm["ld_w"], 16)
            sp.dma_start(w_out[:, :], t["w_out"]).then_inc(sm["ld_w"], 16)
            zeros = lambda r, n: bass.AP(t["zeros"].tensor, 0, [[0, r], [1, n]])
            sp.dma_start(k_op[PR:PR + 1, :, :, :].rearrange("o a b c -> o (a b c)"), t["ones"]).then_inc(sm["ld_one"], 16)
            sp.dma_start(k_op[KR:64, :, :, :].rearrange("o a b c -> o (a b c)"), zeros(64 - KR, 3 * (H // 2) * TOK)).then_inc(sm["ld_one"], 16)
            for e, (r0, r1) in enumerate(((KR, PR), (0, 64))):
                sp.dma_start(q_op[r0:r1, e, :, :].rearrange("o b c -> o (b c)"), zeros(r1 - r0, (H // 2) * TOK)).then_inc(sm["ld_one"], 16)
            sp.dma_start(rel_k[:, :], bass.AP(t["zeros"].tensor, 0, [[0, P], [1, EXT]])).then_inc(sm["rel_zero"], 16)


            def write_parts(n, parts, done, val, scr, cols_=slice(0, TOK)):
                sp.wait_ge(sm[done], val)
                sp.dma_start(t["scr"][n][:, :, cols_], parts[:, :, cols_]).then_inc(sm[scr], 16)

            def read_rows(n, dst, scr, val, op, c0=0, w=TOK):
                sp.wait_ge(sm[scr], val)
                for e in range(2):
                    src = bass.AP(t["scr"].tensor, n * P * SLOTS * TOK + e * KR * TOK + c0,
                                  [[TOK, KR], [2 * KR * TOK, H // 2], [1, w]])
                    sp.dma_start((dst[64 * e:64 * e + KR, e] if op == "op_q" else dst[64 * e:64 * e + KR])[:, :, c0:c0 + w], src).then_inc(sm[op], 16)

            wq = lambda b: write_parts(0, parts_q, "q_split", b + 1, "scr_q", slice(b * S, b * S + S))
            wk = lambda b: write_parts(1, parts_k, "k_split", b + 1, "scr_k", slice(b * S, b * S + S))
            rq = lambda b: read_rows(0, q_op, "scr_q", 16 * (b + 1), "op_q", b * S, S)
            rk = lambda b: read_rows(1, k_op[:, 0], "scr_k", 16 * (b + 1), "op_k", b * S, S)
            wq(0)
            wk(0)
            rq(0)
            rk(0)
            wq(1)
            sp.wait_ge(sm["rel_split"], 1)
            sp.dma_start(t["scr_rel"].rearrange("d s n -> d s n"), relk_parts).then_inc(sm["scr_rel"], 16)
            wk(1)
            rq(1)
            sp.wait_ge(sm["scr_rel"], 16)
            sp.wait_ge(sm["rel_zero"], 16)
            for u in range(2):
                sp.dma_start(rel_k[64 * u:64 * u + KR, :],
                             t["scr_rel"].rearrange("d s n -> (d s) n")).then_inc(sm["rel_ready"], 16)
            rk(1)
            write_parts(3, parts_hi, "hi_split", 1, "scr_hi")
            sp.dma_start(rel_v[:, :], bass.AP(t["relv_ext"].tensor, 0, [[HD, P], [1, 384 * HD]])
                         ).then_inc(sm["relv_ready"], 16)
            read_rows(3, k_op[:, 2], "scr_hi", 16, "op_hi")
            write_parts(2, parts_lo, "lo_split", 1, "scr_lo")
            read_rows(2, k_op[:, 1], "scr_lo", 16, "op_lo")
            for it in range(IT):
                sp.wait_ge(sm["mT_ready"], it + 1)
                for e in range(2):
                    dst = q_op[PR:PR + 1, e, :, :].rearrange("o p (b t) -> o p b t", b=B)[:, :, :, it * P:it * P + P]
                    sp.dma_start(dst, neg_mT[8 * e:8 * e + 8, :].rearrange("p (b t) -> p b t", b=B)).then_inc(sm["m_rows"], 16)
            sp.wait_ge(sm["st_psum"], 2 * STEPS * CH)
            sp.dma_start(w_conv, t["w_conv"].rearrange("r i o -> i r o")).then_inc(sm["ld_wide"], 16)
            sp.dma_start(w_in[0], t["w_sin"]).then_inc(sm["ld_wide"], 16)
            sp.dma_start(w_in[1], t["w_1"]).then_inc(sm["ld_wide"], 16)
            sp.dma_start(w_so, t["w_so"].rearrange("(k i) o -> i k o", i=P)).then_inc(sm["ld_wide"], 16)
            for k in range(2):
                sp.dma_start(w_2[:, k, :].rearrange("p (e o) -> p e o", e=NE),
                             t["w_2"].rearrange("e (k i) o -> k i e o", i=P)[k]).then_inc(sm["ld_wide"], 16)
            for dst, name in ((cos, "cos"), (sin, "sin"), (w_q, "w_q"), (w_o, "w_o"), (w_kc, "w_kc"), (w_vc, "w_vc"),
                              (w_k, "w_k"), (w_v, "w_v"), (w_gate[:, 0:NG], "w_gg"), (w_gate[:, NG:], "w_ge")):
                sp.dma_start(dst, t[name]).then_inc(sm["ld_spare"], 16)
            for dst, name, n in ((b_gate[:, 0:NG], "b_gg", NG), (b_gate[:, NG:], "b_ge", NE), (tri, "tri", 16)):
                sp.dma_start(dst, bass.AP(t[name].tensor, 0, [[0, P], [1, n]])).then_inc(sm["ld_spare"], 16)
            sp.wait_ge(sm["ctx_tr"], NT)
            sp.dma_start(shifted[P - CTX:P, 3:NT:4, :], t["ctx"].rearrange("b t d -> t b d")).then_inc(sm["shift_in"], 16)
            sp.wait_ge(sm["ln_out"], 2 * NT)
            by_b = lambda a: a.rearrange("p (b t) d -> p b t d", b=B)
            for sh, t0 in ((CONV, 0), (CTX, 2)):
                sp.dma_start(by_b(shifted[0:P - sh, :, :])[:, :, t0:t0 + 2, :],
                             by_b(xn[sh:P, :, :])[:, :, t0:t0 + 2, :]).then_inc(sm["shift_in"], 16)
                sp.dma_start(shifted[P - sh:P, t0:NT:4, :], xn[0:sh, t0 + 1:NT:4, :]).then_inc(sm["shift_in"], 16)
            sp.wait_ge(sm["comp_ready"], 1)
            for b in range(B):
                sp.dma_start(shifted[P - CONV:P, IT * b + 1, :], comp[CONV * b:CONV * b + CONV, :]).then_inc(sm["shift_in"], 16)
            for b in range(B):
                bs = slice(b * S, b * S + S)
                write_parts(0, parts2[0], "q_split", b + 3, "scr_q", bs)
                write_parts(1, parts2[1], "k_split", b + 3, "scr_k", bs)
                read_rows(0, q_op, "scr_q", 16 * (b + 3), "op_q", b * S, S)
                read_rows(1, k_op[:, 0], "scr_k", 16 * (b + 3), "op_k", b * S, S)
            for n in range(B * 4):
                b, g = divmod(n, 4)
                sp.wait_ge(sm["nT_ready"], n + 1)
                for e in range(2):
                    sp.dma_start(q_op[PR:PR + 1, e, 2 * g:2 * g + 2, b * S:b * S + S],
                                 nm_T[2 * e:2 * e + 2, n % 2, :]).then_inc(sm["n_rows" if n % 2 == 0 else "n_rows_odd"], 16)
            for tt in range(NT):
                b, it = divmod(tt, IT)
                sp.wait_ge(sm["out_ready"], tt + 1)
                sp.dma_start(t["out"][b, it * P:it * P + P, :], x[:, tt, :]).then_inc(sm["out_done"], 16)
            sp.wait_ge(sm["out_done"], 16 * NT)

        @block.gpsimd
        def _(pool):
            chain = [0]

            def link(ins):
                chain[0] += 1
                ins.then_inc(sm["pool"], 1)
                pool.wait_ge(sm["pool"], chain[0])

            ones_col = v_sb[:, :, :, :].rearrange("p v t (h w) -> p (v t h) w", w=VW)[:, :, HD:VW]
            pool.memset(ones_col, 1.0).then_inc(sm["v_one"], 1)
            pool.wait_ge(sm["ld_w"], 80)
            pool.tensor_scalar(cols[:, 4:5], cols[:, C_BQ:C_BQ + 1], Q_SCALE, None, ALU.mult)
            pool.tensor_scalar(cols[:, 5:7], cols[:, C_LO:C_HI + 1], cols[:, C_BK:C_BK + 1], None, ALU.add).then_inc(sm["cols_ready"], 1)
            for r in (R_LO, R_HI):
                link(pool.tensor_tensor(rows[:, r, :], rows[:, r, :], rows[:, R_BV, :], ALU.add))
            pool.wait_ge(sm["ld_rel"], 16)
            link(pool.tensor_copy(relk_parts[:, 0, :], relk_f))
            link(pool.tensor_tensor(relk_rest, relk_f, relk_parts[:, 0, :], ALU.subtract))
            link(pool.tensor_copy(relk_parts[:, 3, :], relk_rest))
            link(pool.tensor_tensor(relk_parts[:, 4, :], relk_rest, relk_parts[:, 3, :], ALU.subtract))
            for s in (1, 2):
                pool.tensor_copy(relk_parts[:, s, :], relk_parts[:, 0, :])
            link(pool.tensor_copy(relk_parts[:, 5, :], relk_parts[:, 3, :]))
            pool.sem_inc(sm["rel_split"], 1)
            pool.wait_ge(sm["vf_ready"], 1)
            pool.wait_ge(sm["v_one"], 1)
            for v, r in enumerate((R_BV, R_LO, R_HI)):
                row = rows[:, r, :]
                add = bass.AP(row.tensor, row.offset, [[8 * D, P], [0, NT], [HD, H], [1, HD]])
                pool.tensor_tensor(v_sb[:, v, :, :].rearrange("p t (h w) -> p t h w", w=VW)[:, :, :, 0:HD],
                                  v_f32.rearrange("p (t h d) -> p t h d", t=NT, d=HD), add, ALU.add
                                  ).then_inc(sm["v_ready"], 1)
            f, o = f32_of[2], parts_lo
            pool.wait_ge(sm["lo_ready"], 2)
            link(pool.tensor_tensor(rest_pool, f, o[:, 0, :], ALU.subtract))
            link(pool.tensor_copy(o[:, 3, :], rest_pool))
            link(pool.tensor_tensor(o[:, 4, :], rest_pool, o[:, 3, :], ALU.subtract))
            link(pool.tensor_copy(o[:, 1, :], o[:, 0, :]))
            link(pool.tensor_copy(o[:, 2, :], o[:, 0, :]))
            pool.tensor_copy(o[:, 5, :], o[:, 3, :]).then_inc(sm["lo_split"], 1)
            pool.wait_ge(sm["ln_out"], NT)
            pool.wait_ge(sm["ld_w"], 80)
            pool.tensor_tensor(x[:, :, :], x[:, :, :], bass.AP(rows[:, R_BOUT, :].tensor, rows[:, R_BOUT, :].offset, [[8 * D, P], [0, NT], [1, D]]),
                               ALU.add).then_inc(sm["xb_ready"], 1)
            pool.wait_ge(sm["ld_spare"], 16 * 13)
            for w, ws in ((w_q, w_qs), (w_k, w_ks)):
                w, ws = (v.rearrange("p (n c) -> p n c", c=2) for v in (w, ws))
                pool.tensor_scalar(ws[:, :, 0], w[:, :, 1], -1.0, None, ALU.mult).then_inc(sm["sw_ready"], 1)
                pool.tensor_copy(ws[:, :, 1], w[:, :, 0]).then_inc(sm["sw_ready"], 1)

        @block.scalar
        def _(act):
            def ln_sqrt(n):
                act.wait_ge(sm["ln_var"], n + 1)
                act.activation(std[:, :], var[:, :], ACT.Sqrt).then_inc(sm["ln_std"], 1)

            def copy_xT(n):
                for c in range(2):
                    act.wait_ge(sm["xT_psum"], NT * n + 4 * c + 4)
                    act.activation(xnT[:, 512 * c:512 * c + 512], ps[:, c, :], ACT.Identity).then_inc(sm["xT_ready"], 1)

            ln_sqrt(0)
            copy_xT(0)
            act.wait_ge(sm["cols_ready"], 1)

            def operand(n, o, src, bias, scale, cs, done):
                act.activation(f32_of[n][:, cs], src, ACT.Identity, bias=bias, scale=scale).then_inc(sm[done], 1)
                act.activation(o[:, 0, cs], src, ACT.Identity, bias=bias, scale=scale).then_inc(sm[done], 1)

            for b in range(B):
                cs = slice(b * S, b * S + S)
                act.wait_ge(sm["q_psum"], b + 1)
                operand(0, parts_q, ps[:, 2 + b, :], cols[:, 4:5], Q_SCALE, cs, "f_ready")
                act.wait_ge(sm["k_psum"], b + 1)
                operand(1, parts_k, ps[:, 4 + b, :], cols[:, C_BK:C_BK + 1], 1.0, cs, "f_ready")
            k_psum = ps[:, 4:6, :].rearrange("p a b -> p (a b)")
            operand(3, parts_hi, k_psum, cols[:, 6:7], 1.0, slice(0, TOK), "hi_ready")
            act.wait_ge(sm["v_psum"], 1)
            act.activation(v_f32, ps[:, 0:2, :].rearrange("p a b -> p (a b)"), ACT.Identity).then_inc(sm["vf_ready"], 1)
            operand(2, parts_lo, k_psum, cols[:, 5:6], 1.0, slice(0, TOK), "lo_ready")

            def bias_evac(s, k):
                n, slot = CH * s + k, k // 4
                act.wait_ge(sm["bias_psum"], n + 1)
                if s >= 3:
                    act.wait_ge(sm["x_psum"], last_v[s - 3] + 1)
                col = slot * Q + BB * (k % 4)
                act.activation(band[:, s % 3, :, col:col + BB],
                               ps[:, 4, :].rearrange("p (i h) -> p h i", i=BB), ACT.Identity).then_inc(sm["bias_ready"], 1)

            last_v = {u[2][0]: k for k, u in enumerate(units) if u[1] == "v"}

            def copy_units(n):
                for k, kind, a, sem, val in units_of(n):
                    if kind == "m":
                        act.wait_ge(sm["x_psum"], k + 1)
                        if a[0] >= 1:
                            act.wait_ge(sm["m_rows"], 32 * a[0])
                        act.activation(neg_mT[:, :], ps[0:H, XB[k % 2], 0:B * P], ACT.Identity).then_inc(sm[sem], 1)
                    if kind == "v" and V_ACT:
                        act.wait_ge(sm["x_psum"], k + 1)
                        s, u = a
                        if s >= 1:
                            act.wait_ge(sm["crel_added"], s)
                        for q in V_ACT:
                            i0 = 16 * q + 8 * u
                            act.activation(crel[:, i0:i0 + 8, :].rearrange("d i h -> d (i h)"), ps[32 * q:32 * q + HD, XB[k % 2], 0:256],
                                           ACT.Identity).then_inc(sm[sem], 1)

            act.wait_ge(sm["hi_split"], 1)
            for k in range(CH):
                bias_evac(0, k)
            copy_units(-1)
            act.wait_ge(sm["scr_hi"], 16)
            act.wait_ge(sm["scr_lo"], 16)
            for n in range(STEPS * CH + 2 * CH):
                s, c = divmod(n, CH)
                g, b = divmod(c, 2)
                if s < STEPS:
                    act.wait_ge(sm["st_psum"], 2 * n + 2)
                    if n >= 2:
                        act.wait_ge(sm["pv_done"], n - 1)
                    act.activation(p_out[:, n % 2, :, :].rearrange("p (a e) c -> p e a c", e=2),
                                   ps[:, (2 * n + 1) % 3, :].rearrange("p (e a c) -> p e a c", e=2, a=2), ACT.Exp
                                   ).then_inc(sm["oexp_done"], 1)
                if s + 1 < STEPS:
                    bias_evac(s + 1, c)
                if s < STEPS:
                    act.wait_ge(sm["z_ready"], n + 1)
                    z = band[:, s % 3, :, :].rearrange("p (e k b) c -> p e k b c", e=2, b=B)[:, :, 2 * g:2 * g + 2, b, :]
                    act.activation(z, z, ACT.Exp).then_inc(sm["zexp_done"], 1)
                copy_units(n)

            def copy_ctxn(k):
                for tt in range(NT):
                    act.wait_ge(sm["cn_psum"], NT * k + tt + 1)
                    act.activation(xnT[:, tt * P:tt * P + P], ps[:, 2 + tt % 2, 0:P], ACT.Identity).then_inc(sm["cn_ready"], 1)

            copy_ctxn(0)
            ln_sqrt(1)
            act.wait_ge(sm["memT_psum"], 1)
            act.activation(memT, ps[:, 0, 0:B * CTX], ACT.Identity).then_inc(sm["memT_ready"], 1)
            ln_sqrt(2)
            copy_xT(1)
            def latent(kind, b):
                act.wait_ge(sm["latk_psum" if kind == 0 else "latv_psum"], b + 1)
                act.activation(latT[kind][:, b * S:b * S + S], ps[0:DC, (4, 1)[b], :], ACT.Identity
                               ).then_inc(sm["latk_ready" if kind == 0 else "latv_ready"], 1)

            def first_part(n, b):
                act.wait_ge(sm["rot_done"], 2 * b + n + 1)
                for slot in (0, 3, 4) if n == 0 else (0, 1, 2):
                    act.activation(parts2[n][:, slot, b * S:b * S + S], f32_of[n][:, b * S:b * S + S], ACT.Identity
                                   ).then_inc(sm["part_ready"], 1)

            latent(0, 0)
            first_part(0, 0)
            latent(0, 1)
            first_part(1, 0)
            first_part(0, 1)
            latent(1, 0)
            latent(1, 1)
            first_part(1, 1)
            act.wait_ge(sm["v2_psum"], 1)
            act.activation(v_sb[:, 0, :, :].rearrange("p t (h w) -> p (t h) w", w=VW)[:, :, 0:HD],
                           ps[:, 5:7, :].rearrange("p a (n d) -> p (a n) d", d=HD), ACT.Identity).then_inc(sm["v2_ready"], 1)
            for j in range(-16, 128):
                if j % 16 == 2 and j // 16 + 1 < 8:
                    m = j // 16 + 1
                    act.wait_ge(sm["nT_psum"], m + 1)
                    if m >= 2:
                        act.wait_ge(sm["n_rows" if m % 2 == 0 else "n_rows_odd"], 32 * (m // 2))
                    act.activation(nm_T[:, m % 2, :], ps[0:4, 7, :], ACT.Identity).then_inc(sm["nT_ready"], 1)
                if j >= 0:
                    k = j // 4
                    act.wait_ge(sm["g_psum"], j + 1)
                    if k >= 3:
                        act.wait_ge(sm["g_pv"], k - 2)
                    act.activation(p_ring[:, k % 3, j % 4, :], ps[:, 4 + j % 2, :], ACT.Exp).then_inc(sm["g_exp"], 1)
            copy_ctxn(1)

            def sum_squares(k, src):
                for tt in range(NT):
                    if k == 0:
                        act.wait_ge(sm["x_added"], NT + tt + 1)
                    else:
                        act.wait_ge(sm["y3_done"], tt + 1)
                    act.activation(squares[:, tt, :], src[:, tt, :], ACT.Square, accum_out=mv[:, tt, k:k + 1]).then_inc(sm["sq_done"], 1)
                act.wait_ge(sm["rms_var"], k + 1)
                act.activation(std[:, :], var[:, :], ACT.Sqrt).then_inc(sm["rms_std"], 1)

            sum_squares(0, xn)
            copy_xT(2)
            act.wait_ge(sm["g_sub"], 1)
            act.activation(gsc[:, 128:144], gsc[:, 112:128], ACT.Exp).then_inc(sm["g_soft"], 1)
            act.wait_ge(sm["e_sub"], 1)
            act.activation(gsc[:, 256:288], gsc[:, 224:256], ACT.Exp).then_inc(sm["e_soft"], 1)
            for n in range(8):
                act.wait_ge(sm["a_psum"], n + 1)
                if n >= 4:
                    act.wait_ge(sm["hid_ready"], n - 3)
                act.activation(silu[:, n % 4, :], ps[:, 2 * (n % 3), :], ACT.Silu).then_inc(sm["silu_done"], 1)
            sum_squares(1, xn)

        @block.vector
        def _(dve):
            chain = [0]

            def link(ins):
                chain[0] += 1
                ins.then_inc(sm["dve"], 1)
                dve.wait_ge(sm["dve"], chain[0])

            def layernorm(n, src, dst):
                for tt in range(NT):
                    i = dve.bn_stats(stats[:, tt, :], src[:, tt, :])
                link(i)
                for tt in range(NT):
                    i = dve.bn_aggr(mv[:, tt, :], stats[:, tt, :])
                link(i)
                dve.tensor_scalar(var[:, :], mv[:, :, 1], LN_EPS, None, ALU.add).then_inc(sm["ln_var"], 1)
                dve.wait_ge(sm["ln_std"], n + 1)
                link(dve.reciprocal(rstd[:, :], std[:, :]))
                for tt in range(NT):
                    dve.tensor_scalar(dst[:, tt, :], src[:, tt, :], mv[:, tt, 0:1], rstd[:, tt:tt + 1],
                                      ALU.subtract, ALU.mult).then_inc(sm["ln_out"], 1)

            def split(f, o, order, rest, done):
                one, two, three = order
                link(dve.tensor_copy(o[:, one[0], :], f))
                link(dve.tensor_tensor(rest, f, o[:, one[0], :], ALU.subtract))
                link(dve.tensor_copy(o[:, two[0], :], rest))
                link(dve.tensor_tensor(o[:, three[0], :], rest, o[:, two[0], :], ALU.subtract))
                link(dve.tensor_copy(o[:, two[1], :], o[:, two[0], :]))
                link(dve.tensor_copy(o[:, one[1], :], o[:, one[0], :]))
                dve.tensor_copy(o[:, one[2], :], o[:, one[0], :]).then_inc(sm[done], 1)

            slot_of = lambda ps_: [[s for s in range(SLOTS) if ps_[s] == k] for k in range(3)]
            dve.wait_ge(sm["ld_x"], 16)
            layernorm(0, x, xn)
            def split_rest(f, o, order, rest, done):
                one, two, three = order
                link(dve.tensor_tensor(rest, f, o[:, one[0], :], ALU.subtract))
                link(dve.tensor_copy(o[:, two[0], :], rest))
                dve.tensor_tensor(o[:, three[0], :], rest, o[:, two[0], :], ALU.subtract)
                dve.tensor_copy(o[:, two[1], :], o[:, two[0], :])
                dve.tensor_copy(o[:, one[2], :], o[:, one[0], :])
                link(dve.tensor_copy(o[:, one[1], :], o[:, one[0], :]))
                dve.sem_inc(sm[done], 1)

            for b in range(B):
                cs = slice(b * S, b * S + S)
                for n, (o, parts_of, done) in enumerate(((parts_q, Q_PARTS, "q_split"), (parts_k, K_PARTS, "k_split"))):
                    dve.wait_ge(sm["f_ready"], 4 * b + 2 * n + 2)
                    split_rest(f32_of[n][:, cs], o[:, :, cs], slot_of(parts_of), rest_dve[:, 0:S], done)
            def take_unit(k, kind, a, sem, val):
                bank = XB[k % 2]
                if kind == "s":
                    tt, p, e = a
                    dve.wait_ge(sm["x_psum"], k + 1)
                    dve.tensor_reduce(m_qk[:, tt, 8 * e + p:8 * e + p + 1], ps[:, bank, :], AX_X, ALU.max).then_inc(sm[sem], 1)
                if kind == "r":
                    tt, r, e = a
                    nh = min(3, H // 2 - 3 * r)
                    dve.wait_ge(sm["x_psum"], k + 1)
                    dve.tensor_reduce(m_rel[:, tt, 8 * e + 3 * r:8 * e + 3 * r + nh],
                                      ps[:, bank, 0:nh * (2 * R + 1)].rearrange("p (h c) -> p h c", h=nh),
                                      AX_X, ALU.max).then_inc(sm[sem], 1)
                if kind == "m":
                    it = a[0]
                    dve.wait_ge(sm["r_done"], 12 * (it + 1))
                    dve.wait_ge(sm["m_done"], 32 * (it + 1))
                    dve.scalar_tensor_tensor(neg_m[:, it:NT:IT, :], m_qk[:, it:NT:IT, :], -1.0, m_rel[:, it:NT:IT, :],
                                             ALU.mult, ALU.subtract).then_inc(sm["negm_ready"], 1)
                if kind == "v" and V_DVE:
                    dve.wait_ge(sm["x_psum"], k + 1)
                    s, u = a
                    if s >= 1:
                        dve.wait_ge(sm["crel_added"], s)
                    for q in V_DVE:
                        i0 = 16 * q + 8 * u
                        dve.tensor_copy(crel[:, i0:i0 + 8, :].rearrange("d i h -> d (i h)"), ps[32 * q:32 * q + HD, bank, 0:256]
                                        ).then_inc(sm[sem], 1)

            def ctx_evac(s):
                dve.wait_ge(sm["crel_added"], s + 1)
                if s == 0:
                    dve.wait_ge(sm["lo_split"], 1)
                dve.tensor_copy(ctxT[:, :, Q * s:Q * s + Q], ps[:, 5 + s % 2, :].rearrange("p (c i) -> p c i", i=Q)
                                ).then_inc(sm["ctx_ready"], 1)

            for u in units_of(-1):
                if u[0] == HI_AT:
                    dve.wait_ge(sm["hi_ready"], 2)
                    split_rest(f32_of[3], parts_hi, slot_of(K_PARTS), rest_dve, "hi_split")
                    dve.wait_ge(sm["lo_ready"], 2)
                    dve.memset(ps[:, 5:7, :], 0.0).then_inc(sm["pv_zero"], 1)
                take_unit(*u)
            for n in range(STEPS * CH + 2 * CH):
                s, c = divmod(n, CH)
                g, b = divmod(c, 2)
                if c == 1 and s >= 2:
                    ctx_evac(s - 2)
                us = units_of(n)
                if s < STEPS:
                    dve.wait_ge(sm["st_psum"], 2 * n + 1)
                    if c in (0, 4):
                        dve.wait_ge(sm["bias_ready"], CH * (s + 1))
                    z = band[:, s % 3, :, :].rearrange("p (e k b) c -> p e k b c", e=2, b=B)[:, :, 2 * g:2 * g + 2, b, :]
                    dve.tensor_tensor(z, ps[:, 2 * n % 3, :].rearrange("p (e a c) -> p e a c", e=2, a=2), z, ALU.add
                                      ).then_inc(sm["z_ready"], 1)
                for u in us:
                    take_unit(*u)

            def attn_finish(k, dst, resid):
                for tt in range(NT + 3):
                    if tt < NT:
                        dve.wait_ge(sm["ctx_tr"], NT * k + tt + 1)
                        src = ps[:, tt % 2, :].rearrange("p (h r) -> p h r", r=32)
                        link(dve.reciprocal(rsum[:, tt % 2, :], src[:, :, HD]))
                        rs = rsum[:, tt % 2, :]
                        dve.tensor_tensor(dst[:, tt, :].rearrange("p (h d) -> p h d", d=HD), src[:, :, 0:HD],
                                          bass.AP(rs.tensor, rs.offset, [[2 * H, P], [1, H], [0, HD]]), ALU.mult
                                          ).then_inc(sm["ctx_norm"], 1)
                    if tt == 0 and k == 0:
                        dve.wait_ge(sm["xb_ready"], 1)
                    if tt >= 3:
                        dve.wait_ge(sm["y_psum"], NT * k + tt - 2)
                        dve.tensor_tensor(resid[:, tt - 3, :], ps[:, 4 + (tt - 3) % 2, 0:P], resid[:, tt - 3, :], ALU.add
                                          ).then_inc(sm["x_added"], 1)

            attn_finish(0, xn, x)
            dve.wait_ge(sm["x_added"], NT)
            layernorm(1, x, xn)
            dve.wait_ge(sm["comp_psum"], 1)
            dve.tensor_tensor(comp, ps[0:B * CONV, 1, 0:D], rows[0:B * CONV, R_CONV, :], ALU.add).then_inc(sm["comp_ready"], 1)
            dve.wait_ge(sm["shift_in"], 16 * 7)
            link(dve.tensor_tensor(x[:, :, :], x[:, :, :], shifted, ALU.add))
            layernorm(2, x, xn)

            def rotate(n, b):
                bank, scale = ((2, 7), (5, 2))[n][b], (Q_SCALE, 1.0)[n]
                swapped = ((3, 0), (6, 3))[n][b]
                f, r = f32_of[n][:, b * S:b * S + S], rest2[:, 512 * n:512 * n + 512]
                dve.wait_ge(sm["rope_psum"], 2 * b + n + 1)
                dve.scalar_tensor_tensor(f, ps[:, bank, :], scale, cos, ALU.mult, ALU.mult)
                link(dve.scalar_tensor_tensor(r, ps[:, swapped, :], scale, sin, ALU.mult, ALU.mult))
                dve.tensor_tensor(f, f, r, ALU.add).then_inc(sm["rot_done"], 1)

            def other_parts(n, b):
                cs = slice(b * S, b * S + S)
                f, r, o = f32_of[n][:, cs], rest2[:, 512 * n:512 * n + 512], parts2[n][:, :, cs]
                two, three = ((1, 5), 2) if n == 0 else ((3, 4), 5)
                if n == 1:
                    two = (3, 5)
                    three = 4
                dve.wait_ge(sm["rot_done"], 2 * b + n + 1)
                dve.wait_ge(sm["part_ready"], 3 * (2 * b + n) + 3)
                link(dve.tensor_tensor(r, f, o[:, 0, :], ALU.subtract))
                link(dve.tensor_copy(o[:, two[0], :], r))
                dve.tensor_copy(o[:, two[1], :], o[:, two[0], :])
                link(dve.tensor_tensor(o[:, three, :], r, o[:, two[0], :], ALU.subtract))
                dve.sem_inc(sm["q_split" if n == 0 else "k_split"], 1)

            rotate(0, 0)
            rotate(1, 0)
            other_parts(0, 0)
            rotate(0, 1)
            other_parts(1, 0)
            rotate(1, 1)
            other_parts(0, 1)
            other_parts(1, 1)

            for j in range(-32, 128 + 8):
                if j % 2 == 0 and (j + 32) // 2 < 64:
                    su = (j + 32) // 2
                    m, k = divmod(su, 8)
                    b, g = divmod(m, 4)
                    a, it = divmod(k, 4)
                    dve.wait_ge(sm["t_psum"], su + 1)
                    c = 4 * g + a
                    dve.tensor_reduce(m_qk[:, IT * b + it, c:c + 3:2], ps[:, 2 * (su % 2):2 * (su % 2) + 2, :], AX_X, ALU.max
                                      ).then_inc(sm["t_done"], 1)
                if j % 16 == 15 and j // 16 + 2 < 8:
                    m = j // 16 + 2
                    b, g = divmod(m, 4)
                    dve.wait_ge(sm["t_done"], 8 * m + 8)
                    dve.tensor_scalar(neg_m[:, IT * b:IT * b + IT, 4 * g:4 * g + 4], m_qk[:, IT * b:IT * b + IT, 4 * g:4 * g + 4],
                                      -1.0, None, ALU.mult).then_inc(sm["n_ready"], 1)
                if j >= 19 and (j - 19) % 16 == 0:
                    n = (j - 19) // 16
                    b, g = divmod(n, 4)
                    dve.wait_ge(sm["g_pv"], 4 * n + 4)
                    dve.tensor_copy(ctxT[:, 2 * g + b, :], ps[:, 6, :]).then_inc(sm["g_ctx"], 1)

            attn_finish(1, ctxn, xn)

            def rms(k, src, gain, out):
                dve.wait_ge(sm["sq_done"], NT * (k + 1))
                dve.tensor_scalar(var[:, :], mv[:, :, k], 1.0 / D, RMS_EPS, ALU.mult, ALU.add).then_inc(sm["rms_var"], 1)
                dve.wait_ge(sm["rms_std"], k + 1)
                link(dve.reciprocal(rstd[:, :], std[:, :]))
                for tt in range(NT):
                    i = dve.scalar_tensor_tensor(out[:, tt, :], src[:, tt, :], rstd[:, tt:tt + 1], rows[:, gain, :], ALU.mult, ALU.mult)
                    if k == 0:
                        i.then_inc(sm["ln_out"], 1)
                    else:
                        link(i)
                        dve.tensor_tensor(x[:, tt, :], x[:, tt, :], out[:, tt, :], ALU.add).then_inc(sm["out_ready"], 1)

            rms(0, xn, R_N1, xn)

            def cut(a, n, w=1):
                v = gsc[:, a:a + NT * n * w]
                return v.rearrange("p (t n) -> p t n", n=n) if w == 1 else v.rearrange("p (t n w) -> p t n w", n=n, w=w)

            def spread(v, n):
                return bass.AP(v.tensor, v.offset, [v.ap[0], v.ap[1], [0, n]])

            logit, gmax = cut(0, 10), gsc[:, 80:88]
            dve.wait_ge(sm["gate_psum"], 1)
            link(dve.tensor_tensor(logit, ps[:, 7, 0:80].rearrange("p (t n) -> p t n", n=10),
                                   bass.AP(b_gate.tensor, b_gate.offset, [b_gate.ap[0], [0, NT], [1, 10]]), ALU.add))
            link(dve.tensor_reduce(gmax, logit[:, :, 0:NG], AX_X, ALU.max))
            dve.tensor_tensor(cut(112, 2), logit[:, :, 0:NG], spread(gmax, 2), ALU.subtract).then_inc(sm["g_sub"], 1)
            gexp, gsum, grec, gprob = cut(128, 2), gsc[:, 88:96], gsc[:, 96:104], cut(144, 2)
            dve.wait_ge(sm["g_soft"], 1)
            link(dve.tensor_reduce(gsum, gexp, AX_X, ALU.add))
            link(dve.reciprocal(grec, gsum))
            link(dve.tensor_tensor(gprob, gexp, spread(grec, 2), ALU.mult))
            gtop, second, first = gsc[:, 104:112], gsc[:, 160:168], gsc[:, 168:176]
            dve.tensor_reduce(gtop, gprob, AX_X, ALU.max)
            link(dve.tensor_tensor(second, gprob[:, :, 1], gprob[:, :, 0], ALU.is_gt))
            link(dve.tensor_scalar(first, second, -1.0, 1.0, ALU.mult, ALU.add))
            sel, sel2 = cut(192, 4), cut(288, 4)
            dve.tensor_tensor(sel, logit[:, :, 2:6], spread(first, 4), ALU.mult)
            link(dve.tensor_tensor(sel2, logit[:, :, 6:10], spread(second, 4), ALU.mult))
            link(dve.tensor_tensor(sel, sel, sel2, ALU.add))
            emax, esum, erec = gsc[:, 176:184], gsc[:, 184:192], gsc[:, 320:328]
            link(dve.tensor_reduce(emax, sel, AX_X, ALU.max))
            dve.tensor_tensor(cut(224, 4), sel, spread(emax, 4), ALU.subtract).then_inc(sm["e_sub"], 1)
            prob = cut(256, 4)
            dve.wait_ge(sm["e_soft"], 1)
            link(dve.tensor_reduce(esum, prob, AX_X, ALU.add))
            link(dve.reciprocal(erec, esum))
            link(dve.tensor_tensor(prob, prob, spread(erec, 4), ALU.mult))
            link(dve.tensor_tensor(prob, prob, spread(gtop, 4), ALU.mult))
            other = bass.AP(prob.tensor, prob.offset, [prob.ap[0], [4, NT], [0, 4], [1, 4]])
            own = bass.AP(prob.tensor, prob.offset, [prob.ap[0], [4, NT], [1, 4], [0, 4]])
            above, tied, ahead, keep = cut(384, 4, 4), cut(512, 4, 4), cut(640, 4), cut(672, 4)
            dve.tensor_tensor(above, other, own, ALU.is_gt)
            link(dve.tensor_tensor(tied, other, own, ALU.is_equal))
            link(dve.tensor_tensor(tied, tied, bass.AP(tri.tensor, tri.offset, [tri.ap[0], [0, NT], [4, 4], [1, 4]]), ALU.mult))
            link(dve.tensor_tensor(above, above, tied, ALU.add))
            link(dve.tensor_reduce(ahead, above, AX_X, ALU.add))
            link(dve.scalar_tensor_tensor(keep, ahead, 1.5, prob, ALU.is_lt, ALU.mult))
            gate = cut(768, 8)
            dve.tensor_tensor(gate[:, :, 0:4], keep, spread(first, 4), ALU.mult)
            link(dve.tensor_tensor(gate[:, :, 4:8], keep, spread(second, 4), ALU.mult))

            for n in range(8):
                w, k, c = n // 4, (n // 2) % 2, n % 2
                dve.wait_ge(sm["silu_done"], n + 1)
                dve.tensor_tensor(hid[w][:, k, c * 512:c * 512 + 512], ps[:, 2 * (n % 3) + 1, :], silu[:, n % 4, :], ALU.mult
                                  ).then_inc(sm["hid_ready"], 1)
            for tt in range(NT):
                dve.wait_ge(sm["y3_psum"], tt + 1)
                b0 = 3 * (tt % 2)
                link(dve.tensor_tensor(xn[:, tt, :], ps[:, b0 + 2, 0:D], xn[:, tt, :], ALU.add))
                for e in range(NE):
                    i = dve.scalar_tensor_tensor(xn[:, tt, :], ps[:, b0 + e // 4, (e % 4) * D:(e % 4) * D + D], gate[:, tt, e:e + 1],
                                                 xn[:, tt, :], ALU.mult, ALU.add)
                    if e < NE - 1:
                        link(i)
                    else:
                        i.then_inc(sm["y3_done"], 1)
            rms(1, xn, R_N2, shifted)

        @block.tensor
        def _(pe):
            def transpose_x(n):
                for tt in range(NT):
                    pe.wait_ge(sm["ln_out"], NT * n + tt + 1)
                    pe.transpose(ps[:, tt // 4, (tt % 4) * P:(tt % 4) * P + P], xn[:, tt, :], ident[:, :]).then_inc(sm["xT_psum"], 1)

            pe.wait_ge(sm["ld_w"], 80)
            transpose_x(0)
            pe.wait_ge(sm["xT_ready"], 2)
            for c in range(2):
                for n, done in ((0, "q_psum"), (1, "k_psum")):
                    pe.matmul(ps[:, 2 + 2 * n + c, :], w_qkv[:, n * D:n * D + D], xnT[:, 512 * c:512 * c + 512],
                              start=True, stop=True).then_inc(sm[done], 1)
            for tt in range(NT):
                i = pe.matmul(ps[:, tt // 4, (tt % 4) * P:(tt % 4) * P + P], xnT[:, tt * P:tt * P + P], w_qkv[:, 2 * D:3 * D],
                              start=True, stop=True)
            i.then_inc(sm["v_psum"], 1)

            def fill_unit(k, kind, a, sem, val):
                bank = XB[k % 2]
                if k >= 2:
                    pe.wait_ge(sm[units[k - 2][3]], units[k - 2][4])
                if kind == "s":
                    tt, p, e = a
                    b = tt // IT
                    i = pe.matmul(ps[:, bank, :], q_op[0:PR, e, p, tt * P:tt * P + P], k_op[0:PR, 0, p, b * S:b * S + S], start=True, stop=True)
                if kind == "r":
                    tt, r, e = a
                    for j, p in enumerate(range(3 * r, min(3 * r + 3, H // 2))):
                        i = pe.matmul(ps[:, bank, j * (2 * R + 1):(j + 1) * (2 * R + 1)],
                                      q_op[0:PR, e, p, tt * P:tt * P + P], rel_k[0:PR, ZERO - R:ZERO + R + 1], start=True, stop=True)
                if kind == "m":
                    pe.wait_ge(sm["negm_ready"], a[0] + 1)
                    for b in range(B):
                        i = pe.transpose(ps[0:H, bank, b * P:b * P + P], neg_m[:, IT * b + a[0], :], ident[:, :])
                if kind == "v":
                    s, u = a
                    if u == 0:
                        pe.wait_ge(sm["zexp_done"], CH * (s + 1))
                    for ii in range(8):
                        for slot in range(2):
                            jt = slots_of(s)[slot][0]
                            for q in range(4):
                                qi = 16 * q + 8 * u + ii
                                w = P * jt - (Q * s + qi) + ZERO
                                i = pe.matmul(ps[32 * q:32 * q + HD, bank, B * H * ii:B * H * (ii + 1)], rel_v[:, w * HD:(w + 1) * HD],
                                              band[:, s % 3, :, slot * Q + qi], start=(slot == 0), stop=(slot == 1), skip_group_check=True)
                i.then_inc(sm["x_psum"], 1)

            def bias_block(s, k):
                n, jt = CH * s + k, slots_of(s)[k // 4][0]
                if n >= 1:
                    pe.wait_ge(sm["bias_ready"], n)
                for ii in range(BB):
                    i = Q * s + BB * (k % 4) + ii
                    w = P * jt - i + ZERO
                    mm = pe.matmul(ps[:, 4, B * H * ii:B * H * (ii + 1)], rel_k[0:PR, w:w + P], q_flat[0:PR, :, i], start=True, stop=True)
                mm.then_inc(sm["bias_psum"], 1)

            def scores(m):
                n, other = divmod(m, 2)
                s, c = divmod(n, CH)
                g, b = divmod(c, 2)
                if m >= 3:
                    if other:
                        pe.wait_ge(sm["z_ready"], n)
                    else:
                        pe.wait_ge(sm["oexp_done"], n - 1)
                for k, (jt, v) in enumerate(slots_of(s)[2 * other:2 * other + 2]):
                    for e in range(2):
                        for a in range(2):
                            col = 2 * P * e + P * a + Q * k
                            i = pe.matmul(ps[:, m % 3, col:col + Q],
                                          k_op[0:PR + 1, v, 2 * g + a, b * S + jt * P:b * S + jt * P + P],
                                          q_op[0:PR + 1, e, 2 * g + a, b * S + Q * s:b * S + Q * s + Q],
                                          start=True, stop=True)
                i.then_inc(sm["st_psum"], 1)

            def products(n):
                s, c = divmod(n, CH)
                g, b = divmod(c, 2)
                pe.wait_ge(sm["oexp_done"], n + 1)
                pe.wait_ge(sm["zexp_done"], n + 1)
                if c == 0 and s >= 2:
                    pe.wait_ge(sm["ctx_ready"], s - 1)
                for slot, (jt, v) in enumerate(slots_of(s)):
                    for hh in range(4):
                        h = 4 * g + hh
                        if slot < 2:
                            rhs = band[:, s % 3, row_of(h, b), slot * Q:slot * Q + Q]
                        else:
                            rhs = p_out[:, n % 2, hh, (slot - 2) * Q:(slot - 1) * Q]
                        i = pe.matmul(ps[32 * hh:32 * hh + VW, 5 + s % 2, Q * c:Q * c + Q],
                                      v_sb[:, v, IT * b + jt, h * VW:h * VW + VW], rhs,
                                      start=(c == 0 and slot == 0), stop=False, skip_group_check=True)
                i.then_inc(sm["pv_done"], 1)

            def add_crel(s):
                pe.wait_ge(sm["crel_ready"], 8 * (s + 1))
                for c in range(CH):
                    g, b = divmod(c, 2)
                    for hh in range(4):
                        i = pe.matmul(ps[32 * hh:32 * hh + HD, 5 + s % 2, Q * c:Q * c + Q], ident[0:HD, 0:HD],
                                      crel[:, :, row_of(4 * g + hh, b)], start=False, stop=True, skip_group_check=True)
                i.then_inc(sm["crel_added"], 1)


            pe.wait_ge(sm["f_ready"], 8)
            pe.wait_ge(sm["ld_one"], 64)
            first = units_of(-1)
            for k, u in enumerate(first):
                if k == 0 or (u[1] == "s" and u[2][0] == IT and first[k - 1][2][0] == 0):
                    b = 1 if k else 0
                    pe.wait_ge(sm["op_q"], 32 * (b + 1))
                    pe.wait_ge(sm["op_k"], 32 * (b + 1))
                if u[1] == "r":
                    pe.wait_ge(sm["rel_ready"], 32)
                if k >= FIRST_BIAS and (k - FIRST_BIAS) % 2 == 0 and (k - FIRST_BIAS) // 2 < CH:
                    if k == FIRST_BIAS:
                        pe.wait_ge(sm["hi_ready"], 2)
                        pe.wait_ge(sm["lo_ready"], 2)
                    bias_block(0, (k - FIRST_BIAS) // 2)
                fill_unit(*u)

            for name, val in (("pv_zero", 1), ("m_rows", 32), ("ld_one", 64), ("v_ready", 3), ("op_hi", 32)):
                pe.wait_ge(sm[name], val)
            scores(0)
            scores(1)
            for n in range(STEPS * CH + 2 * CH):
                s, c = divmod(n, CH)
                us = units_of(n)
                nxt = n + 1 if n + 1 < STEPS * CH else None
                if nxt and nxt % (2 * CH) == 0:
                    pe.wait_ge(sm["m_rows"], 32 * (nxt // (2 * CH) + 1))
                if nxt == 3 * CH:
                    pe.wait_ge(sm["op_lo"], 32)
                if nxt == 1:
                    pe.wait_ge(sm["relv_ready"], 16)
                if nxt:
                    scores(2 * nxt)
                if us:
                    fill_unit(*us.pop(0))
                if s + 1 < STEPS:
                    bias_block(s + 1, c)
                if us:
                    fill_unit(*us.pop(0))
                if nxt:
                    scores(2 * nxt + 1)
                if c == 0 and s >= 2:
                    add_crel(s - 2)
                if us:
                    fill_unit(*us.pop(0))
                if 1 <= n <= STEPS * CH:
                    products(n - 1)
                for u in us:
                    fill_unit(*u)

            def attn_finish(k, src, w):
                for tt in range(NT + 2):
                    b, it = divmod(tt, IT)
                    if tt < NT:
                        if tt >= 2:
                            pe.wait_ge(sm["ctx_norm"], NT * k + tt - 1)
                        for g in range(4):
                            i = pe.transpose(ps[:, tt % 2, g * P:g * P + P], ctxT[:, 2 * g + b, it * P:it * P + P], ident[:, :])
                        i.then_inc(sm["ctx_tr"], 1)
                    if 1 <= tt <= NT:
                        u = tt - 1
                        pe.wait_ge(sm["ctx_norm"], NT * k + u + 1)
                        if u >= 2:
                            pe.wait_ge(sm["cn_ready"], NT * k + u - 1)
                        pe.transpose(ps[:, 2 + u % 2, 0:P], src[:, u, :], ident[:, :]).then_inc(sm["cn_psum"], 1)
                    if tt >= 2:
                        u = tt - 2
                        pe.wait_ge(sm["cn_ready"], NT * k + u + 1)
                        if u >= 2:
                            pe.wait_ge(sm["x_added"], NT * k + u - 1)
                        pe.matmul(ps[:, 4 + u % 2, 0:P], xnT[:, u * P:u * P + P], w, start=True, stop=True).then_inc(sm["y_psum"], 1)

            pe.wait_ge(sm["ctx_ready"], STEPS)
            attn_finish(0, xn, w_out[:, :])

            pe.wait_ge(sm["ln_out"], 2 * NT)
            for b in range(B):
                i = pe.transpose(ps[:, 0, CTX * b:CTX * b + CTX], xn[0:CTX, IT * b + 2, :], ident[0:CTX, 0:CTX])
            i.then_inc(sm["memT_psum"], 1)
            pe.wait_ge(sm["memT_ready"], 1)
            pe.wait_ge(sm["ld_wide"], 16 * 6)
            for r in range(RATE):
                i = pe.matmul(ps[0:B * CONV, 1, 0:D], memT[:, r:B * CTX:RATE], w_conv[:, r, :], start=(r == 0), stop=(r == RATE - 1))
            i.then_inc(sm["comp_psum"], 1)

            def transpose_again(k, n):
                for tt in range(NT):
                    pe.wait_ge(sm["ln_out"], NT * n + tt + 1)
                    pe.transpose(ps[:, tt // 4, (tt % 4) * P:(tt % 4) * P + P], xn[:, tt, :], ident[:, :]).then_inc(sm["xT_psum"], 1)
                pe.wait_ge(sm["xT_ready"], 2 * (k + 1))

            for tt in range(NT):
                pe.wait_ge(sm["ln_out"], NT * 2 + tt + 1)
                pe.transpose(ps[:, tt // 4, (tt % 4) * P:(tt % 4) * P + P], xn[:, tt, :], ident[:, :]).then_inc(sm["xT_psum"], 1)

            def project(bank, w, rhs, b, done=None):
                i = pe.matmul(ps[0:w.shape[1], bank, :], w, rhs[:, b * S:b * S + S], start=True, stop=True)
                if done:
                    i.then_inc(sm[done], 1)

            pe.wait_ge(sm["sw_ready"], 4)
            for b in range(B):
                pe.wait_ge(sm["xT_ready"], 3 + b)
                project((2, 7)[b], w_q, xnT, b)
                project((3, 0)[b], w_qs, xnT, b, "rope_psum")
                project((4, 1)[b], w_kc, xnT, b, "latk_psum")
                if b == 0:
                    pe.wait_ge(sm["latk_ready"], 1)
                    project(5, w_k, latT[0], 0)
                    project(6, w_ks, latT[0], 0, "rope_psum")
            pe.wait_ge(sm["latk_ready"], 2)
            pe.wait_ge(sm["rot_done"], 1)
            project(2, w_k, latT[0], 1)
            project(3, w_ks, latT[0], 1, "rope_psum")
            project(4, w_vc, xnT, 0, "latv_psum")
            project(1, w_vc, xnT, 1, "latv_psum")
            pe.wait_ge(sm["latv_ready"], 2)
            pe.wait_ge(sm["rot_done"], 2)
            for tt in range(NT):
                i = pe.matmul(ps[:, 5 + tt // 4, (tt % 4) * P:(tt % 4) * P + P], latT[1][:, tt * P:tt * P + P], w_v, start=True, stop=True)
            i.then_inc(sm["v2_psum"], 1)

            pe.wait_ge(sm["op_q"], 96)
            pe.wait_ge(sm["op_k"], 96)
            pe.wait_ge(sm["rot_done"], 4)
            pe.wait_ge(sm["v2_ready"], 1)
            for j in range(-32, 128 + 8):
                if 0 <= j < 128:
                    n, k = divmod(j, 16)
                    b, g = divmod(n, 4)
                    jt, hh = divmod(k, 4)
                    a, e = divmod(hh, 2)
                    if k == 0:
                        pe.wait_ge(sm["n_rows" if n % 2 == 0 else "n_rows_odd"], 32 * (n // 2 + 1))
                    if j >= 2:
                        pe.wait_ge(sm["g_exp"], j - 1)
                    pe.matmul(ps[:, 4 + j % 2, :], k_op[0:PR + 1, 0, 2 * g + a, b * S + jt * P:b * S + jt * P + P],
                              q_op[0:PR + 1, e, 2 * g + a, b * S:b * S + S], start=True, stop=True).then_inc(sm["g_psum"], 1)
                if j % 2 == 0 and (j + 32) // 2 < 64:
                    su = (j + 32) // 2
                    m, k = divmod(su, 8)
                    b, g = divmod(m, 4)
                    a, it = divmod(k, 4)
                    if su >= 2:
                        pe.wait_ge(sm["t_done"], su - 1)
                    if su == 32:
                        pe.wait_ge(sm["op_q"], 128)
                        pe.wait_ge(sm["op_k"], 128)
                    for e in range(2):
                        i = pe.matmul(ps[:, 2 * (su % 2) + e, :], q_op[0:PR, e, 2 * g + a, b * S + it * P:b * S + it * P + P],
                                      k_op[0:PR, 0, 2 * g + a, b * S:b * S + S], start=True, stop=True)
                    i.then_inc(sm["t_psum"], 1)
                if j % 16 == 1 and 0 <= j // 16 + 1 < 8:
                    m = j // 16 + 1
                    b, g = divmod(m, 4)
                    pe.wait_ge(sm["n_ready"], m + 1)
                    if m >= 1:
                        pe.wait_ge(sm["nT_ready"], m)
                    for it in range(IT):
                        i = pe.transpose(ps[0:4, 7, it * P:it * P + P], neg_m[:, IT * b + it, 4 * g:4 * g + 4], ident[:, :])
                    i.then_inc(sm["nT_psum"], 1)
                if j >= 6 and (j - 6) % 4 == 0 and (j - 6) // 4 < 32:
                    k = (j - 6) // 4
                    n, jt = divmod(k, 4)
                    b, g = divmod(n, 4)
                    pe.wait_ge(sm["g_exp"], 4 * k + 4)
                    if jt == 0 and n >= 1:
                        pe.wait_ge(sm["g_ctx"], n)
                    for hh in range(4):
                        h = 4 * g + hh
                        i = pe.matmul(ps[32 * hh:32 * hh + VW, 6, :], v_sb[:, 0, IT * b + jt, h * VW:h * VW + VW],
                                      p_ring[:, k % 3, hh, :], start=(jt == 0), stop=(jt == IT - 1))
                    i.then_inc(sm["g_pv"], 1)

            pe.wait_ge(sm["g_ctx"], 8)
            attn_finish(1, ctxn, w_o)

            pe.wait_ge(sm["x_added"], 2 * NT)
            transpose_again(2, 3)
            for tt in range(NT):
                i = pe.matmul(ps[:, 7, 10 * tt:10 * tt + 10], xnT[:, tt * P:tt * P + P], w_gate, start=True, stop=True)
            i.then_inc(sm["gate_psum"], 1)
            for n in range(8):
                w, k, c = n // 4, (n // 2) % 2, n % 2
                if n >= 3:
                    pe.wait_ge(sm["hid_ready"], n - 2)
                for z in range(2):
                    i = pe.matmul(ps[:, 2 * (n % 3) + z, :], w_in[w][:, HID * z + P * k:HID * z + P * k + P], xnT[:, c * 512:c * 512 + 512],
                                  start=True, stop=True)
                i.then_inc(sm["a_psum"], 1)
            pe.wait_ge(sm["hid_ready"], 8)
            for tt in range(NT):
                b0 = 3 * (tt % 2)
                if tt >= 2:
                    pe.wait_ge(sm["y3_done"], tt - 1)
                for c in range(2):
                    for k in range(2):
                        pe.matmul(ps[:, b0 + c, :], hid[1][:, k, tt * P:tt * P + P], w_2[:, k, c * 512:c * 512 + 512],
                                  start=(k == 0), stop=(k == 1))
                for k in range(2):
                    i = pe.matmul(ps[:, b0 + 2, 0:D], hid[0][:, k, tt * P:tt * P + P], w_so[:, k, :], start=(k == 0), stop=(k == 1))
                i.then_inc(sm["y3_psum"], 1)


def kernel(**inputs):
    import numpy as np
    import concourse.bacc as bacc
    from concourse.bass_utils import run_bass_kernel_spmd

    a = {k: np.ascontiguousarray(v) for k, v in inputs.items()}
    off = np.clip(np.arange(EXT) - ZERO, -R, R) + R
    relk, relv = a["L0_attn_rel_emb_k"], a["L0_attn_rel_emb_v"]
    bqkv = a["L0_attn_b_qkv"]
    import ml_dtypes
    freq = (np.float32(1.0) / np.float32(10000.0) ** (np.arange(0, HD, 2, dtype=np.float32) / np.float32(HD))).astype(np.float32)
    angle = np.tile(np.repeat(freq, 2), H)[:, None] * np.arange(S, dtype=np.float32)[None, :]
    arrays = {
        "x": a["x"],
        "w_qkv": a["L0_attn_W_qkv"],
        "w_out": a["L0_attn_W_out"],
        "ident": np.eye(P, dtype=np.float32),
        "zeros": np.zeros((1, 3 * (H // 2) * TOK), ml_dtypes.bfloat16),
        "ones": np.ones((1, 3 * (H // 2) * TOK), ml_dtypes.bfloat16),
        "cols": np.ascontiguousarray(np.stack([bqkv[:D], bqkv[D:2 * D], np.tile(relk[0], H), np.tile(relk[2 * R], H)], 1)),
        "rows": np.ascontiguousarray(np.stack([bqkv[2 * D:], np.tile(relv[0], H), np.tile(relv[2 * R], H), a["L0_attn_b_out"],
                          a["L0_xattn_conv_b"], a["L0_ffn_norm1_w"], a["L0_ffn_norm2_w"]])),
        "relk_ext": np.ascontiguousarray(relk[off].T),
        "relv_ext": relv[off],
        "ctx": a["ctx_1024"],
        "w_conv": a["L0_xattn_conv_w"],
        "w_q": a["L0_ffn_Wq"], "w_kc": a["L0_ffn_Wk_c"], "w_vc": a["L0_ffn_Wv_c"],
        "w_k": a["L0_ffn_Wk"], "w_v": a["L0_ffn_Wv"], "w_o": a["L0_ffn_Wo"],
        "w_sin": a["L0_ffn_W_shared_in"], "w_so": a["L0_ffn_W_shared_out"],
        "w_1": a["L0_ffn_W1_shared"], "w_2": a["L0_ffn_W2_experts"],
        "w_gg": a["L0_ffn_Wg_gate"], "w_ge": a["L0_ffn_We_gate"],
        "b_gg": a["L0_ffn_group_bias"], "b_ge": a["L0_ffn_expert_bias"],
        "cos": np.ascontiguousarray(np.cos(angle)), "sin": np.ascontiguousarray(np.sin(angle)),
        "tri": np.tril(np.ones((EPG, EPG), np.float32), -1).reshape(-1),
    }
    nc = bacc.Bacc("TRN2", target_bir_lowering=False, num_devices=1)
    t = {n: nc.dram_tensor("in_" + n, v.shape, mybir.dt.from_np(v.dtype), kind="ExternalInput").ap() for n, v in arrays.items()}
    t["scr"] = nc.dram_tensor("scr", (4, P, SLOTS, TOK), BF16, kind="Internal").ap()
    t["scr_rel"] = nc.dram_tensor("scr_rel", (HD, SLOTS, EXT), BF16, kind="Internal").ap()
    t["out"] = nc.dram_tensor("out", (B, S, D), F32, kind="ExternalOutput").ap()
    build(nc, t)
    r = run_bass_kernel_spmd(nc, [{"in_" + n: v for n, v in arrays.items()}], core_ids=[0])
    return r.results[0]["out"]
```

```python
from contextlib import ExitStack

import concourse.bass as bass
from concourse import mybir

F32 = mybir.dt.float32
BF16 = mybir.dt.bfloat16
ALU = mybir.AluOpType
ACT = mybir.ActivationFunctionType
AX_X = mybir.AxisListType.X

P = 128
B, S, D, H = 2, 512, 128, 16
HD = D // H
NT = B * S // P
IT = S // P
TOK = B * S
R = 64
SLOTS = 6
KR = HD * SLOTS
PR = 64 + KR
Q_PARTS = (0, 1, 2, 0, 0, 1)
K_PARTS = (0, 0, 0, 1, 2, 1)
EXT = 512
ZERO = 255
VW = HD + 1
DC, HID, NE, NG = 32, 256, 8, 2
EPG = NE // NG
LN_EPS, RMS_EPS = 1e-5, 1e-6
Q_SCALE = float(HD) ** -0.5
Q = 64
STEPS = S // Q
CH = 8
BB = 16
SHARED_BANKS = (3, 7)
Y_BANKS = ((4, 5, 6), (0, 1, 7))
LEAD = 28
SILU_FIRST = 1
HID_FIRST = 3
FIRST_BIAS = 10
M_FIRST, M_LEAD, M_END = 1, 3, 2
CTX, RATE = 32, 4
CONV = CTX // RATE
C_BQ, C_BK, C_LO, C_HI, C_BQ_SCALED, C_BK_LO, C_BK_HI = range(7)
R_BV, R_LO, R_HI, R_BOUT, R_CONV, R_N1, R_N2 = range(7)


def slots_of(s):
    it, half = divmod(s, 2)
    ja = min(max(it if half else it - 1, 0), IT - 2)
    rest = [j for j in range(IT) if j not in (ja, ja + 1)]
    return [(ja, 0), (ja + 1, 0)] + [(j, 1 if j < ja else 2) for j in rest]


def shared_bank_units():
    heads = [("s", (p, e)) for p in range(H // 2) for e in range(2)]
    heads += [("r", (r, e)) for r in range(3) for e in range(2)]
    plan = []
    for it in range(IT):
        first = M_FIRST if it == 1 else 2 * CH * (it - 1) - M_LEAD
        last = 2 * CH * it - 1 - M_END
        for b in range(B):
            for k, (kind, a) in enumerate(heads):
                n = -1 if it == 0 else first + (len(heads) * b + k) * (last - first) // (B * len(heads))
                plan.append((n, kind, (IT * b + it, *a)))
            plan.append((n if it == 0 else n + 1, "m", (it, b)))
    for s in range(STEPS):
        plan += [(CH * (s + 1) + 2 + 3 * u, "v", (s, u)) for u in range(2)]
    return sorted(plan, key=lambda x: (x[0], x[0] >= 0 and x[1] in "mv"))


def build(nc, t):
    with ExitStack() as ctx:
        def sb(name, shape, dt=F32):
            return ctx.enter_context(nc.sbuf_tensor(name, shape, dt))

        x = sb("x_sb", [P, NT, D])
        xn = sb("xn", [P, NT, D])
        xnT = sb("xnT", [P, TOK])
        q_op = sb("q_op", [P, 2, H // 2, TOK], BF16)
        k_op = sb("k_op", [P, 3, H // 2, TOK], BF16)
        band = sb("band", [P, 3, B * H, P])
        v_sb = sb("v_sb", [P, 3, NT, H * VW])
        rel_v = sb("rel_v", [P, 384 * HD])
        rel_k = sb("rel_k", [P, EXT], BF16)
        ctxT = sb("ctxT", [P, CH, S])
        p_out = sb("p_out", [P, 2, 4, P])
        crel = sb("crel", [HD, Q, B * H])
        ident = sb("ident", [P, P])
        rows = sb("rows", [P, 8, D])
        cols = sb("cols", [P, 8])
        w_qkv = sb("w_qkv", [P, 3 * D])
        w_out = sb("w_out", [P, D])
        stats = sb("stats", [P, NT, 6])
        mv = sb("mv", [P, NT, 2])
        var = sb("var", [P, NT])
        std = sb("std", [P, NT])
        rstd = sb("rstd", [P, NT])
        m_qk = sb("m_qk", [P, NT, H])
        m_rel = sb("m_rel", [P, NT, H])
        neg_m = sb("neg_m", [P, NT, H])
        rsum = sb("rsum", [P, 2, H])
        arena = band[:, :, :, :].rearrange("p a b c -> p (a b c)")
        f32_of = [arena[:, n * TOK:(n + 1) * TOK] for n in (0, 1, 8, 2)]
        rest_dve = arena[:, 3 * TOK:4 * TOK]
        scratchT = ctxT[:, :, :].rearrange("p a b -> p (a b)")
        v_f32 = arena[:, 7 * TOK:8 * TOK]
        rest_pool = scratchT[:, 3 * TOK:4 * TOK]
        parts_q, parts_k, parts_lo, parts_hi = (m.bitcast(BF16).rearrange("p (s t) -> p s t", s=SLOTS) for m in
                                      (arena[:, 4 * TOK:7 * TOK], rel_v[:, :], arena[:, 9 * TOK:12 * TOK], scratchT[:, 0:3 * TOK]))
        relk_f, relk_rest = (p_out[0:HD, n, :, :].rearrange("p a b -> p (a b)") for n in range(2))
        relk_parts = crel[:, :, :].rearrange("d i h -> d (i h)")[:, 0:3 * EXT].bitcast(BF16).rearrange("p (s t) -> p s t", s=SLOTS)
        neg_mT = sb("neg_mT", [H, B * P], BF16)
        spare = k_op[:, 1:3, :, :].rearrange("p v a t -> p (v a t)").bitcast(F32)
        wide = spare[:, 2048:5888]
        w_conv = wide[:, 0:512].rearrange("p (r o) -> p r o", r=RATE)
        w_in = [wide[:, 512 + 512 * n:1024 + 512 * n] for n in range(2)]
        w_so = wide[:, 1536:1792].rearrange("p (k o) -> p k o", k=2)
        w_2 = wide[:, 1792:3840].rearrange("p (k n) -> p k n", k=2)
        cos, sin = spare[:, 0:S], spare[:, S:2 * S]
        w_q, w_o = spare[:, 1024:1152], spare[:, 1152:1280]
        w_kc, w_vc = spare[:, 1280:1312], spare[:, 1312:1344]
        w_k, w_v = spare[0:DC, 1344:1472], spare[0:DC, 1472:1600]
        w_gate, b_gate = spare[:, 1600:1610], spare[:, 1610:1620]
        tri = spare[:, 1620:1636]
        w_qs, w_ks = spare[:, 1664:1792], spare[0:DC, 1792:1920]
        w_cT = spare[0:DC, 5888:6144].rearrange("r (n i) -> r n i", n=2)
        w_full = spare[:, 6144:6528].rearrange("i (n o) -> i n o", n=3)
        p_ring = arena[:, 0:8192].rearrange("p (r h t) -> p r h t", r=4, h=4)
        hid = [arena[:, 2048 * n:2048 + 2048 * n].rearrange("p (k t) -> p k t", k=2) for n in range(2)]
        silu = arena[:, 4096:6144].rearrange("p (r t) -> p r t", r=4)
        shifted = scratchT[:, 0:NT * D].rearrange("p (t d) -> p t d", d=D)
        memT, comp = scratchT[:, 1024:1088], scratchT[0:B * CONV, 1088:1216]
        parts2 = [arena[:, (6 + 3 * n) * TOK:(9 + 3 * n) * TOK].bitcast(BF16).rearrange("p (s t) -> p s t", s=SLOTS) for n in range(2)]
        rest2 = arena[:, 4 * TOK:5 * TOK]
        ctxn = arena[:, 10240:11264].rearrange("p (t d) -> p t d", d=D)
        squares = arena[:, 9216:10240].rearrange("p (t d) -> p t d", d=D)
        nm_T = crel[0:4, 0:16, :].rearrange("d i h -> d (i h)").bitcast(BF16).rearrange("d (r t) -> d r t", r=2)
        q_flat = q_op[:, :, :, :].rearrange("r e p (b t) -> r (e p b) t", b=B)
        odd_sum = arena[:, 11264:11520].rearrange("p (r d) -> p r d", r=2)
        ctxn0 = arena[:, 9216:10240].rearrange("p (t d) -> p t d", d=D)
        gsc = arena[:, 8192:9216]
        ps = ctx.enter_context(nc.psum_tensor("ps", [P, 8, 512], F32))

        units = shared_bank_units()

        def freed(k):
            kind = units[k][1]
            sem = {"s": "m_done", "r": "r_done", "m": "mT_ready", "v": "crel_ready"}[kind]
            return sm[sem], sum(u[1] == kind for u in units[:k + 1]) * (4 if kind == "v" else 1)

        names = """
            ld_x0 ld_x1 ld_w ld_rel ld_one ld_wide ld_spare
            ln_var ln_std ln_out bn_done aggr_done rstd_done xT_psum xT_ready
            q_psum k_psum v_psum cols_ready f_ready lo_ready hi_ready vf_ready v_ones v_ready
            q_split k_split lo_split hi_split rel_split scr_q scr_k scr_lo scr_hi scr_rel
            op_q op_k op_lo op_hi rel_zero rel_ready relv_ready
            unit_psum m_done r_done negm_ready mT_ready m_rows0 m_rows1
            pv_zero bias_psum bias_ready st_psum oexp_done z_ready zexp_done pv_done
            crel_ready crel_added ctx_ready
            ctx_tr rsum_done ctx_norm ctxnT_psum ctxnT_ready y_psum x_added xb_ready
            rope_scr_half0 rope_scr_half1 rope_op_half0 rope_op_half1
            shift_in conv_in memT_psum memT_ready comp_psum comp_ready
            swapped_ready rope_psum rot_done part_ready w_cT_psum w_cT_ready w_full_psum w_full_ready v2_psum v2_ready
            rmax_psum rmax_done rope_negm rope_negT_psum rope_negT rope_rows_even rope_rows_odd
            rope_st_psum rope_exp_done rope_pv_done rope_ctx_ready
            sq_done rms_var rms_std rms_done gate_psum group_sub group_exp expert_sub expert_exp
            mlp_psum silu_done hid_ready expert_psum ffn_added
            dve pool out_ready out_done""".split()
        sm = {n: ctx.enter_context(nc.semaphore(n)) for n in names}
        block = ctx.enter_context(nc.Block())

        def row_of(h, b):
            return H * (h % 2) + 2 * (h // 2) + b

        ld_x = ("ld_x0", "ld_x1")
        m_rows = ("m_rows0", "m_rows1")

        def units_of(n):
            return [(k, *u[1:]) for k, u in enumerate(units) if u[0] == n]

        def write_parts(eng, n, parts, done, val, scr, cols_=slice(0, TOK)):
            eng.wait_ge(sm[done], val)
            eng.dma_start(t["scr"][n][:, :, cols_], parts[:, :, cols_]).then_inc(sm[scr], 16)

        def read_rows(eng, n, dst, scr, val, op, c0=0, w=TOK):
            eng.wait_ge(sm[scr], val)
            for e in range(2):
                src = bass.AP(t["scr"].tensor, n * P * SLOTS * TOK + e * KR * TOK + c0,
                              [[TOK, KR], [2 * KR * TOK, H // 2], [1, w]])
                rows_of = dst[64 * e:64 * e + KR, e] if op == "op_q" else dst[64 * e:64 * e + KR]
                eng.dma_start(rows_of[:, :, c0:c0 + w], src).then_inc(sm[op], 16)

        def other_parts(eng, link, n, b):
            cs = slice(b * S, b * S + S)
            f, r, o = f32_of[n][:, cs], rest2[:, 512 * n:512 * n + 512], parts2[n][:, :, cs]
            two, three = ((1, 5), 2) if n == 0 else ((3, 5), 4)
            eng.wait_ge(sm["rot_done"], 2 * b + n + 1)
            eng.wait_ge(sm["part_ready"], 3 * (2 * b + n) + 3)
            link(eng.tensor_tensor(r, f, o[:, 0, :], ALU.subtract))
            link(eng.tensor_copy(o[:, two[0], :], r))
            link(eng.tensor_copy(o[:, two[1], :], o[:, two[0], :]))
            link(eng.tensor_tensor(o[:, three, :], r, o[:, two[0], :], ALU.subtract))
            eng.sem_inc(sm["q_split" if n == 0 else "k_split"], 1)

        @block.sync
        def _(sp):
            for b in range(B):
                sp.dma_start(x[:, IT * b:IT * b + IT, :], t["x"][b].rearrange("(t p) d -> p t d", p=P)).then_inc(sm[ld_x[b]], 16)
            sp.dma_start(ident[:, :], t["ident"]).then_inc(sm["ld_w"], 16)
            sp.dma_start(w_qkv[:, :], t["w_qkv"]).then_inc(sm["ld_w"], 16)
            sp.dma_start(cols[:, 0:4], t["cols"]).then_inc(sm["ld_w"], 16)
            sp.dma_start(relk_f, t["relk_ext"]).then_inc(sm["ld_rel"], 16)
            sp.dma_start(rows[:, 0:7, :], bass.AP(t["rows"].tensor, 0, [[0, P], [1, 7 * D]])).then_inc(sm["ld_w"], 16)
            sp.dma_start(w_out[:, :], t["w_out"]).then_inc(sm["ld_w"], 16)
            zeros = lambda r, n: bass.AP(t["zeros"].tensor, 0, [[0, r], [1, n]])
            sp.dma_start(k_op[PR:PR + 1, :, :, :].rearrange("o a b c -> o (a b c)"), t["ones"]).then_inc(sm["ld_one"], 16)
            sp.dma_start(k_op[KR:64, :, :, :].rearrange("o a b c -> o (a b c)"), zeros(64 - KR, 3 * (H // 2) * TOK)).then_inc(sm["ld_one"], 16)
            for e, (r0, r1) in enumerate(((KR, PR), (0, 64))):
                sp.dma_start(q_op[r0:r1, e, :, :].rearrange("o b c -> o (b c)"), zeros(r1 - r0, (H // 2) * TOK)).then_inc(sm["ld_one"], 16)
            sp.dma_start(rel_k[:, :], bass.AP(t["zeros"].tensor, 0, [[0, P], [1, EXT]])).then_inc(sm["rel_zero"], 16)

            wq = lambda b: write_parts(sp, 0, parts_q, "q_split", b + 1, "scr_q", slice(b * S, b * S + S))
            wk = lambda b: write_parts(sp, 1, parts_k, "k_split", b + 1, "scr_k", slice(b * S, b * S + S))
            rq = lambda b: read_rows(sp, 0, q_op, "scr_q", 16 * (b + 1), "op_q", b * S, S)
            rk = lambda b: read_rows(sp, 1, k_op[:, 0], "scr_k", 16 * (b + 1), "op_k", b * S, S)
            wq(0)
            wk(0)
            rq(0)
            rk(0)
            wq(1)
            sp.wait_ge(sm["rel_split"], 1)
            sp.dma_start(t["scr_rel"].rearrange("d s n -> d s n"), relk_parts).then_inc(sm["scr_rel"], 16)
            wk(1)
            rq(1)
            sp.wait_ge(sm["scr_rel"], 16)
            sp.wait_ge(sm["rel_zero"], 16)
            for u in range(2):
                sp.dma_start(rel_k[64 * u:64 * u + KR, :],
                             t["scr_rel"].rearrange("d s n -> (d s) n")).then_inc(sm["rel_ready"], 16)
            rk(1)
            write_parts(sp, 3, parts_hi, "hi_split", 1, "scr_hi")
            sp.dma_start(rel_v[:, :], bass.AP(t["relv_ext"].tensor, 0, [[HD, P], [1, 384 * HD]])
                         ).then_inc(sm["relv_ready"], 16)
            read_rows(sp, 3, k_op[:, 2], "scr_hi", 16, "op_hi")
            for it in range(IT):
                for b in range(B):
                    sp.wait_ge(sm["mT_ready"], B * it + b + 1)
                    for e in range(2):
                        sp.dma_start(q_op[PR:PR + 1, e, :, b * S + it * P:b * S + it * P + P],
                                     neg_mT[8 * e:8 * e + 8, b * P:b * P + P]).then_inc(sm[m_rows[b]], 16)
            sp.wait_ge(sm["st_psum"], 2 * STEPS * CH)
            sp.dma_start(w_conv, t["w_conv"].rearrange("r i o -> i r o")).then_inc(sm["ld_wide"], 16)
            sp.dma_start(w_in[0], t["w_sin"]).then_inc(sm["ld_wide"], 16)
            sp.dma_start(w_in[1], t["w_1"]).then_inc(sm["ld_wide"], 16)
            sp.dma_start(w_so, t["w_so"].rearrange("(k i) o -> i k o", i=P)).then_inc(sm["ld_wide"], 16)
            for k in range(2):
                sp.dma_start(w_2[:, k, :].rearrange("p (e o) -> p e o", e=NE),
                             t["w_2"].rearrange("e (k i) o -> k i e o", i=P)[k]).then_inc(sm["ld_wide"], 16)
            for dst, name in ((cos, "cos"), (sin, "sin"), (w_q, "w_q"), (w_o, "w_o"), (w_kc, "w_kc"), (w_vc, "w_vc"),
                              (w_k, "w_k"), (w_v, "w_v"), (w_gate[:, 0:NG], "w_gg"), (w_gate[:, NG:], "w_ge")):
                sp.dma_start(dst, t[name]).then_inc(sm["ld_spare"], 16)
            for dst, name, n in ((b_gate[:, 0:NG], "b_gg", NG), (b_gate[:, NG:], "b_ge", NE), (tri, "tri", 16)):
                sp.dma_start(dst, bass.AP(t[name].tensor, 0, [[0, P], [1, n]])).then_inc(sm["ld_spare"], 16)
            sp.wait_ge(sm["ctx_tr"], NT)
            sp.dma_start(shifted[P - CTX:P, 3:NT:4, :], t["ctx"].rearrange("b t d -> t b d")).then_inc(sm["shift_in"], 16)
            sp.wait_ge(sm["ln_out"], 2 * NT)
            by_b = lambda a: a.rearrange("p (b t) d -> p b t d", b=B)
            for sh, t0 in ((CONV, 0), (CTX, 2)):
                sp.dma_start(by_b(shifted[0:P - sh, :, :])[:, :, t0:t0 + 2, :],
                             by_b(xn[sh:P, :, :])[:, :, t0:t0 + 2, :]).then_inc(sm["shift_in"], 16)
                sp.dma_start(shifted[P - sh:P, t0:NT:4, :], xn[0:sh, t0 + 1:NT:4, :]).then_inc(sm["shift_in"], 16)
            sp.wait_ge(sm["comp_ready"], 1)
            for b in range(B):
                sp.dma_start(shifted[P - CONV:P, IT * b + 1, :], comp[CONV * b:CONV * b + CONV, :]).then_inc(sm["conv_in"], 16)
            for n, split in enumerate(("q_split", "k_split")):
                sp.wait_ge(sm[split], 3)
                for u in range(2):
                    sp.dma_start(t["scr"][n][64 * u:64 * u + 64, :, 0:S], parts2[n][64 * u:64 * u + 64, :, 0:S]
                                 ).then_inc(sm["rope_scr_half%d" % u], 16)
            for u in range(2):
                sp.wait_ge(sm["rope_scr_half%d" % u], 32)
                for n, dst in enumerate((q_op, k_op[:, 0])):
                    for e in range(2):
                        src = bass.AP(t["scr"].tensor, (n * P * SLOTS + (4 * u * 2 + e) * KR) * TOK,
                                      [[TOK, KR], [2 * KR * TOK, 4], [1, S]])
                        rows_of = dst[64 * e:64 * e + KR, e] if n == 0 else dst[64 * e:64 * e + KR]
                        sp.dma_start(rows_of[:, 4 * u:4 * u + 4, 0:S], src).then_inc(sm["rope_op_half%d" % u], 16)
            write_parts(sp, 0, parts2[0], "q_split", 4, "scr_q", slice(S, TOK))
            write_parts(sp, 1, parts2[1], "k_split", 4, "scr_k", slice(S, TOK))
            for n in range(B * 4):
                b, g = divmod(n, 4)
                if n == 1:
                    read_rows(sp, 0, q_op, "scr_q", 16 * 3, "op_q", S, S)
                    read_rows(sp, 1, k_op[:, 0], "scr_k", 16 * 3, "op_k", S, S)
                sp.wait_ge(sm["rope_negT"], n + 1)
                for e in range(2):
                    sp.dma_start(q_op[PR:PR + 1, e, 2 * g:2 * g + 2, b * S:b * S + S],
                                 nm_T[2 * e:2 * e + 2, n % 2, :]).then_inc(sm["rope_rows_even" if n % 2 == 0 else "rope_rows_odd"], 16)
            for tt in range(NT):
                b, it = divmod(tt, IT)
                sp.wait_ge(sm["out_ready"], tt + 1)
                sp.dma_start(t["out"][b, it * P:it * P + P, :], x[:, tt, :]).then_inc(sm["out_done"], 16)
            sp.wait_ge(sm["out_done"], 16 * NT)

        @block.gpsimd
        def _(pool):
            chain = [0]

            def link(ins):
                chain[0] += 1
                ins.then_inc(sm["pool"], 1)
                pool.wait_ge(sm["pool"], chain[0])

            ones_col = v_sb[:, :, :, :].rearrange("p v t (h w) -> p (v t h) w", w=VW)[:, :, HD:VW]
            pool.memset(ones_col, 1.0).then_inc(sm["v_ones"], 1)
            pool.wait_ge(sm["ld_w"], 80)
            pool.tensor_scalar(cols[:, C_BQ_SCALED:C_BQ_SCALED + 1], cols[:, C_BQ:C_BQ + 1], Q_SCALE, None, ALU.mult)
            pool.tensor_scalar(cols[:, C_BK_LO:C_BK_HI + 1], cols[:, C_LO:C_HI + 1], cols[:, C_BK:C_BK + 1], None, ALU.add).then_inc(sm["cols_ready"], 1)
            for r in (R_LO, R_HI):
                link(pool.tensor_tensor(rows[:, r, :], rows[:, r, :], rows[:, R_BV, :], ALU.add))
            pool.wait_ge(sm["ld_rel"], 16)
            link(pool.tensor_copy(relk_parts[:, 0, :], relk_f))
            link(pool.tensor_tensor(relk_rest, relk_f, relk_parts[:, 0, :], ALU.subtract))
            link(pool.tensor_copy(relk_parts[:, 3, :], relk_rest))
            link(pool.tensor_tensor(relk_parts[:, 4, :], relk_rest, relk_parts[:, 3, :], ALU.subtract))
            for s in (1, 2):
                pool.tensor_copy(relk_parts[:, s, :], relk_parts[:, 0, :])
            link(pool.tensor_copy(relk_parts[:, 5, :], relk_parts[:, 3, :]))
            pool.sem_inc(sm["rel_split"], 1)
            pool.wait_ge(sm["vf_ready"], 1)
            pool.wait_ge(sm["v_ones"], 1)
            for v, r in enumerate((R_BV, R_LO, R_HI)):
                row = rows[:, r, :]
                add = bass.AP(row.tensor, row.offset, [[8 * D, P], [0, NT], [HD, H], [1, HD]])
                pool.tensor_tensor(v_sb[:, v, :, :].rearrange("p t (h w) -> p t h w", w=VW)[:, :, :, 0:HD],
                                  v_f32.rearrange("p (t h d) -> p t h d", t=NT, d=HD), add, ALU.add
                                  ).then_inc(sm["v_ready"], 1)
            f, o = f32_of[2], parts_lo
            pool.wait_ge(sm["lo_ready"], 2)
            link(pool.tensor_tensor(rest_pool, f, o[:, 0, :], ALU.subtract))
            link(pool.tensor_copy(o[:, 3, :], rest_pool))
            link(pool.tensor_tensor(o[:, 4, :], rest_pool, o[:, 3, :], ALU.subtract))
            link(pool.tensor_copy(o[:, 1, :], o[:, 0, :]))
            link(pool.tensor_copy(o[:, 2, :], o[:, 0, :]))
            pool.tensor_copy(o[:, 5, :], o[:, 3, :]).then_inc(sm["lo_split"], 1)
            write_parts(pool, 2, parts_lo, "lo_split", 1, "scr_lo")
            read_rows(pool, 2, k_op[:, 1], "scr_lo", 16, "op_lo")
            pool.wait_ge(sm["ln_out"], NT)
            pool.wait_ge(sm["ld_w"], 80)
            pool.tensor_tensor(x[:, :, :], x[:, :, :], bass.AP(rows[:, R_BOUT, :].tensor, rows[:, R_BOUT, :].offset, [[8 * D, P], [0, NT], [1, D]]),
                               ALU.add).then_inc(sm["xb_ready"], 1)
            pool.wait_ge(sm["ld_spare"], 16 * 13)
            for w, ws in ((w_q, w_qs), (w_k, w_ks)):
                w, ws = (v.rearrange("p (n c) -> p n c", c=2) for v in (w, ws))
                pool.tensor_scalar(ws[:, :, 0], w[:, :, 1], -1.0, None, ALU.mult).then_inc(sm["swapped_ready"], 1)
                pool.tensor_copy(ws[:, :, 1], w[:, :, 0]).then_inc(sm["swapped_ready"], 1)

            for n in range(2):
                other_parts(pool, link, n, 1)

            for tt in range(NT):
                pool.wait_ge(sm["rms_done"], tt + 1)
                pool.tensor_tensor(x[:, tt, :], x[:, tt, :], shifted[:, tt, :], ALU.add).then_inc(sm["out_ready"], 1)

        @block.scalar
        def _(act):
            def ln_sqrt(done):
                for b in range(B):
                    act.wait_ge(sm["ln_var"], done + b + 1)
                    half = slice(IT * b, IT * b + IT)
                    act.activation(std[:, half], var[:, half], ACT.Sqrt).then_inc(sm["ln_std"], 1)

            def copy_xT(n):
                for c in range(2):
                    act.wait_ge(sm["xT_psum"], NT * n + 4 * c + 4)
                    act.activation(xnT[:, 512 * c:512 * c + 512], ps[:, c, :], ACT.Identity).then_inc(sm["xT_ready"], 1)

            ln_sqrt(0)
            copy_xT(0)
            act.wait_ge(sm["cols_ready"], 1)

            def operand(n, o, src, bias, scale, cs, done):
                act.activation(f32_of[n][:, cs], src, ACT.Identity, bias=bias, scale=scale).then_inc(sm[done], 1)
                act.activation(o[:, 0, cs], src, ACT.Identity, bias=bias, scale=scale).then_inc(sm[done], 1)

            for b in range(B):
                cs = slice(b * S, b * S + S)
                act.wait_ge(sm["q_psum"], b + 1)
                operand(0, parts_q, ps[:, 2 + b, :], cols[:, C_BQ_SCALED:C_BQ_SCALED + 1], Q_SCALE, cs, "f_ready")
                act.wait_ge(sm["k_psum"], b + 1)
                operand(1, parts_k, ps[:, 4 + b, :], cols[:, C_BK:C_BK + 1], 1.0, cs, "f_ready")
            k_psum = ps[:, 4:6, :].rearrange("p a b -> p (a b)")
            operand(3, parts_hi, k_psum, cols[:, C_BK_HI:C_BK_HI + 1], 1.0, slice(0, TOK), "hi_ready")
            act.wait_ge(sm["v_psum"], 1)
            act.activation(v_f32, ps[:, 0:2, :].rearrange("p a b -> p (a b)"), ACT.Identity).then_inc(sm["vf_ready"], 1)
            operand(2, parts_lo, k_psum, cols[:, C_BK_LO:C_BK_LO + 1], 1.0, slice(0, TOK), "lo_ready")

            def bias_evac(s, k):
                n, slot = CH * s + k, k // 4
                act.wait_ge(sm["bias_psum"], n + 1)
                if s >= 3:
                    act.wait_ge(sm["unit_psum"], max(i for i, u in enumerate(units) if u[1:] == ("v", (s - 3, 1))) + 1)
                col = slot * Q + BB * (k % 4)
                act.activation(band[:, s % 3, :, col:col + BB],
                               ps[:, 4, :].rearrange("p (i h) -> p h i", i=BB), ACT.Identity).then_inc(sm["bias_ready"], 1)

            def copy_units(n):
                for k, kind, a in units_of(n):
                    if kind == "m":
                        it, b = a
                        act.wait_ge(sm["unit_psum"], k + 1)
                        if it >= 1:
                            act.wait_ge(sm[m_rows[b]], 32 * it)
                        act.activation(neg_mT[:, b * P:b * P + P], ps[0:H, SHARED_BANKS[k % 2], 0:P], ACT.Identity
                                       ).then_inc(sm["mT_ready"], 1)
                    if kind == "v":
                        s, u = a
                        act.wait_ge(sm["unit_psum"], k + 1)
                        if s >= 1:
                            act.wait_ge(sm["crel_added"], s)
                        for q in range(4):
                            i0 = 16 * q + 8 * u
                            act.activation(crel[:, i0:i0 + 8, :].rearrange("d i h -> d (i h)"),
                                           ps[32 * q:32 * q + HD, SHARED_BANKS[k % 2], 0:8 * B * H], ACT.Identity
                                           ).then_inc(sm["crel_ready"], 1)

            act.wait_ge(sm["hi_split"], 1)
            for k in range(CH):
                bias_evac(0, k)
            copy_units(-1)
            act.wait_ge(sm["scr_hi"], 16)
            act.wait_ge(sm["scr_lo"], 16)
            for n in range(STEPS * CH + 2 * CH):
                s, c = divmod(n, CH)
                b, g = divmod(c, CH // B)
                if s < STEPS:
                    act.wait_ge(sm["st_psum"], 2 * n + 2)
                    if n >= 2:
                        act.wait_ge(sm["pv_done"], n - 1)
                    act.activation(p_out[:, n % 2, :, :].rearrange("p (a e) c -> p e a c", e=2),
                                   ps[:, (2 * n + 1) % 3, :].rearrange("p (e a c) -> p e a c", e=2, a=2), ACT.Exp
                                   ).then_inc(sm["oexp_done"], 1)
                if s + 1 < STEPS:
                    bias_evac(s + 1, c)
                if s < STEPS:
                    act.wait_ge(sm["z_ready"], n + 1)
                    z = band[:, s % 3, :, :].rearrange("p (e k b) c -> p e k b c", e=2, b=B)[:, :, 2 * g:2 * g + 2, b, :]
                    act.activation(z, z, ACT.Exp).then_inc(sm["zexp_done"], 1)
                copy_units(n)

            def copy_ctxn(k, tt):
                act.wait_ge(sm["ctxnT_psum"], NT * k + tt + 1)
                act.activation(xnT[:, tt * P:tt * P + P], ps[:, 2 + tt % 2, 0:P], ACT.Identity).then_inc(sm["ctxnT_ready"], 1)

            def tile_sqrt(tt):
                act.wait_ge(sm["ln_var"], B + tt + 1)
                act.activation(std[:, tt:tt + 1], var[:, tt:tt + 1], ACT.Sqrt).then_inc(sm["ln_std"], 1)

            def square(k, tt):
                if k == 0:
                    act.wait_ge(sm["x_added"], NT + tt + 1)
                else:
                    act.wait_ge(sm["ffn_added"], tt + 1)
                act.activation(squares[:, tt, :], xn[:, tt, :], ACT.Square, accum_out=mv[:, tt, k:k + 1]).then_inc(sm["sq_done"], 1)

            def rms_sqrt(k, tt):
                act.wait_ge(sm["rms_var"], NT * k + tt + 1)
                act.activation(std[:, tt:tt + 1], var[:, tt:tt + 1], ACT.Sqrt).then_inc(sm["rms_std"], 1)

            for tt in range(NT + 6):
                if tt < NT:
                    copy_ctxn(0, tt)
                if tt >= 6:
                    tile_sqrt(tt - 6)
            act.wait_ge(sm["memT_psum"], 1)
            act.activation(memT, ps[:, 0, 0:B * CTX], ACT.Identity).then_inc(sm["memT_ready"], 1)
            act.wait_ge(sm["w_cT_psum"], 1)
            act.activation(w_cT, ps[0:DC, 6, 0:2 * D].rearrange("r (n i) -> r n i", n=2), ACT.Identity).then_inc(sm["w_cT_ready"], 1)
            act.wait_ge(sm["w_full_psum"], 1)
            act.activation(w_full, ps[:, 7, 0:3 * D].rearrange("i (n o) -> i n o", n=3), ACT.Identity).then_inc(sm["w_full_ready"], 1)
            ln_sqrt(B + NT)
            copy_xT(1)

            def first_part(n, b):
                act.wait_ge(sm["rot_done"], 2 * b + n + 1)
                for slot in (0, 3, 4) if n == 0 else (0, 1, 2):
                    act.activation(parts2[n][:, slot, b * S:b * S + S], f32_of[n][:, b * S:b * S + S], ACT.Identity
                                   ).then_inc(sm["part_ready"], 1)

            for b in range(B):
                for n in range(2):
                    first_part(n, b)
            act.wait_ge(sm["v2_psum"], 1)
            for b in range(B):
                act.activation(v_sb[:, 0, IT * b:IT * b + IT, :].rearrange("p t (h w) -> p (t h) w", w=VW)[:, :, 0:HD],
                               ps[:, (1, 4)[b], :].rearrange("p (n d) -> p n d", d=HD), ACT.Identity).then_inc(sm["v2_ready"], 1)
            for j in range(-LEAD, 128):
                m = (j + LEAD - 19) // 16
                if (j + LEAD - 19) % 16 == 0 and 0 <= m < 8:
                    act.wait_ge(sm["rope_negT_psum"], m + 1)
                    if m >= 2:
                        act.wait_ge(sm["rope_rows_even" if m % 2 == 0 else "rope_rows_odd"], 32 * (m // 2))
                    act.activation(nm_T[:, m % 2, :], ps[0:4, 7, :], ACT.Identity).then_inc(sm["rope_negT"], 1)
                if j == 0:
                    act.wait_ge(sm["q_split"], 4)
                    act.wait_ge(sm["k_split"], 4)
                if j == 12:
                    act.wait_ge(sm["scr_q"], 16 * 3)
                if j >= 0:
                    k = j // 4
                    act.wait_ge(sm["rope_st_psum"], j + 1)
                    if k >= 4:
                        act.wait_ge(sm["rope_pv_done"], k - 3)
                    act.activation(p_ring[:, k % 4, j % 4, :], ps[:, 3 + j % 3, :], ACT.Exp).then_inc(sm["rope_exp_done"], 1)
            for tt in range(NT + 5):
                if tt < NT:
                    copy_ctxn(1, tt)
                if 0 <= tt - 4 < NT:
                    square(0, tt - 4)
                if 0 <= tt - 5 < NT:
                    rms_sqrt(0, tt - 5)

            def silu_of(n):
                act.wait_ge(sm["mlp_psum"], n + 1)
                if n >= 4:
                    act.wait_ge(sm["hid_ready"], n - 3)
                act.activation(silu[:, n % 4, :], ps[:, 2 * (n % 3), :], ACT.Silu).then_inc(sm["silu_done"], 1)

            for c in range(2):
                act.wait_ge(sm["xT_psum"], NT * 2 + 4 * c + 4)
                act.activation(xnT[:, 512 * c:512 * c + 512], ps[:, 6 + c, :], ACT.Identity).then_inc(sm["xT_ready"], 1)
            for n in range(SILU_FIRST):
                silu_of(n)
            act.wait_ge(sm["group_sub"], 1)
            act.activation(gsc[:, 128:144], gsc[:, 112:128], ACT.Exp).then_inc(sm["group_exp"], 1)
            act.wait_ge(sm["expert_sub"], 1)
            act.activation(gsc[:, 256:288], gsc[:, 224:256], ACT.Exp).then_inc(sm["expert_exp"], 1)
            for n in range(SILU_FIRST, 8):
                silu_of(n)
            for tt in range(NT):
                square(1, tt)
                rms_sqrt(1, tt)

        @block.vector
        def _(dve):
            chain = [0]

            def link(ins):
                chain[0] += 1
                ins.then_inc(sm["dve"], 1)
                dve.wait_ge(sm["dve"], chain[0])

            def stats_of(tt):
                return dve.bn_stats(stats[:, tt, :], x[:, tt, :])

            def layernorm(done, left=range(IT)):
                for b in range(B):
                    if done == 0:
                        dve.wait_ge(sm[ld_x[b]], 16)
                    ts, half = range(IT * b, IT * b + IT), slice(IT * b, IT * b + IT)
                    for it in left:
                        i = stats_of(IT * b + it)
                    link(i)
                    for tt in ts:
                        i = dve.bn_aggr(mv[:, tt, :], stats[:, tt, :])
                    link(i)
                    dve.tensor_scalar(var[:, half], mv[:, half, 1], LN_EPS, None, ALU.add).then_inc(sm["ln_var"], 1)
                for b in range(B):
                    half = slice(IT * b, IT * b + IT)
                    dve.wait_ge(sm["ln_std"], done + b + 1)
                    link(dve.reciprocal(rstd[:, half], std[:, half]))
                    for tt in range(IT * b, IT * b + IT):
                        dve.tensor_scalar(xn[:, tt, :], x[:, tt, :], mv[:, tt, 0:1], rstd[:, tt:tt + 1],
                                          ALU.subtract, ALU.mult).then_inc(sm["ln_out"], 1)

            slot_of = lambda ps_: [[s for s in range(SLOTS) if ps_[s] == k] for k in range(3)]
            layernorm(0)
            def split_rest(f, o, order, rest, done):
                one, two, three = order
                link(dve.tensor_tensor(rest, f, o[:, one[0], :], ALU.subtract))
                link(dve.tensor_copy(o[:, two[0], :], rest))
                dve.tensor_tensor(o[:, three[0], :], rest, o[:, two[0], :], ALU.subtract)
                dve.tensor_copy(o[:, two[1], :], o[:, two[0], :])
                dve.tensor_copy(o[:, one[2], :], o[:, one[0], :])
                link(dve.tensor_copy(o[:, one[1], :], o[:, one[0], :]))
                dve.sem_inc(sm[done], 1)

            for b in range(B):
                cs = slice(b * S, b * S + S)
                for n, (o, parts_of, done) in enumerate(((parts_q, Q_PARTS, "q_split"), (parts_k, K_PARTS, "k_split"))):
                    dve.wait_ge(sm["f_ready"], 4 * b + 2 * n + 2)
                    split_rest(f32_of[n][:, cs], o[:, :, cs], slot_of(parts_of), rest_dve[:, 0:S], done)
            def take_unit(k, kind, a):
                bank = SHARED_BANKS[k % 2]
                if kind == "s":
                    tt, p, e = a
                    dve.wait_ge(sm["unit_psum"], k + 1)
                    dve.tensor_reduce(m_qk[:, tt, 8 * e + p:8 * e + p + 1], ps[:, bank, :], AX_X, ALU.max
                                      ).then_inc(sm["m_done"], 1)
                if kind == "r":
                    tt, r, e = a
                    nh = min(3, H // 2 - 3 * r)
                    dve.wait_ge(sm["unit_psum"], k + 1)
                    dve.tensor_reduce(m_rel[:, tt, 8 * e + 3 * r:8 * e + 3 * r + nh],
                                      ps[:, bank, 0:nh * (2 * R + 1)].rearrange("p (h c) -> p h c", h=nh),
                                      AX_X, ALU.max).then_inc(sm["r_done"], 1)
                if kind == "m":
                    it, b = a
                    tt = IT * b + it
                    dve.wait_ge(sm["r_done"], 6 * (B * it + b + 1))
                    dve.wait_ge(sm["m_done"], 16 * (B * it + b + 1))
                    dve.scalar_tensor_tensor(neg_m[:, tt, :], m_qk[:, tt, :], -1.0, m_rel[:, tt, :],
                                             ALU.mult, ALU.subtract).then_inc(sm["negm_ready"], 1)

            def ctx_evac(s):
                dve.wait_ge(sm["crel_added"], s + 1)
                if s == 0:
                    dve.wait_ge(sm["lo_split"], 1)
                dve.tensor_copy(ctxT[:, :, Q * s:Q * s + Q], ps[:, 5 + s % 2, :].rearrange("p (c i) -> p c i", i=Q)
                                ).then_inc(sm["ctx_ready"], 1)

            dve.wait_ge(sm["hi_ready"], 2)
            split_rest(f32_of[3], parts_hi, slot_of(K_PARTS), rest_dve, "hi_split")
            dve.wait_ge(sm["lo_ready"], 2)
            dve.memset(ps[:, 5:7, :], 0.0).then_inc(sm["pv_zero"], 1)
            for u in units_of(-1):
                take_unit(*u)
            for n in range(STEPS * CH + 2 * CH):
                s, c = divmod(n, CH)
                b, g = divmod(c, CH // B)
                if c == 1 and s >= 2:
                    ctx_evac(s - 2)
                us = units_of(n)
                if s < STEPS:
                    dve.wait_ge(sm["st_psum"], 2 * n + 1)
                    if c in (0, 4):
                        dve.wait_ge(sm["bias_ready"], CH * (s + 1))
                    z = band[:, s % 3, :, :].rearrange("p (e k b) c -> p e k b c", e=2, b=B)[:, :, 2 * g:2 * g + 2, b, :]
                    dve.tensor_tensor(z, ps[:, 2 * n % 3, :].rearrange("p (e a c) -> p e a c", e=2, a=2), z, ALU.add
                                      ).then_inc(sm["z_ready"], 1)
                for u in us:
                    take_unit(*u)

            def ln_stats(tt):
                dve.wait_ge(sm["x_added"], tt + 1)
                dve.bn_stats(stats[:, tt, :], x[:, tt, :]).then_inc(sm["bn_done"], 1)

            def ln_aggr(tt):
                dve.wait_ge(sm["bn_done"], tt + 1)
                dve.bn_aggr(mv[:, tt, :], stats[:, tt, :]).then_inc(sm["aggr_done"], 1)

            def ln_var(tt):
                dve.wait_ge(sm["aggr_done"], tt + 1)
                dve.tensor_scalar(var[:, tt:tt + 1], mv[:, tt, 1:2], LN_EPS, None, ALU.add).then_inc(sm["ln_var"], 1)

            def ln_rstd(tt):
                dve.wait_ge(sm["ln_std"], B + tt + 1)
                dve.reciprocal(rstd[:, tt:tt + 1], std[:, tt:tt + 1]).then_inc(sm["rstd_done"], 1)

            def ln_norm(tt):
                dve.wait_ge(sm["rstd_done"], tt + 1)
                dve.tensor_scalar(xn[:, tt, :], x[:, tt, :], mv[:, tt, 0:1], rstd[:, tt:tt + 1],
                                  ALU.subtract, ALU.mult).then_inc(sm["ln_out"], 1)

            def rms_var(k, tt):
                dve.wait_ge(sm["sq_done"], NT * k + tt + 1)
                dve.tensor_scalar(var[:, tt:tt + 1], mv[:, tt, k:k + 1], 1.0 / D, RMS_EPS, ALU.mult, ALU.add).then_inc(sm["rms_var"], 1)

            def rms_rstd(k, tt):
                dve.wait_ge(sm["rms_std"], NT * k + tt + 1)
                dve.reciprocal(rstd[:, tt:tt + 1], std[:, tt:tt + 1]).then_inc(sm["rstd_done"], 1)

            def rms_out(k, tt):
                dve.wait_ge(sm["rstd_done"], NT * (k + 1) + tt + 1)
                dst, gain, done = ((xn, R_N1, "ln_out"), (shifted, R_N2, "rms_done"))[k]
                dve.scalar_tensor_tensor(dst[:, tt, :], xn[:, tt, :], rstd[:, tt:tt + 1], rows[:, gain, :], ALU.mult, ALU.mult
                                         ).then_inc(sm[done], 1)

            def attn_finish(k, dst, resid, later):
                for tt in range(NT + max(later)):
                    if tt < NT:
                        dve.wait_ge(sm["ctx_tr"], NT * k + tt + 1)
                        src = ps[:, tt % 2, :].rearrange("p (h r) -> p h r", r=32)
                        dve.reciprocal(rsum[:, tt % 2, :], src[:, :, HD]).then_inc(sm["rsum_done"], 1)
                    if tt == 0 and k == 0:
                        dve.wait_ge(sm["xb_ready"], 1)
                    if 3 <= tt < NT + 3:
                        dve.wait_ge(sm["y_psum"], NT * k + tt - 2)
                        dve.tensor_tensor(resid[:, tt - 3, :], ps[:, 4 + (tt - 3) % 2, 0:P], resid[:, tt - 3, :], ALU.add
                                          ).then_inc(sm["x_added"], 1)
                    if tt < NT:
                        dve.wait_ge(sm["rsum_done"], NT * k + tt + 1)
                        rs = rsum[:, tt % 2, :]
                        dve.tensor_tensor(dst[:, tt, :].rearrange("p (h d) -> p h d", d=HD), src[:, :, 0:HD],
                                          bass.AP(rs.tensor, rs.offset, [[2 * H, P], [1, H], [0, HD]]), ALU.mult
                                          ).then_inc(sm["ctx_norm"], 1)
                    for lag, step in sorted(later.items(), reverse=True):
                        if 0 <= tt - lag < NT:
                            step(tt - lag)

            attn_finish(0, ctxn0, x, {4: ln_stats, 5: ln_aggr, 6: ln_var, 8: ln_rstd, 9: ln_norm})
            dve.wait_ge(sm["comp_psum"], 1)
            dve.tensor_tensor(comp, ps[0:B * CONV, 1, 0:D], rows[0:B * CONV, R_CONV, :], ALU.add).then_inc(sm["comp_ready"], 1)
            dve.wait_ge(sm["shift_in"], 16 * 5)
            by_b = lambda a: a.rearrange("p (b t) d -> p b t d", b=B)
            add_shifted = lambda t0, n: dve.tensor_tensor(*(by_b(a)[:, :, t0:t0 + n, :] for a in (x[:, :, :], x[:, :, :], shifted)), ALU.add)
            add_shifted(0, 1)
            link(add_shifted(2, 2))
            for b in range(B):
                for it in (0, 2, 3):
                    stats_of(IT * b + it)
            dve.wait_ge(sm["conv_in"], 16 * B)
            link(add_shifted(1, 1))
            layernorm(B + NT, (1,))

            def rotate(n, b):
                bank, scale = ((2, 7), (5, 2))[n][b], (Q_SCALE, 1.0)[n]
                swapped = ((3, 0), (6, 3))[n][b]
                f, r = f32_of[n][:, b * S:b * S + S], rest2[:, 512 * n:512 * n + 512]
                dve.wait_ge(sm["rope_psum"], 4 * b + 2 * n + 1)
                dve.scalar_tensor_tensor(f, ps[:, bank, :], scale, cos, ALU.mult, ALU.mult)
                dve.wait_ge(sm["rope_psum"], 4 * b + 2 * n + 2)
                link(dve.scalar_tensor_tensor(r, ps[:, swapped, :], scale, sin, ALU.mult, ALU.mult))
                dve.tensor_tensor(f, f, r, ALU.add).then_inc(sm["rot_done"], 1)

            for n in range(2):
                rotate(n, 0)
            for n in range(2):
                other_parts(dve, link, n, 0)
            for n in range(2):
                rotate(n, 1)

            for j in range(-LEAD, 128 + 10):
                su = j + LEAD
                if su < 128:
                    m, k = divmod(su, 16)
                    b, g = divmod(m, 4)
                    it, hh = divmod(k, 4)
                    dve.wait_ge(sm["rmax_psum"], su + 1)
                    dve.tensor_reduce(m_qk[:, IT * b + it, 4 * g + hh:4 * g + hh + 1], ps[:, su % 3, :], AX_X, ALU.max
                                      ).then_inc(sm["rmax_done"], 1)
                    if k == 15:
                        dve.wait_ge(sm["rmax_done"], 16 * m + 16)
                        dve.tensor_scalar(neg_m[:, IT * b:IT * b + IT, 4 * g:4 * g + 4], m_qk[:, IT * b:IT * b + IT, 4 * g:4 * g + 4],
                                          -1.0, None, ALU.mult).then_inc(sm["rope_negm"], 1)
                if j >= 21 and (j - 21) % 16 == 0:
                    n = (j - 21) // 16
                    b, g = divmod(n, 4)
                    dve.wait_ge(sm["rope_pv_done"], 4 * n + 4)
                    dve.tensor_copy(ctxT[:, 4 * b + g, :], ps[:, 6, :]).then_inc(sm["rope_ctx_ready"], 1)

            attn_finish(1, ctxn, xn, {5: lambda u: rms_var(0, u), 7: lambda u: rms_rstd(0, u), 8: lambda u: rms_out(0, u)})

            def cut(a, n, w=1):
                v = gsc[:, a:a + NT * n * w]
                return v.rearrange("p (t n) -> p t n", n=n) if w == 1 else v.rearrange("p (t n w) -> p t n w", n=n, w=w)

            def spread(v, n):
                return bass.AP(v.tensor, v.offset, [v.ap[0], v.ap[1], [0, n]])

            def hidden(n):
                c, w, k = n // 4, (n // 2) % 2, n % 2
                dve.wait_ge(sm["silu_done"], n + 1)
                dve.tensor_tensor(hid[w][:, k, c * 512:c * 512 + 512], ps[:, 2 * (n % 3) + 1, :], silu[:, n % 4, :], ALU.mult
                                  ).then_inc(sm["hid_ready"], 1)

            for n in range(SILU_FIRST):
                hidden(n)
            logit, gmax = cut(0, 10), gsc[:, 80:88]
            dve.wait_ge(sm["gate_psum"], 1)
            link(dve.tensor_tensor(logit, ps[:, 6, 0:80].rearrange("p (t n) -> p t n", n=10),
                                   bass.AP(b_gate.tensor, b_gate.offset, [b_gate.ap[0], [0, NT], [1, 10]]), ALU.add))
            link(dve.tensor_reduce(gmax, logit[:, :, 0:NG], AX_X, ALU.max))
            dve.tensor_tensor(cut(112, 2), logit[:, :, 0:NG], spread(gmax, 2), ALU.subtract).then_inc(sm["group_sub"], 1)
            gexp, gsum, grec, gprob = cut(128, 2), gsc[:, 88:96], gsc[:, 96:104], cut(144, 2)
            dve.wait_ge(sm["group_exp"], 1)
            link(dve.tensor_reduce(gsum, gexp, AX_X, ALU.add))
            link(dve.reciprocal(grec, gsum))
            link(dve.tensor_tensor(gprob, gexp, spread(grec, 2), ALU.mult))
            gtop, second, first = gsc[:, 104:112], gsc[:, 160:168], gsc[:, 168:176]
            dve.tensor_reduce(gtop, gprob, AX_X, ALU.max)
            link(dve.tensor_tensor(second, gprob[:, :, 1], gprob[:, :, 0], ALU.is_gt))
            link(dve.tensor_scalar(first, second, -1.0, 1.0, ALU.mult, ALU.add))
            sel, sel2 = cut(192, 4), cut(288, 4)
            dve.tensor_tensor(sel, logit[:, :, 2:6], spread(first, 4), ALU.mult)
            link(dve.tensor_tensor(sel2, logit[:, :, 6:10], spread(second, 4), ALU.mult))
            link(dve.tensor_tensor(sel, sel, sel2, ALU.add))
            emax, esum, erec = gsc[:, 176:184], gsc[:, 184:192], gsc[:, 320:328]
            link(dve.tensor_reduce(emax, sel, AX_X, ALU.max))
            dve.tensor_tensor(cut(224, 4), sel, spread(emax, 4), ALU.subtract).then_inc(sm["expert_sub"], 1)
            for n in range(SILU_FIRST, HID_FIRST):
                hidden(n)
            prob = cut(256, 4)
            dve.wait_ge(sm["expert_exp"], 1)
            link(dve.tensor_reduce(esum, prob, AX_X, ALU.add))
            link(dve.reciprocal(erec, esum))
            link(dve.tensor_tensor(prob, prob, spread(erec, 4), ALU.mult))
            link(dve.tensor_tensor(prob, prob, spread(gtop, 4), ALU.mult))
            other = bass.AP(prob.tensor, prob.offset, [prob.ap[0], [4, NT], [0, 4], [1, 4]])
            own = bass.AP(prob.tensor, prob.offset, [prob.ap[0], [4, NT], [1, 4], [0, 4]])
            above, tied, ahead, keep = cut(384, 4, 4), cut(512, 4, 4), cut(640, 4), cut(672, 4)
            dve.tensor_tensor(above, other, own, ALU.is_gt)
            link(dve.tensor_tensor(tied, other, own, ALU.is_equal))
            link(dve.tensor_tensor(tied, tied, bass.AP(tri.tensor, tri.offset, [tri.ap[0], [0, NT], [4, 4], [1, 4]]), ALU.mult))
            link(dve.tensor_tensor(above, above, tied, ALU.add))
            link(dve.tensor_reduce(ahead, above, AX_X, ALU.add))
            link(dve.scalar_tensor_tensor(keep, ahead, 1.5, prob, ALU.is_lt, ALU.mult))
            gate = cut(768, 8)
            dve.tensor_tensor(gate[:, :, 0:4], keep, spread(first, 4), ALU.mult)
            link(dve.tensor_tensor(gate[:, :, 4:8], keep, spread(second, 4), ALU.mult))

            for n in range(HID_FIRST, 8):
                hidden(n)

            def combine(tt):
                dve.wait_ge(sm["expert_psum"], tt + 1)
                banks = Y_BANKS[tt % 2]
                expert = lambda e: ps[:, banks[e // 4], (e % 4) * D:(e % 4) * D + D]
                acc, acc2 = xn[:, tt, :], odd_sum[:, tt % 2, :]

                def link2(ins):
                    chain[0] += 1
                    ins.then_inc(sm["dve"], 1)
                    dve.wait_ge(sm["dve"], chain[0] - 1)

                link2(dve.tensor_tensor(acc, ps[:, banks[2], 0:D], acc, ALU.add))
                link2(dve.tensor_scalar(acc2, expert(1), gate[:, tt, 1:2], None, ALU.mult))
                for e in (0, 3, 2, 5, 4, 7):
                    a = acc2 if e % 2 else acc
                    link2(dve.scalar_tensor_tensor(a, expert(e), gate[:, tt, e:e + 1], a, ALU.mult, ALU.add))
                link(dve.scalar_tensor_tensor(acc, expert(6), gate[:, tt, 6:7], acc, ALU.mult, ALU.add))
                dve.tensor_tensor(acc, acc, acc2, ALU.add).then_inc(sm["ffn_added"], 1)

            for tt in range(NT + 1):
                if tt >= 1:
                    rms_var(1, tt - 1)
                if tt < NT:
                    combine(tt)
                if tt >= 1:
                    rms_rstd(1, tt - 1)
                    rms_out(1, tt - 1)
        @block.tensor
        def _(pe):
            pe.wait_ge(sm["ld_w"], 80)
            for b in range(B):
                for tt in range(IT * b, IT * b + IT):
                    pe.wait_ge(sm["ln_out"], tt + 1)
                    pe.transpose(ps[:, b, (tt % IT) * P:(tt % IT) * P + P], xn[:, tt, :], ident[:, :]).then_inc(sm["xT_psum"], 1)
            for b in range(B):
                pe.wait_ge(sm["xT_ready"], b + 1)
                for n, done in ((0, "q_psum"), (1, "k_psum")):
                    pe.matmul(ps[:, 2 + 2 * n + b, :], w_qkv[:, n * D:n * D + D], xnT[:, b * S:b * S + S],
                              start=True, stop=True).then_inc(sm[done], 1)
            for tt in range(NT):
                i = pe.matmul(ps[:, tt // 4, (tt % 4) * P:(tt % 4) * P + P], xnT[:, tt * P:tt * P + P], w_qkv[:, 2 * D:3 * D],
                              start=True, stop=True)
            i.then_inc(sm["v_psum"], 1)

            def fill_unit(k, kind, a):
                bank = SHARED_BANKS[k % 2]
                if k >= 2:
                    pe.wait_ge(*freed(k - 2))
                if kind == "s":
                    tt, p, e = a
                    b = tt // IT
                    i = pe.matmul(ps[:, bank, :], q_op[0:PR, e, p, tt * P:tt * P + P], k_op[0:PR, 0, p, b * S:b * S + S], start=True, stop=True)
                if kind == "r":
                    tt, r, e = a
                    for j, p in enumerate(range(3 * r, min(3 * r + 3, H // 2))):
                        i = pe.matmul(ps[:, bank, j * (2 * R + 1):(j + 1) * (2 * R + 1)],
                                      q_op[0:PR, e, p, tt * P:tt * P + P], rel_k[0:PR, ZERO - R:ZERO + R + 1], start=True, stop=True)
                if kind == "m":
                    it, b = a
                    pe.wait_ge(sm["negm_ready"], B * it + b + 1)
                    i = pe.transpose(ps[0:H, bank, 0:P], neg_m[:, IT * b + it, :], ident[:, :])
                if kind == "v":
                    s, u = a
                    if u == 0:
                        pe.wait_ge(sm["zexp_done"], CH * (s + 1))
                    for ii in range(8):
                        for slot in range(2):
                            jt = slots_of(s)[slot][0]
                            for q in range(4):
                                qi = 16 * q + 8 * u + ii
                                w = P * jt - (Q * s + qi) + ZERO
                                i = pe.matmul(ps[32 * q:32 * q + HD, bank, B * H * ii:B * H * (ii + 1)], rel_v[:, w * HD:(w + 1) * HD],
                                              band[:, s % 3, :, slot * Q + qi], start=(slot == 0), stop=(slot == 1), skip_group_check=True)
                i.then_inc(sm["unit_psum"], 1)

            def bias_block(s, k):
                n, jt = CH * s + k, slots_of(s)[k // 4][0]
                if n >= 1:
                    pe.wait_ge(sm["bias_ready"], n)
                for ii in range(BB):
                    i = Q * s + BB * (k % 4) + ii
                    w = P * jt - i + ZERO
                    mm = pe.matmul(ps[:, 4, B * H * ii:B * H * (ii + 1)], rel_k[0:PR, w:w + P], q_flat[0:PR, :, i], start=True, stop=True)
                mm.then_inc(sm["bias_psum"], 1)

            def scores(m):
                n, other = divmod(m, 2)
                s, c = divmod(n, CH)
                b, g = divmod(c, CH // B)
                if m >= 3:
                    if other:
                        pe.wait_ge(sm["z_ready"], n)
                    else:
                        pe.wait_ge(sm["oexp_done"], n - 1)
                for k, (jt, v) in enumerate(slots_of(s)[2 * other:2 * other + 2]):
                    for e in range(2):
                        for a in range(2):
                            col = 2 * P * e + P * a + Q * k
                            i = pe.matmul(ps[:, m % 3, col:col + Q],
                                          k_op[0:PR + 1, v, 2 * g + a, b * S + jt * P:b * S + jt * P + P],
                                          q_op[0:PR + 1, e, 2 * g + a, b * S + Q * s:b * S + Q * s + Q],
                                          start=True, stop=True)
                i.then_inc(sm["st_psum"], 1)

            def products(n):
                s, c = divmod(n, CH)
                b, g = divmod(c, CH // B)
                pe.wait_ge(sm["oexp_done"], n + 1)
                pe.wait_ge(sm["zexp_done"], n + 1)
                if c == 0 and s >= 2:
                    pe.wait_ge(sm["ctx_ready"], s - 1)
                for slot, (jt, v) in enumerate(slots_of(s)):
                    for hh in range(4):
                        h = 4 * g + hh
                        if slot < 2:
                            rhs = band[:, s % 3, row_of(h, b), slot * Q:slot * Q + Q]
                        else:
                            rhs = p_out[:, n % 2, hh, (slot - 2) * Q:(slot - 1) * Q]
                        i = pe.matmul(ps[32 * hh:32 * hh + VW, 5 + s % 2, Q * c:Q * c + Q],
                                      v_sb[:, v, IT * b + jt, h * VW:h * VW + VW], rhs,
                                      start=(c == 0 and slot == 0), stop=False, skip_group_check=True)
                i.then_inc(sm["pv_done"], 1)

            def add_crel(s):
                pe.wait_ge(sm["crel_ready"], 8 * (s + 1))
                for c in range(CH):
                    b, g = divmod(c, CH // B)
                    for hh in range(4):
                        i = pe.matmul(ps[32 * hh:32 * hh + HD, 5 + s % 2, Q * c:Q * c + Q], ident[0:HD, 0:HD],
                                      crel[:, :, row_of(4 * g + hh, b)], start=False, stop=True, skip_group_check=True)
                i.then_inc(sm["crel_added"], 1)


            pe.wait_ge(sm["f_ready"], 8)
            pe.wait_ge(sm["ld_one"], 64)
            first = units_of(-1)
            for k, u in enumerate(first):
                if u[1] == "s" and u[2][1:] == (0, 0):
                    b = u[2][0] // IT
                    pe.wait_ge(sm["op_q"], 32 * (b + 1))
                    pe.wait_ge(sm["op_k"], 32 * (b + 1))
                if u[1] == "r":
                    pe.wait_ge(sm["rel_ready"], 32)
                if k >= FIRST_BIAS and (k - FIRST_BIAS) % 2 == 0 and (k - FIRST_BIAS) // 2 < CH:
                    if k == FIRST_BIAS:
                        pe.wait_ge(sm["op_q"], 64)
                        pe.wait_ge(sm["rel_ready"], 32)
                        pe.wait_ge(sm["hi_ready"], 2)
                        pe.wait_ge(sm["lo_ready"], 2)
                    bias_block(0, (k - FIRST_BIAS) // 2)
                fill_unit(*u)

            for name, val in (("pv_zero", 1), ("m_rows0", 32), ("ld_one", 64), ("v_ready", 3), ("op_hi", 32)):
                pe.wait_ge(sm[name], val)
            scores(0)
            scores(1)
            for n in range(STEPS * CH + 2 * CH):
                s, c = divmod(n, CH)
                us = units_of(n)
                nxt = n + 1 if n + 1 < STEPS * CH else None
                if nxt and nxt % (2 * CH) in (0, CH // B):
                    pe.wait_ge(sm[m_rows[nxt % CH // (CH // B)]], 32 * (nxt // (2 * CH) + 1))
                if nxt == 3 * CH:
                    pe.wait_ge(sm["op_lo"], 32)
                if nxt == 1:
                    pe.wait_ge(sm["relv_ready"], 16)
                if nxt:
                    scores(2 * nxt)
                if us:
                    fill_unit(*us.pop(0))
                if s + 1 < STEPS:
                    bias_block(s + 1, c)
                if us:
                    fill_unit(*us.pop(0))
                if nxt:
                    scores(2 * nxt + 1)
                if c == 0 and s >= 2:
                    add_crel(s - 2)
                if us:
                    fill_unit(*us.pop(0))
                if 1 <= n <= STEPS * CH:
                    products(n - 1)
                for u in us:
                    fill_unit(*u)

            def attn_finish(k, src, w):
                for tt in range(NT + 2):
                    b, it = divmod(tt, IT)
                    if tt < NT:
                        if tt >= 2:
                            pe.wait_ge(sm["ctx_norm"], NT * k + tt - 1)
                        for g in range(4):
                            i = pe.transpose(ps[:, tt % 2, g * P:g * P + P], ctxT[:, 4 * b + g, it * P:it * P + P], ident[:, :])
                        i.then_inc(sm["ctx_tr"], 1)
                    if 1 <= tt <= NT:
                        u = tt - 1
                        pe.wait_ge(sm["ctx_norm"], NT * k + u + 1)
                        if u >= 2:
                            pe.wait_ge(sm["ctxnT_ready"], NT * k + u - 1)
                        pe.transpose(ps[:, 2 + u % 2, 0:P], src[:, u, :], ident[:, :]).then_inc(sm["ctxnT_psum"], 1)
                    if tt >= 2:
                        u = tt - 2
                        pe.wait_ge(sm["ctxnT_ready"], NT * k + u + 1)
                        if u >= 2:
                            pe.wait_ge(sm["x_added"], NT * k + u - 1)
                        pe.matmul(ps[:, 4 + u % 2, 0:P], xnT[:, u * P:u * P + P], w, start=True, stop=True).then_inc(sm["y_psum"], 1)

            pe.wait_ge(sm["ctx_ready"], STEPS)
            attn_finish(0, ctxn0, w_out[:, :])

            pe.wait_ge(sm["swapped_ready"], 4)
            for n, w in enumerate((w_kc, w_vc)):
                i = pe.transpose(ps[0:DC, 6, n * D:n * D + D], w, ident[:, :])
            i.then_inc(sm["w_cT_psum"], 1)

            pe.wait_ge(sm["ln_out"], NT + IT + 3)
            for b in range(B):
                i = pe.transpose(ps[:, 0, CTX * b:CTX * b + CTX], xn[0:CTX, IT * b + 2, :], ident[0:CTX, 0:CTX])
            i.then_inc(sm["memT_psum"], 1)
            pe.wait_ge(sm["memT_ready"], 1)
            pe.wait_ge(sm["ld_wide"], 16 * 6)
            for r in range(RATE):
                i = pe.matmul(ps[0:B * CONV, 1, 0:D], memT[:, r:B * CTX:RATE], w_conv[:, r, :], start=(r == 0), stop=(r == RATE - 1))
            i.then_inc(sm["comp_psum"], 1)

            pe.wait_ge(sm["w_cT_ready"], 1)
            for n, (c, w) in enumerate(((0, w_k), (0, w_ks), (1, w_v))):
                i = pe.matmul(ps[:, 7, n * D:n * D + D], w_cT[:, c, :], w, start=True, stop=True)
            i.then_inc(sm["w_full_psum"], 1)

            for tt in range(NT):
                pe.wait_ge(sm["ln_out"], NT * 2 + tt + 1)
                pe.transpose(ps[:, tt // 4, (tt % 4) * P:(tt % 4) * P + P], xn[:, tt, :], ident[:, :]).then_inc(sm["xT_psum"], 1)

            def project(bank, w, b):
                pe.matmul(ps[:, bank, :], w, xnT[:, b * S:b * S + S], start=True, stop=True).then_inc(sm["rope_psum"], 1)

            pe.wait_ge(sm["w_full_ready"], 1)
            for b in range(B):
                pe.wait_ge(sm["xT_ready"], 3 + b)
                project((2, 7)[b], w_q, b)
                project((3, 0)[b], w_qs, b)
                if b == 1:
                    pe.wait_ge(sm["rot_done"], 1)
                project((5, 2)[b], w_full[:, 0, :], b)
                project((6, 3)[b], w_full[:, 1, :], b)
            for tt in range(NT):
                i = pe.matmul(ps[:, (1, 4)[tt // IT], (tt % IT) * P:(tt % IT) * P + P], xnT[:, tt * P:tt * P + P], w_full[:, 2, :],
                              start=True, stop=True)
            i.then_inc(sm["v2_psum"], 1)

            pe.wait_ge(sm["rope_op_half0"], 64)
            pe.wait_ge(sm["rot_done"], 4)
            pe.wait_ge(sm["v2_ready"], 2)
            for j in range(-LEAD, 128 + 8):
                if 0 <= j < 128:
                    n, k = divmod(j, 16)
                    b, g = divmod(n, 4)
                    jt, hh = divmod(k, 4)
                    a, e = divmod(hh, 2)
                    if k == 0:
                        pe.wait_ge(sm["rope_rows_even" if n % 2 == 0 else "rope_rows_odd"], 32 * (n // 2 + 1))
                    if j >= 3:
                        pe.wait_ge(sm["rope_exp_done"], j - 2)
                    pe.matmul(ps[:, 3 + j % 3, :], k_op[0:PR + 1, 0, 2 * g + a, b * S + jt * P:b * S + jt * P + P],
                              q_op[0:PR + 1, e, 2 * g + a, b * S:b * S + S], start=True, stop=True).then_inc(sm["rope_st_psum"], 1)
                su = j + LEAD
                if su < 128:
                    m, k = divmod(su, 16)
                    b, g = divmod(m, 4)
                    it, hh = divmod(k, 4)
                    a, e = divmod(hh, 2)
                    if su >= 3:
                        pe.wait_ge(sm["rmax_done"], su - 2)
                    if su == 64:
                        pe.wait_ge(sm["op_q"], 96)
                        pe.wait_ge(sm["op_k"], 96)
                    if su == 32:
                        pe.wait_ge(sm["rope_op_half1"], 64)
                    pe.matmul(ps[:, su % 3, :], q_op[0:PR, e, 2 * g + a, b * S + it * P:b * S + it * P + P],
                              k_op[0:PR, 0, 2 * g + a, b * S:b * S + S], start=True, stop=True).then_inc(sm["rmax_psum"], 1)
                m = (su - 18) // 16
                if (su - 18) % 16 == 0 and 0 <= m < 8:
                    b, g = divmod(m, 4)
                    pe.wait_ge(sm["rope_negm"], m + 1)
                    if m >= 1:
                        pe.wait_ge(sm["rope_negT"], m)
                    for it in range(IT):
                        i = pe.transpose(ps[0:4, 7, it * P:it * P + P], neg_m[:, IT * b + it, 4 * g:4 * g + 4], ident[:, :])
                    i.then_inc(sm["rope_negT_psum"], 1)
                k, half = divmod(j - 6, 4)
                if 0 <= k < 32 and half < 2:
                    n, jt = divmod(k, 4)
                    b, g = divmod(n, 4)
                    pe.wait_ge(sm["rope_exp_done"], 4 * k + 4)
                    if jt == 0 and half == 0 and n >= 1:
                        pe.wait_ge(sm["rope_ctx_ready"], n)
                    for hh in range(4):
                        h = 4 * g + hh
                        i = pe.matmul(ps[32 * hh:32 * hh + VW, 6, 256 * half:256 * half + 256], v_sb[:, 0, IT * b + jt, h * VW:h * VW + VW],
                                      p_ring[:, k % 4, hh, 256 * half:256 * half + 256], start=(jt == 0 and half == 0),
                                      stop=(jt == IT - 1), skip_group_check=True)
                    if half:
                        i.then_inc(sm["rope_pv_done"], 1)

            pe.wait_ge(sm["rope_ctx_ready"], 8)
            attn_finish(1, ctxn, w_o)

            def mlp(n):
                c, w, k = n // 4, (n // 2) % 2, n % 2
                if n >= 3:
                    pe.wait_ge(sm["hid_ready"], n - 2)
                for z in range(2):
                    i = pe.matmul(ps[:, 2 * (n % 3) + z, :], w_in[w][:, HID * z + P * k:HID * z + P * k + P], xnT[:, c * 512:c * 512 + 512],
                                  start=True, stop=True)
                i.then_inc(sm["mlp_psum"], 1)

            def transpose_again(tt):
                pe.wait_ge(sm["ln_out"], NT * 3 + tt + 1)
                pe.transpose(ps[:, 6 + tt // 4, (tt % 4) * P:(tt % 4) * P + P], xn[:, tt, :], ident[:, :]).then_inc(sm["xT_psum"], 1)

            def gate_logits(tt):
                i = pe.matmul(ps[:, 6, 10 * tt:10 * tt + 10], xnT[:, tt * P:tt * P + P], w_gate, start=True, stop=True)
                if tt == NT - 1:
                    i.then_inc(sm["gate_psum"], 1)

            for tt in range(IT):
                transpose_again(tt)
            pe.wait_ge(sm["xT_ready"], 5)
            for tt in range(IT):
                gate_logits(tt)
            pe.wait_ge(sm["x_added"], 2 * NT)
            for tt in range(IT, NT):
                transpose_again(tt)
            mlp(0)
            pe.wait_ge(sm["xT_ready"], 6)
            for tt in range(IT, NT):
                gate_logits(tt)
            for n in range(1, 8):
                mlp(n)
            for tt in range(NT):
                b0, b1, b2 = Y_BANKS[tt % 2]
                if tt in (0, 1):
                    pe.wait_ge(sm["hid_ready"], 6 + tt)
                if tt == IT:
                    pe.wait_ge(sm["hid_ready"], 8)
                if tt >= 2:
                    pe.wait_ge(sm["ffn_added"], tt - 1)
                for c in range(2):
                    for k in range(2):
                        pe.matmul(ps[:, (b0, b1)[c], :], hid[1][:, k, tt * P:tt * P + P], w_2[:, k, c * 512:c * 512 + 512],
                                  start=(k == 0), stop=(k == 1))
                for k in range(2):
                    i = pe.matmul(ps[:, b2, 0:D], hid[0][:, k, tt * P:tt * P + P], w_so[:, k, :], start=(k == 0), stop=(k == 1))
                i.then_inc(sm["expert_psum"], 1)


def kernel(**inputs):
    import numpy as np
    import concourse.bacc as bacc
    from concourse.bass_utils import run_bass_kernel_spmd

    a = {k: np.ascontiguousarray(v) for k, v in inputs.items()}
    off = np.clip(np.arange(EXT) - ZERO, -R, R) + R
    relk, relv = a["L0_attn_rel_emb_k"], a["L0_attn_rel_emb_v"]
    bqkv = a["L0_attn_b_qkv"]
    import ml_dtypes
    freq = (np.float32(1.0) / np.float32(10000.0) ** (np.arange(0, HD, 2, dtype=np.float32) / np.float32(HD))).astype(np.float32)
    angle = np.tile(np.repeat(freq, 2), H)[:, None] * np.arange(S, dtype=np.float32)[None, :]
    arrays = {
        "x": a["x"],
        "w_qkv": a["L0_attn_W_qkv"],
        "w_out": a["L0_attn_W_out"],
        "ident": np.eye(P, dtype=np.float32),
        "zeros": np.zeros((1, 3 * (H // 2) * TOK), ml_dtypes.bfloat16),
        "ones": np.ones((1, 3 * (H // 2) * TOK), ml_dtypes.bfloat16),
        "cols": np.ascontiguousarray(np.stack([bqkv[:D], bqkv[D:2 * D], np.tile(relk[0], H), np.tile(relk[2 * R], H)], 1)),
        "rows": np.ascontiguousarray(np.stack([bqkv[2 * D:], np.tile(relv[0], H), np.tile(relv[2 * R], H), a["L0_attn_b_out"],
                          a["L0_xattn_conv_b"], a["L0_ffn_norm1_w"], a["L0_ffn_norm2_w"]])),
        "relk_ext": np.ascontiguousarray(relk[off].T),
        "relv_ext": relv[off],
        "ctx": a["ctx_1024"],
        "w_conv": a["L0_xattn_conv_w"],
        "w_q": a["L0_ffn_Wq"], "w_kc": a["L0_ffn_Wk_c"], "w_vc": a["L0_ffn_Wv_c"],
        "w_k": a["L0_ffn_Wk"], "w_v": a["L0_ffn_Wv"], "w_o": a["L0_ffn_Wo"],
        "w_sin": a["L0_ffn_W_shared_in"], "w_so": a["L0_ffn_W_shared_out"],
        "w_1": a["L0_ffn_W1_shared"], "w_2": a["L0_ffn_W2_experts"],
        "w_gg": a["L0_ffn_Wg_gate"], "w_ge": a["L0_ffn_We_gate"],
        "b_gg": a["L0_ffn_group_bias"], "b_ge": a["L0_ffn_expert_bias"],
        "cos": np.ascontiguousarray(np.cos(angle)), "sin": np.ascontiguousarray(np.sin(angle)),
        "tri": np.tril(np.ones((EPG, EPG), np.float32), -1).reshape(-1),
    }
    nc = bacc.Bacc("TRN2", target_bir_lowering=False, num_devices=1)
    t = {n: nc.dram_tensor("in_" + n, v.shape, mybir.dt.from_np(v.dtype), kind="ExternalInput").ap() for n, v in arrays.items()}
    t["scr"] = nc.dram_tensor("scr", (4, P, SLOTS, TOK), BF16, kind="Internal").ap()
    t["scr_rel"] = nc.dram_tensor("scr_rel", (HD, SLOTS, EXT), BF16, kind="Internal").ap()
    t["out"] = nc.dram_tensor("out", (B, S, D), F32, kind="ExternalOutput").ap()
    build(nc, t)
    r = run_bass_kernel_spmd(nc, [{"in_" + n: v for n, v in arrays.items()}], core_ids=[0])
    return r.results[0]["out"]
```
